# Optimizing a Trainium2 kernel written in Bass

```python
import numpy as np
import jax
import jax.numpy as jnp

def _softmax(x, axis=-1):
    return jax.nn.softmax(x, axis=axis)

def _gelu(x):
    return jax.nn.gelu(x, approximate=True)

def _silu(x):
    return jax.nn.silu(x)

def _sigmoid(x):
    return jax.nn.sigmoid(x)

def _layernorm(x, axis=-1, eps=1e-05):
    m = jnp.mean(x, axis=axis, keepdims=True)
    v = jnp.var(x, axis=axis, keepdims=True)
    return (x - m) / jnp.sqrt(v + eps)

def _scatter_add(tgt, idx, src, axis=0):
    return tgt.at[idx].add(src)

def _segment_sum(src, seg, n):
    return jax.ops.segment_sum(src, seg, n)
kernel_name = 'mk_cond_resid_d4_seqx_r8_6bd789'

def setup_inputs(seed: int=0):
    np.random.seed(seed)
    _w = jnp.asarray

    def _rec_inputs():
        import jax
        import jax.numpy as jnp
        _rk = jax.random.key(seed)
        x = -0.000125 + 0.9999 * jax.random.normal(jax.random.fold_in(_rk, 1), (8, 128, 512), jnp.float32)
        _lenS = 128 - jax.random.randint(jax.random.fold_in(_rk, 7), (8,), 0, max(1, 128 // 4) + 1, jnp.int32)
        _lenS2 = 128 - jax.random.randint(jax.random.fold_in(_rk, 8), (8,), 0, max(1, 128 // 4) + 1, jnp.int32)
        itok_B_3_7 = jax.random.randint(jax.random.fold_in(_rk, 11), (8,), 3, 8, jnp.int32)
        pos_BxS = jnp.broadcast_to(jnp.arange(128, dtype=jnp.int32), (8, 128))
        itok_B_0_7 = jax.random.randint(jax.random.fold_in(_rk, 14), (8,), 0, 8, jnp.int32)
        itok_B_0_23 = jax.random.randint(jax.random.fold_in(_rk, 15), (8,), 0, 24, jnp.int32)
        _validS = jnp.arange(128)[None, :] < _lenS[:, None]
        _validS2 = jnp.arange(128)[None, :] < _lenS2[:, None]
        _causal = jnp.tril(jnp.ones((128, 128), dtype=bool))
        mask_BxS_bf1 = jnp.ones((8, 128), dtype=bool)
        return (x, itok_B_3_7, pos_BxS, itok_B_0_7, itok_B_0_23, mask_BxS_bf1)
    x, itok_B_3_7, pos_BxS, itok_B_0_7, itok_B_0_23, mask_BxS_bf1 = _rec_inputs()

    def _L0_cond_setup():
        import jax, jax.numpy as jnp
        import numpy as np
        MAX_LORAS, OUT, IN = (8, 512, 512)
        B, S = (4, 256)
        key = jax.random.key(seed)
        k1, k2, k3 = jax.random.split(key, 3)
        x = jax.random.normal(k1, (B, S, IN), dtype=jnp.float32)
        weight = jax.random.normal(k2, (MAX_LORAS, OUT, IN), dtype=jnp.float32) * 0.02
        adapter_ids = jax.random.randint(k3, (B,), 0, MAX_LORAS, dtype=jnp.int32)
        return {'x': x, 'weight': weight, 'adapter_ids': adapter_ids}
    _L0_cond_all = _L0_cond_setup()
    _L0_cond_in = {k: v for k, v in _L0_cond_all.items() if k in ('weight',)}
    del _L0_cond_all

    def _L1_cond_setup():
        import jax, jax.numpy as jnp
        import numpy as np
        H, HKV, D, HID = (32, 8, 128, 512)
        THETA = 500000.0
        NAD, R = (8, 16)
        BATCH, T = (4, 128)

        def apply_rope(x, positions, head_dim, theta):
            half = head_dim // 2
            freq = theta ** (-jnp.arange(half, dtype=jnp.float32) / half)
            ang = positions.astype(jnp.float32)[..., None] * freq
            cos = jnp.cos(ang)[:, :, None, :]
            sin = jnp.sin(ang)[:, :, None, :]
            x1, x2 = jnp.split(x, 2, axis=-1)
            out = jnp.concatenate([x1 * cos - x2 * sin, x2 * cos + x1 * sin], axis=-1)
            return out.astype(x.dtype)

        def lora_linear(x, w, a, b, adapter_indices):
            base = jnp.einsum('bti,io->bto', x, w)
            ax = jnp.einsum('bti,bir->btr', x, a[adapter_indices])
            return base + jnp.einsum('btr,bro->bto', ax, b[adapter_indices])
        key = jax.random.key(seed)
        ks = jax.random.split(key, 16)
        s = 0.02
        inp = {'x': jax.random.normal(ks[0], (BATCH, T, HID), jnp.float32), 'attention_mask': jnp.ones((BATCH, T), bool), 'positions': jnp.tile(jnp.arange(T, dtype=jnp.int32)[None, :], (BATCH, 1)), 'adapter_indices': jax.random.randint(ks[1], (BATCH,), 0, NAD, jnp.int32), 'wq': jax.random.normal(ks[2], (HID, H * D), jnp.float32) * s, 'wk': jax.random.normal(ks[3], (HID, HKV * D), jnp.float32) * s, 'wv': jax.random.normal(ks[4], (HID, HKV * D), jnp.float32) * s, 'wo': jax.random.normal(ks[5], (H * D, HID), jnp.float32) * s, 'aq': jax.random.normal(ks[6], (NAD, HID, R), jnp.float32) * 0.01, 'bq': jax.random.normal(ks[7], (NAD, R, H * D), jnp.float32) * 0.01, 'ak': jax.random.normal(ks[8], (NAD, HID, R), jnp.float32) * 0.01, 'bk': jax.random.normal(ks[9], (NAD, R, HKV * D), jnp.float32) * 0.01, 'av': jax.random.normal(ks[10], (NAD, HID, R), jnp.float32) * 0.01, 'bv': jax.random.normal(ks[11], (NAD, R, HKV * D), jnp.float32) * 0.01, 'ao': jax.random.normal(ks[12], (NAD, H * D, R), jnp.float32) * 0.01, 'bo': jax.random.normal(ks[13], (NAD, R, HID), jnp.float32) * 0.01}
        return inp
    _L1_cond_all = _L1_cond_setup()
    _L1_cond_in = {k: v for k, v in _L1_cond_all.items() if k in ('wq', 'wk', 'wv', 'wo', 'aq', 'bq', 'ak', 'bk', 'av', 'bv', 'ao', 'bo')}
    del _L1_cond_all

    def _L2_cond_setup():
        import jax, jax.numpy as jnp
        import numpy as np
        RANK = 16
        ALPHA = 16.0
        SCALING = ALPHA / RANK
        N_ADAPTERS = 8
        IN_F = 512
        OUT_F = 512
        BATCH = 4
        SEQ = 256
        key = jax.random.key(seed)
        kx, ka, kb, ki = jax.random.split(key, 4)
        x = jax.random.normal(kx, (BATCH, SEQ, IN_F), dtype=jnp.float32)
        A = jax.random.normal(ka, (N_ADAPTERS, OUT_F, RANK), dtype=jnp.float32) * 0.02
        B = jax.random.normal(kb, (N_ADAPTERS, RANK, IN_F), dtype=jnp.float32) * 0.02
        adapter_ids = jax.random.randint(ki, (BATCH,), 0, N_ADAPTERS, dtype=jnp.int32)
        return {'x': x, 'A': A, 'B': B, 'adapter_ids': adapter_ids}
    _L2_cond_all = _L2_cond_setup()
    _L2_cond_in = {k: v for k, v in _L2_cond_all.items() if k in ('A', 'B')}
    del _L2_cond_all

    def _L3_cond_setup():
        import jax, jax.numpy as jnp
        import numpy as np
        R = 16
        ALPHA = 32
        SCALING = ALPHA / R
        SLOTS = 32
        IN_F = 512
        OUT_F = 512
        B, T = (8, 128)
        key = jax.random.key(seed)
        k1, k2, k3, k4, k5, k6 = jax.random.split(key, 6)
        x = jax.random.normal(k1, (B, T, IN_F), dtype=jnp.float32)
        adapter_mapping = jax.random.randint(k2, (B,), 0, SLOTS, dtype=jnp.int32)
        W = jax.random.normal(k3, (OUT_F, IN_F), dtype=jnp.float32) * 0.02
        b = jax.random.normal(k4, (OUT_F,), dtype=jnp.float32) * 0.02
        lora_As = jax.random.normal(k5, (SLOTS, IN_F, R), dtype=jnp.float32) * 0.02
        lora_Bs = jax.random.normal(k6, (SLOTS, R, OUT_F), dtype=jnp.float32) * 0.02
        return {'x': x, 'adapter_mapping': adapter_mapping, 'W': W, 'b': b, 'lora_As': lora_As, 'lora_Bs': lora_Bs}
    _L3_cond_all = _L3_cond_setup()
    _L3_cond_in = {k: v for k, v in _L3_cond_all.items() if k in ('W', 'b', 'lora_As', 'lora_Bs')}
    del _L3_cond_all
    return {'x': x, 'itok_B_3_7': itok_B_3_7, 'pos_BxS': pos_BxS, 'itok_B_0_7': itok_B_0_7, 'itok_B_0_23': itok_B_0_23, 'mask_BxS_bf1': mask_BxS_bf1, 'L0_cond_weight': _L0_cond_in['weight'], 'L1_cond_wq': _L1_cond_in['wq'], 'L1_cond_wk': _L1_cond_in['wk'], 'L1_cond_wv': _L1_cond_in['wv'], 'L1_cond_wo': _L1_cond_in['wo'], 'L1_cond_aq': _L1_cond_in['aq'], 'L1_cond_bq': _L1_cond_in['bq'], 'L1_cond_ak': _L1_cond_in['ak'], 'L1_cond_bk': _L1_cond_in['bk'], 'L1_cond_av': _L1_cond_in['av'], 'L1_cond_bv': _L1_cond_in['bv'], 'L1_cond_ao': _L1_cond_in['ao'], 'L1_cond_bo': _L1_cond_in['bo'], 'L2_cond_A': _L2_cond_in['A'], 'L2_cond_B': _L2_cond_in['B'], 'L3_cond_W': _L3_cond_in['W'], 'L3_cond_b': _L3_cond_in['b'], 'L3_cond_lora_As': _L3_cond_in['lora_As'], 'L3_cond_lora_Bs': _L3_cond_in['lora_Bs']}

def reference(x, itok_B_3_7, pos_BxS, itok_B_0_7, itok_B_0_23, mask_BxS_bf1, L0_cond_weight, L1_cond_wq, L1_cond_wk, L1_cond_wv, L1_cond_wo, L1_cond_aq, L1_cond_bq, L1_cond_ak, L1_cond_bk, L1_cond_av, L1_cond_bv, L1_cond_ao, L1_cond_bo, L2_cond_A, L2_cond_B, L3_cond_W, L3_cond_b, L3_cond_lora_As, L3_cond_lora_Bs):
    import jax
    import jax.numpy as jnp

    def _L0_cond_ref(x, weight, adapter_ids):
        import jax, jax.numpy as jnp
        import numpy as np
        MAX_LORAS, OUT, IN = (8, 512, 512)
        B, S = (4, 256)
        w = weight[adapter_ids]
        return jnp.einsum('bsi,boi->bso', x, w)

    def _L1_cond_ref(x, attention_mask, positions, adapter_indices, wq, wk, wv, wo, aq, bq, ak, bk, av, bv, ao, bo):
        import jax, jax.numpy as jnp
        import numpy as np
        H, HKV, D, HID = (32, 8, 128, 512)
        THETA = 500000.0
        NAD, R = (8, 16)
        BATCH, T = (4, 128)

        def apply_rope(x, positions, head_dim, theta):
            half = head_dim // 2
            freq = theta ** (-jnp.arange(half, dtype=jnp.float32) / half)
            ang = positions.astype(jnp.float32)[..., None] * freq
            cos = jnp.cos(ang)[:, :, None, :]
            sin = jnp.sin(ang)[:, :, None, :]
            x1, x2 = jnp.split(x, 2, axis=-1)
            out = jnp.concatenate([x1 * cos - x2 * sin, x2 * cos + x1 * sin], axis=-1)
            return out.astype(x.dtype)

        def lora_linear(x, w, a, b, adapter_indices):
            base = jnp.einsum('bti,io->bto', x, w)
            ax = jnp.einsum('bti,bir->btr', x, a[adapter_indices])
            return base + jnp.einsum('btr,bro->bto', ax, b[adapter_indices])
        B, Tt, _ = x.shape
        G = H // HKV
        q = lora_linear(x, wq, aq, bq, adapter_indices).reshape(B, Tt, H, D)
        k = lora_linear(x, wk, ak, bk, adapter_indices).reshape(B, Tt, HKV, D)
        v = lora_linear(x, wv, av, bv, adapter_indices).reshape(B, Tt, HKV, D)
        q = apply_rope(q, positions, D, THETA)
        k = apply_rope(k, positions, D, THETA)
        qg = q.reshape(B, Tt, HKV, G, D)
        scale = 1.0 / np.sqrt(D)
        logits = jnp.einsum('bqhgd,bkhd->bhgqk', qg, k) * scale
        causal = jnp.tril(jnp.ones((Tt, Tt), bool))
        mask = causal[None, None, None] & attention_mask[:, None, None, None, :]
        logits = jnp.where(mask, logits, jnp.finfo(logits.dtype).min)
        p = jax.nn.softmax(logits, axis=-1)
        o = jnp.einsum('bhgqk,bkhd->bqhgd', p, v).reshape(B, Tt, H * D)
        return lora_linear(o, wo, ao, bo, adapter_indices)

    def _L2_cond_ref(x, A, B, adapter_ids):
        import jax, jax.numpy as jnp
        import numpy as np
        RANK = 16
        ALPHA = 16.0
        SCALING = ALPHA / RANK
        N_ADAPTERS = 8
        IN_F = 512
        OUT_F = 512
        BATCH = 4
        SEQ = 256
        B_sel = B[adapter_ids]
        A_sel = A[adapter_ids]
        Bx = jnp.einsum('bni,bri->bnr', x, B_sel)
        out = jnp.einsum('bnr,bor->bno', Bx, A_sel)
        return out * SCALING

    def _L3_cond_ref(x, adapter_mapping, W, b, lora_As, lora_Bs):
        import jax, jax.numpy as jnp
        import numpy as np
        R = 16
        ALPHA = 32
        SCALING = ALPHA / R
        SLOTS = 32
        IN_F = 512
        OUT_F = 512
        B, T = (8, 128)
        base_out = jnp.einsum('bti,oi->bto', x, W) + b
        A = lora_As[adapter_mapping]
        Bm = lora_Bs[adapter_mapping]
        lora_h = jnp.einsum('bti,bir->btr', x, A)
        lora_out = jnp.einsum('btr,bro->bto', lora_h, Bm)
        return base_out + lora_out * SCALING
    x = x + _L0_cond_ref(x, L0_cond_weight, itok_B_3_7)
    x = x + _L1_cond_ref(x, mask_BxS_bf1, pos_BxS, itok_B_0_7, L1_cond_wq, L1_cond_wk, L1_cond_wv, L1_cond_wo, L1_cond_aq, L1_cond_bq, L1_cond_ak, L1_cond_bk, L1_cond_av, L1_cond_bv, L1_cond_ao, L1_cond_bo)
    x = x + _L2_cond_ref(x, L2_cond_A, L2_cond_B, itok_B_3_7)
    x = x + _L3_cond_ref(x, itok_B_0_23, L3_cond_W, L3_cond_b, L3_cond_lora_As, L3_cond_lora_Bs)
    return x

_drawn_inputs = setup_inputs


def setup_inputs(seed=0):
    import zlib

    import numpy as np

    out = dict(_drawn_inputs(seed))
    spreads = {}
    factors = {'L1_cond_aq': 8.0,
     'L1_cond_bq': 8.0,
     'L1_cond_ak': 8.0,
     'L1_cond_bk': 8.0,
     'L1_cond_av': 8.0,
     'L1_cond_bv': 8.0,
     'L1_cond_ao': 8.0,
     'L1_cond_bo': 8.0,
     'L3_cond_b': 3.664}
    for name, (base, spread) in spreads.items():
        noise = np.random.default_rng([zlib.crc32(name.encode()), seed]).standard_normal(out[name].shape)
        drawn = base * np.exp(spread * noise) if base else spread * noise
        out[name] = jnp.asarray(drawn.astype(out[name].dtype))
    for name, factor in factors.items():
        out[name] = (out[name] * factor).astype(out[name].dtype)
    return out
```

```python
from contextlib import ExitStack

import numpy as np

import concourse.bass as bass
from concourse import mybir

P = 128
F32 = mybir.dt.float32
F32R = mybir.dt.float32r
I32 = mybir.dt.int32
U8 = mybir.dt.uint8
ALU = mybir.AluOpType
ACT = mybir.ActivationFunctionType

NEG = -1.0e30
MAGIC = 1.5 * 2.0**23
TWO_PI = 2.0 * float(np.pi)
PI_A = 6.28125
PI_B = float(np.float32(np.floor((TWO_PI - PI_A) * 2.0**20) / 2.0**20))
PI_C = TWO_PI - PI_A - PI_B
PI_LIMIT = 3.1415925
THETA = 500000.0
HEAD_DIM = 128
LORA_SCALE = 2.0


def program(nc, x, lora_ids, pos, attn_ids, slot_ids, mask, w0, wq, wk, wv, wo, aq, bq, ak, bk, av, bv, ao, bo,
            l2a, l2b, w3, b3, l3a, l3b, ident_c, causal_c, rope_c, out):
    B, T, HID = x.shape
    KC = HID // P
    D = P
    KVH = wk.shape[1] // D
    G = wq.shape[1] // wk.shape[1]
    R = aq.shape[2]
    NT = B * T
    HALF = B // 2
    HT = HALF * T
    PAIRS = B // 2
    GW = G * D

    bq_sel = nc.dram_tensor("bq_sel", (B, R, KVH * GW), F32, kind="Internal").ap()
    bkv_sel = nc.dram_tensor("bkv_sel", (B, R, 2, KVH * D), F32, kind="Internal").ap()
    ao_sel = nc.dram_tensor("ao_sel", (B, KVH * GW, R), F32, kind="Internal").ap()
    k_rot = nc.dram_tensor("k_rot", (KVH, D, NT), F32, kind="Internal").ap()
    v_hi_d = nc.dram_tensor("v_hi_d", (KVH, T, B, D), F32, kind="Internal").ap()
    v_lo_d = nc.dram_tensor("v_lo_d", (KVH, T, B, D), F32, kind="Internal").ap()

    whole = ExitStack()
    with whole:
        def sb(ctx, name, shape, dt=F32):
            return ctx.enter_context(nc.sbuf_tensor(name, shape, dt))

        def ps(ctx, name, shape, dt=F32):
            return ctx.enter_context(nc.psum_tensor(name, shape, dt))

        def sem(ctx, name):
            return ctx.enter_context(nc.semaphore(name))

        def project(pe, bank, w_hi, w_lo, b_pack, ax, cols, half):
            tok = slice(half * HT, (half + 1) * HT)
            for k in range(KC):
                pe.matmul(bank[:, :], w_hi[:, k, cols], x1t_hi[:, k, tok], start=(k == 0), stop=False)
                pe.matmul(bank[:, :], w_hi[:, k, cols], x1t_lo[:, k, tok], start=False, stop=False)
                pe.matmul(bank[:, :], w_lo[:, k, cols], x1t_hi[:, k, tok], start=False, stop=False)
            for pair in range(PAIRS // 2):
                n = half * PAIRS // 2 + pair
                last = pe.matmul(bank[:, pair * 2 * T:(pair + 1) * 2 * T], b_pack[:, n, cols],
                                 ax[:, n * 2 * T:(n + 1) * 2 * T], start=False, stop=(pair == PAIRS // 2 - 1))
            return last

        res = sb(whole, "res", [P, B, HID])
        ident = sb(whole, "ident", [P, P])
        ident_r = sb(whole, "ident_r", [P, P], F32R)
        axo = sb(whole, "axo", [2 * R, B, T])

        id_rows = sb(whole, "id_rows", [1, 3, B], I32)

        attn = ExitStack()
        attn.__enter__()
        x1t_hi = sb(attn, "x1t_hi", [P, KC, NT], F32R)
        x1t_lo = sb(attn, "x1t_lo", [P, KC, NT], F32R)
        cos_t = sb(attn, "cos_t", [P, NT])
        sin_t = sb(attn, "sin_t", [P, NT])
        maskbias = sb(attn, "maskbias", [P, B, T])
        axt = [sb(attn, f"axt_{n}", [P, NT], F32R) for n in "qk"]

        with ExitStack() as c:
            w0_raw = [sb(c, f"w0_raw{i}", [P, KC, HID]) for i in range(2)]
            xt_hi = [sb(c, f"xt_hi{i}", [P, KC, T], F32R) for i in range(2)]
            xt_lo = [sb(c, f"xt_lo{i}", [P, KC, T], F32R) for i in range(2)]
            wt_hi = [sb(c, f"wt_hi{i}", [P, KC, HID], F32R) for i in range(2)]
            wt_lo = [sb(c, f"wt_lo{i}", [P, KC, HID], F32R) for i in range(2)]
            pos_i = sb(c, "pos_i", [P, NT], I32)
            ang = sb(c, "ang", [P, NT])
            turns = sb(c, "turns", [P, NT])
            rope_cols = sb(c, "rope_cols", [P, 3])
            mask_u8 = sb(c, "mask_u8", [P, NT], U8)
            causal = sb(c, "causal", [P, T])
            ps_w = [ps(c, f"ps_w{i}", [P, HID]) for i in range(KC)]
            ps_x = ps(c, "ps_x", [P, KC, T])
            ps_y = [ps(c, f"ps_y{i}", [P, HID]) for i in range(2)]
            ps_x1 = ps(c, "ps_x1", [P, KC, T])
            ids_in = sem(c, "ids_in")
            consts_in = sem(c, "consts_in")
            tables_in = sem(c, "tables_in")
            x_in = [sem(c, f"x_in{b}") for b in range(B)]
            w0_in = [sem(c, f"w0_in{i}") for i in range(2)]
            gathered = sem(c, "gathered")
            ident_ready = sem(c, "ident_ready")
            xt_ready = sem(c, "xt_ready")
            wt_ready = sem(c, "wt_ready")
            xt_hi_done = sem(c, "xt_hi_done")
            xt_lo_done = sem(c, "xt_lo_done")
            wt_hi_done = sem(c, "wt_hi_done")
            wt_lo_done = sem(c, "wt_lo_done")
            y_ready = sem(c, "y_ready")
            x1_done = sem(c, "x1_done")
            x1t_ready = sem(c, "x1t_ready")
            x1t_hi_done = sem(c, "x1t_hi_done")
            x1t_lo_done = sem(c, "x1t_lo_done")
            tab = sem(c, "tab")
            sines = sem(c, "sines")

            with nc.Block() as block:
                @block.sync
                def _(sp):
                    for n, ids in enumerate((lora_ids, attn_ids, slot_ids)):
                        sp.dma_start(id_rows[:, n, :], ids.rearrange("(a b) -> a b", a=1)).then_inc(ids_in, 16)
                    sp.dma_start(ident[:, :], ident_c).then_inc(consts_in, 16)
                    for b in range(B):
                        sp.dma_start(res[:, b, :], x[b]).then_inc(x_in[b], 16)
                    sp.wait_ge(ids_in, 48)
                    for b in range(B):
                        a = sp.value_load(id_rows[0:1, 0, b:b + 1], min_val=0, max_val=w0.shape[0] - 1)
                        if b >= 2:
                            sp.wait_ge(wt_ready, KC * (b - 1))
                        sp.dma_start(w0_raw[b % 2][:, :, :],
                                     w0[bass.DynSlice(a, 1), :, :].rearrange("a (c p) i -> p (a c) i", p=P)).then_inc(w0_in[b % 2], 16)
                    for b in range(B):
                        a = sp.value_load(id_rows[0:1, 1, b:b + 1], min_val=0, max_val=bq.shape[0] - 1)
                        pick = bass.DynSlice(a, 1)
                        sp.dma_start(bkv_sel[b:b + 1, :, 0, :], bk[pick]).then_inc(gathered, 16)
                        sp.dma_start(bkv_sel[b:b + 1, :, 1, :], bv[pick]).then_inc(gathered, 16)
                        sp.dma_start(bq_sel[b:b + 1], bq[pick]).then_inc(gathered, 16)
                        sp.dma_start(ao_sel[b:b + 1], ao[pick]).then_inc(gathered, 16)
                    sp.wait_ge(gathered, 4 * B * 16)

                @block.gpsimd
                def _(pool):
                    pool.dma_start(pos_i[:, :], pos.rearrange("b t -> (b t)").partition_broadcast(P)).then_inc(tables_in, 16)
                    pool.dma_start(mask_u8[:, :], mask.rearrange("b t -> (b t)").partition_broadcast(P)).then_inc(tables_in, 16)
                    pool.dma_start(causal[:, :], causal_c).then_inc(tables_in, 16)
                    pool.dma_start(rope_cols[:, :], rope_c).then_inc(tables_in, 16)
                    pool.wait_ge(tables_in, 64)

                @block.tensor
                def _(pe):
                    def transposes(b):
                        pe.wait_ge(x_in[b], 16)
                        if b == 0:
                            pe.wait_ge(consts_in, 16)
                        if b >= 1:
                            pe.wait_ge(xt_lo_done, b)
                        for k in range(KC):
                            mm = pe.matmul(ps_x[:, k, :], res[:, b, k * P:(k + 1) * P], ident[:, :], start=True, stop=True)
                        mm.then_inc(xt_ready, 1)
                        pe.wait_ge(w0_in[b % 2], 16 * (b // 2 + 1))
                        for k in range(KC):
                            if b >= 1:
                                pe.wait_ge(wt_lo_done, KC * (b - 1) + k + 1)
                            for o in range(KC):
                                mm = pe.matmul(ps_w[k][:, o * P:(o + 1) * P], w0_raw[b % 2][:, o, k * P:(k + 1) * P],
                                               ident[:, :], start=True, stop=True)
                            mm.then_inc(wt_ready, 1)

                    def product(b):
                        pe.wait_ge(xt_lo_done, b + 1)
                        if b >= 2:
                            pe.wait_ge(x1_done, b - 1)
                        i = b % 2
                        for k in range(KC):
                            pe.wait_ge(wt_lo_done, KC * b + k + 1)
                            pe.matmul(ps_y[i][:, :], xt_hi[i][:, k, :], wt_hi[i][:, k, :], start=(k == 0), stop=False)
                            pe.matmul(ps_y[i][:, :], xt_hi[i][:, k, :], wt_lo[i][:, k, :], start=False, stop=False)
                            mm = pe.matmul(ps_y[i][:, :], xt_lo[i][:, k, :], wt_hi[i][:, k, :], start=False, stop=(k == KC - 1))
                        mm.then_inc(y_ready, 1)

                    def turn_x1(b):
                        pe.wait_ge(x1_done, b + 1)
                        if b >= 1:
                            pe.wait_ge(x1t_lo_done, b)
                        for k in range(KC):
                            mm = pe.matmul(ps_x1[:, k, :], res[:, b, k * P:(k + 1) * P], ident[:, :], start=True, stop=True)
                        mm.then_inc(x1t_ready, 1)

                    transposes(0)
                    for b in range(B):
                        if b + 1 < B:
                            transposes(b + 1)
                        product(b)
                        if b >= 1:
                            turn_x1(b - 1)
                    turn_x1(B - 1)

                @block.scalar
                def _(act):
                    def split(b):
                        i = b % 2
                        if b >= 2:
                            act.wait_ge(y_ready, b - 1)
                        act.wait_ge(xt_ready, b + 1)
                        act.activation(xt_hi[i][:, :, :], ps_x[:, :, :], ACT.Copy).then_inc(xt_hi_done, 1)
                        for k in range(KC):
                            act.wait_ge(wt_ready, KC * b + k + 1)
                            act.activation(wt_hi[i][:, k, :], ps_w[k][:, :], ACT.Copy).then_inc(wt_hi_done, 1)

                    def split_x1(b):
                        act.wait_ge(x1t_ready, b + 1)
                        act.activation(x1t_hi[:, :, b * T:(b + 1) * T], ps_x1[:, :, :], ACT.Copy).then_inc(x1t_hi_done, 1)

                    act.wait_ge(consts_in, 16)
                    act.activation(ident_r[:, :], ident[:, :], ACT.Copy).then_inc(ident_ready, 1)
                    split(0)
                    for b in range(B):
                        if b + 1 < B:
                            split(b + 1)
                        if b >= 1:
                            split_x1(b - 1)
                    split_x1(B - 1)
                    act.wait_ge(tab, 7)
                    act.activation(sin_t[:, :], ang[:, :], ACT.Sin).then_inc(sines, 1)
                    act.wait_ge(tab, 15)
                    act.activation(cos_t[:, :], ang[:, :], ACT.Sin).then_inc(sines, 1)

                @block.vector
                def _(dve):
                    def split(b):
                        i = b % 2
                        dve.wait_ge(xt_hi_done, b + 1)
                        dve.tensor_tensor(xt_lo[i][:, :, :], ps_x[:, :, :], xt_hi[i][:, :, :].bitcast(F32),
                                          ALU.subtract).then_inc(xt_lo_done, 1)
                        for k in range(KC):
                            dve.wait_ge(wt_hi_done, KC * b + k + 1)
                            dve.tensor_tensor(wt_lo[i][:, k, :], ps_w[k][:, :], wt_hi[i][:, k, :].bitcast(F32),
                                              ALU.subtract).then_inc(wt_lo_done, 1)

                    def add(b):
                        dve.wait_ge(y_ready, b + 1)
                        dve.tensor_tensor(res[:, b, :], ps_y[b % 2][:, :], res[:, b, :], ALU.add).then_inc(x1_done, 1)

                    def split_x1(b):
                        dve.wait_ge(x1t_hi_done, b + 1)
                        cols = slice(b * T, (b + 1) * T)
                        dve.tensor_tensor(x1t_lo[:, :, cols], ps_x1[:, :, :], x1t_hi[:, :, cols].bitcast(F32),
                                          ALU.subtract).then_inc(x1t_lo_done, 1)

                    split(0)
                    for b in range(B):
                        if b + 1 < B:
                            split(b + 1)
                        add(b)
                        if b >= 1:
                            split_x1(b - 1)
                    split_x1(B - 1)

                    steps = [0]

                    def step(instruction):
                        steps[0] += 1
                        instruction.then_inc(tab, 1)
                        dve.wait_ge(tab, steps[0])

                    dve.wait_ge(tables_in, 64)
                    for quarter in (0.0, 0.25):
                        if quarter:
                            dve.wait_ge(sines, 1)
                        step(dve.tensor_scalar(ang[:, :], pos_i[:, :], rope_cols[:, 0:1], None, ALU.mult))
                        step(dve.tensor_scalar(turns[:, :], ang[:, :], 1.0 / TWO_PI, quarter, ALU.mult, ALU.add))
                        step(dve.tensor_scalar(turns[:, :], turns[:, :], MAGIC, -MAGIC, ALU.add, ALU.add))
                        for part in (PI_A, PI_B, PI_C):
                            step(dve.scalar_tensor_tensor(ang[:, :], turns[:, :], -part, ang[:, :], ALU.mult, ALU.add))
                        if quarter:
                            step(dve.tensor_scalar(ang[:, :], ang[:, :], TWO_PI / 4, None, ALU.add))
                        step(dve.tensor_scalar(ang[:, :], ang[:, :], PI_LIMIT, -PI_LIMIT, ALU.min, ALU.max))
                    assert steps[0] == 15
                    dve.wait_ge(sines, 2)
                    step(dve.tensor_scalar(cos_t[:, :], cos_t[:, :], rope_cols[:, 1:2], None, ALU.mult))
                    step(dve.tensor_scalar(sin_t[:, :], sin_t[:, :], rope_cols[:, 2:3], None, ALU.mult))
                    mb = maskbias[:, :, :].rearrange("p b t -> p (b t)")
                    step(dve.tensor_scalar(mb, mask_u8[:, :], -NEG, NEG, ALU.mult, ALU.add))
                    for b in range(B):
                        step(dve.tensor_tensor(maskbias[:, b, :], maskbias[:, b, :], causal[:, :], ALU.min))

        with ExitStack() as c:
            w_raw = sb(c, "w_raw", [P, KC, KVH * D])
            w_hi = [sb(c, f"w_hi{i}", [P, KC, KVH * D], F32R) for i in range(1)]
            w_lo = [sb(c, f"w_lo{i}", [P, KC, KVH * D], F32R) for i in range(1)]
            a_raw = [sb(c, f"a_raw{i}", [P, KC, 3, R]) for i in range(2)]
            a_hi = [sb(c, f"a_hi{i}", [P, KC, 3, R], F32R) for i in range(2)]
            a_lo = [sb(c, f"a_lo{i}", [P, KC, 3, R], F32R) for i in range(2)]
            axn = [sb(c, f"axn{i}", [P, 3, 4, 2, R], F32R) for i in range(2)]
            axt_v = sb(c, "axt_v", [P, NT], F32R)
            b_raw = sb(c, "b_raw", [P, PAIRS, KVH * D])
            b_pack = sb(c, "b_pack", [P, PAIRS, KVH * D], F32R)
            v_hi = [sb(c, f"v_hi{i}", [P, HID], F32R) for i in range(2)]
            v_lo = [sb(c, f"v_lo{i}", [P, HID], F32R) for i in range(2)]
            rot = [sb(c, f"rot{i}", [P, HT]) for i in range(2)]
            kr = [sb(c, f"kr{i}", [P, HT]) for i in range(2)]
            ps_a = ps(c, "ps_a", [P, 3, R])
            ps_at = ps(c, "ps_at", [P, 3, T])
            ps_v = [ps(c, f"ps_v{i}", [P, HID]) for i in range(2)]
            ps_k = [ps(c, f"ps_k{i}", [P, HT]) for i in range(2)]
            a_in = [sem(c, f"a_in{i}") for i in range(2)]
            w_in = sem(c, "w_in")
            b_in = sem(c, "b_in")
            zeroed = sem(c, "zeroed")
            a_hi_done = sem(c, "a_hi_done")
            a_lo_done = sem(c, "a_lo_done")
            ax_ready = sem(c, "ax_ready")
            axn_done = sem(c, "axn_done")
            axt_ready = sem(c, "axt_ready")
            axt_done = sem(c, "axt_done")
            w_hi_done = sem(c, "w_hi_done")
            w_lo_done = sem(c, "w_lo_done")
            b_hi_done = sem(c, "b_hi_done")
            b_lo_done = sem(c, "b_lo_done")
            v_ready = sem(c, "v_ready")
            v_hi_done = sem(c, "v_hi_done")
            v_lo_done = sem(c, "v_lo_done")
            v_out = [sem(c, f"v_out{i}") for i in range(2)]
            k_ready = sem(c, "k_ready")
            k_mult = sem(c, "k_mult")
            k_done = sem(c, "k_done")
            k_out = [sem(c, f"k_out{i}") for i in range(2)]
            VH = KVH * D // HID
            GPV = KVH // VH

            with nc.Block() as block:
                @block.sync
                def _(sp):
                    def load_weights(w, n):
                        sp.dma_start(w_raw[:, :, :], w.rearrange("(c p) n -> p c n", p=P)).then_inc(w_in, 16)
                        for quad in range(4):
                            sp.dma_start(b_raw[32 * quad:32 * quad + 32, :, :],
                                         bkv_sel.rearrange("(c two) r s n -> (two r) c s n", two=2)[:, :, n, :]).then_inc(b_in, 16)

                    for b in range(B):
                        a = sp.value_load(id_rows[0:1, 1, b:b + 1], min_val=0, max_val=aq.shape[0] - 1)
                        if b >= 2:
                            sp.wait_ge(a_lo_done, b - 1)
                        for n, src in enumerate((aq, ak, av)):
                            sp.dma_start(a_raw[b % 2][:, :, n, :],
                                         src[bass.DynSlice(a, 1), :, :].rearrange("a (c p) r -> p (a c) r", p=P)).then_inc(a_in[b % 2], 16)
                        if b == 1:
                            load_weights(wv, 1)
                    sp.wait_ge(w_lo_done, KC)
                    sp.wait_ge(b_lo_done, PAIRS)
                    load_weights(wk, 0)
                    for n in range(B * VH):
                        b, h = divmod(n, VH)
                        sp.wait_ge(v_lo_done, n + 1)
                        for src, dst in ((v_hi, v_hi_d), (v_lo, v_lo_d)):
                            sp.dma_start(dst[h * GPV:(h + 1) * GPV, :, b, :].rearrange("g t d -> t g d"),
                                         src[n % 2][:, :].bitcast(F32).rearrange("t (g d) -> t g d", d=D)).then_inc(v_out[n % 2], 16)
                    for n in range(2 * KVH):
                        g, h = divmod(n, 2)
                        sp.wait_ge(k_done, n + 1)
                        sp.dma_start(k_rot[g, :, h * HT:(h + 1) * HT], kr[n % 2][:, :]).then_inc(k_out[n % 2], 16)
                    for i in range(2):
                        sp.wait_ge(v_out[i], 32 * B * VH // 2)
                        sp.wait_ge(k_out[i], 16 * KVH)

                @block.scalar
                def _(act):
                    def copy_axt(b):
                        cols = slice(b * T, (b + 1) * T)
                        for n, dst in enumerate((axt[0], axt[1], axt_v)):
                            act.activation(dst[:, cols], ps_at[:, n, :], ACT.Copy).then_inc(axt_done, 1)

                    def split_weights(n):
                        act.wait_ge(w_in, 16 * (n + 1))
                        if n:
                            act.wait_ge(v_ready, B * VH)
                        for k in range(KC):
                            act.activation(w_hi[0][:, k, :], w_raw[:, k, :], ACT.Copy).then_inc(w_hi_done, 1)
                        act.wait_ge(b_in, 64 * (n + 1))
                        for p in range(PAIRS):
                            act.activation(b_pack[:, p, :], b_raw[:, p, :], ACT.Copy).then_inc(b_hi_done, 1)

                    for b in range(B):
                        i = b % 2
                        act.wait_ge(a_in[i], 48 * (b // 2 + 1))
                        if b >= 2:
                            act.wait_ge(ax_ready, b - 1)
                        act.activation(a_hi[i][:, :, :, :], a_raw[i][:, :, :, :], ACT.Copy).then_inc(a_hi_done, 1)
                        if b >= 1:
                            act.wait_ge(axt_ready, b)
                            copy_axt(b - 1)
                        if b == 1:
                            split_weights(0)
                    act.wait_ge(axt_ready, B)
                    copy_axt(B - 1)
                    for n in range(B * VH):
                        act.wait_ge(v_ready, n + 1)
                        if n >= 2:
                            act.wait_ge(v_out[n % 2], 32 * (n // 2))
                        act.activation(v_hi[n % 2][:, :], ps_v[n % 2][:, :], ACT.Copy).then_inc(v_hi_done, 1)
                    split_weights(1)

                @block.vector
                def _(dve):
                    for i in range(2):
                        dve.memset(axn[i][:, :, :, :, :].bitcast(F32), 0.0).then_inc(zeroed, 1)
                    for n in range(2):
                        if n == 0:
                            for b in range(B):
                                i = b % 2
                                dve.wait_ge(a_hi_done, b + 1)
                                dve.tensor_tensor(a_lo[i][:, :, :, :], a_raw[i][:, :, :, :], a_hi[i][:, :, :, :].bitcast(F32),
                                                  ALU.subtract).then_inc(a_lo_done, 1)
                                dve.wait_ge(zeroed, i + 1)
                                dve.wait_ge(ax_ready, b + 1)
                                if b >= 2:
                                    dve.wait_ge(axt_ready, b - 1)
                                for quad in (0, 2):
                                    dve.tensor_copy(axn[i][:, :, quad, i, :], ps_a[:, :, :]).then_inc(axn_done, 1)
                                dve.wait_ge(axn_done, 4 * b + 2)
                                for quad in (1, 3):
                                    dve.tensor_tensor(axn[i][:, :, quad, i, :], ps_a[:, :, :],
                                                      axn[i][:, :, 0, i, :].bitcast(F32), ALU.subtract).then_inc(axn_done, 1)
                        for k in range(KC):
                            dve.wait_ge(w_hi_done, KC * n + k + 1)
                            dve.tensor_tensor(w_lo[0][:, k, :], w_raw[:, k, :], w_hi[0][:, k, :].bitcast(F32),
                                              ALU.subtract).then_inc(w_lo_done, 1)
                        for p in range(PAIRS):
                            dve.wait_ge(b_hi_done, PAIRS * n + p + 1)
                            dve.tensor_tensor(b_pack[64:128, p, :], b_raw[64:128, p, :], b_pack[64:128, p, :].bitcast(F32),
                                              ALU.subtract).then_inc(b_lo_done, 1)
                        if n == 0:
                            for m in range(B * VH):
                                dve.wait_ge(v_hi_done, m + 1)
                                dve.tensor_tensor(v_lo[m % 2][:, :], ps_v[m % 2][:, :], v_hi[m % 2][:, :].bitcast(F32),
                                                  ALU.subtract).then_inc(v_lo_done, 1)
                    for n in range(2 * KVH):
                        i, h = n % 2, n % 2
                        cols = slice(h * HT, (h + 1) * HT)
                        dve.wait_ge(k_ready, n + 1)
                        if n >= 2:
                            dve.wait_ge(k_out[i], 16 * (n // 2))
                            dve.wait_ge(k_done, n - 1)
                        dve.tensor_tensor(kr[i][:, :], ps_k[i][:, :], cos_t[:, cols], ALU.mult).then_inc(k_mult, 1)
                        dve.tensor_tensor(rot[i][0:64, :], ps_k[i][64:128, :], sin_t[0:64, cols], ALU.mult).then_inc(k_mult, 1)
                        dve.tensor_tensor(rot[i][64:128, :], ps_k[i][0:64, :], sin_t[64:128, cols], ALU.mult).then_inc(k_mult, 1)
                        dve.wait_ge(k_mult, 3 * n + 3)
                        dve.tensor_tensor(kr[i][:, :], kr[i][:, :], rot[i][:, :], ALU.add).then_inc(k_done, 1)

                @block.tensor
                def _(pe):
                    def products(b):
                        i = b % 2
                        cols = slice(b * T, (b + 1) * T)
                        pe.wait_ge(a_lo_done, b + 1)
                        if b >= 1:
                            pe.wait_ge(axn_done, 4 * b)
                        for k in range(KC):
                            pe.matmul(ps_a[:, :, :], x1t_hi[:, k, cols], a_hi[i][:, k, :, :], start=(k == 0), stop=False)
                            pe.matmul(ps_a[:, :, :], x1t_hi[:, k, cols], a_lo[i][:, k, :, :], start=False, stop=False)
                            mm = pe.matmul(ps_a[:, :, :], x1t_lo[:, k, cols], a_hi[i][:, k, :, :], start=False, stop=(k == KC - 1))
                        mm.then_inc(ax_ready, 1)

                    def turn(b):
                        pe.wait_ge(axn_done, 4 * b + 4)
                        if b >= 1:
                            pe.wait_ge(axt_done, 3 * b)
                        for n in range(3):
                            mm = pe.matmul(ps_at[:, n, :], axn[b % 2][:, n, :, :, :].rearrange("p a b r -> p (a b r)"),
                                           ident_r[:, :], start=True, stop=True)
                        mm.then_inc(axt_ready, 1)

                    for b in range(B):
                        products(b)
                        turn(b)
                    pe.wait_ge(w_lo_done, KC)
                    pe.wait_ge(b_lo_done, PAIRS)
                    pe.wait_ge(axt_done, 3 * B)
                    for n in range(B * VH):
                        b, h = divmod(n, VH)
                        cols, wide = slice(b * T, (b + 1) * T), slice(h * HID, (h + 1) * HID)
                        if n >= 2:
                            pe.wait_ge(v_lo_done, n - 1)
                        o = ps_v[n % 2][:, :]
                        for k in range(KC):
                            pe.matmul(o, x1t_hi[:, k, cols], w_hi[0][:, k, wide], start=(k == 0), stop=False)
                            pe.matmul(o, x1t_hi[:, k, cols], w_lo[0][:, k, wide], start=False, stop=False)
                            pe.matmul(o, x1t_lo[:, k, cols], w_hi[0][:, k, wide], start=False, stop=False)
                        pe.matmul(o, axt_v[:, cols], b_pack[:, b // 2, wide], start=False, stop=True).then_inc(v_ready, 1)
                    pe.wait_ge(w_lo_done, 2 * KC)
                    pe.wait_ge(b_lo_done, 2 * PAIRS)
                    for n in range(2 * KVH):
                        g, h = divmod(n, 2)
                        if n >= 2:
                            pe.wait_ge(k_mult, 3 * (n - 1))
                        head = slice(g * D, (g + 1) * D)
                        project(pe, ps_k[n % 2], w_hi[0], w_lo[0], b_pack, axt[1], head, h).then_inc(k_ready, 1)

        with ExitStack() as c:
            wq_raw = sb(c, "wq_raw", [P, KC, GW])
            wq_hi = sb(c, "wq_hi", [P, KC, GW], F32R)
            wq_lo = sb(c, "wq_lo", [P, KC, GW], F32R)
            wo_raw = sb(c, "wo_raw", [P, G, HID])
            wo_hi = sb(c, "wo_hi", [P, G, HID], F32R)
            wo_lo = sb(c, "wo_lo", [P, G, HID], F32R)
            bq_raw = sb(c, "bq_raw", [P, PAIRS, GW])
            bq_pack = sb(c, "bq_pack", [P, PAIRS, GW], F32R)
            ao_raw = sb(c, "ao_raw", [P, B, G, R])
            ao_pack = sb(c, "ao_pack", [P, B, G, 2, R], F32R)
            kt = sb(c, "kt", [P, NT])
            v_hi = sb(c, "v_hi3", [P, B, D], F32R)
            v_lo = sb(c, "v_lo3", [P, B, D], F32R)
            qc = sb(c, "qc", [P, HT])
            qs = sb(c, "qs", [P, HT])
            qt = sb(c, "qt", [P, 2, G, HT])
            gate = sb(c, "gate", [P, 1])
            sm = sb(c, "sm", [P, G, T])
            nmax = [sb(c, f"nmax{i}", [P, G]) for i in range(2)]
            rsum = [sb(c, f"rsum{i}", [P, G]) for i in range(2)]
            rinv = [sb(c, f"rinv{i}", [P, G]) for i in range(2)]
            prob = [sb(c, f"prob{i}", [P, G, T]) for i in range(2)]
            pt_hi = sb(c, "pt_hi", [P, G * T], F32R)
            pt_lo = sb(c, "pt_lo", [P, G * T], F32R)
            ot_hi = sb(c, "ot_hi", [P, G * T], F32R)
            ot_lo = sb(c, "ot_lo", [P, G * T], F32R)
            ps_s = ps(c, "ps_s", [P, G, T])
            ps_q = ps(c, "ps_q", [P, HT])
            ps_t = ps(c, "ps_t", [P, G * T])
            ps_o = ps(c, "ps_o", [P, G * T])
            ps_out = ps(c, "ps_out", [P, HID])
            ps_ao = ps(c, "ps_ao", [P, 512])
            wq_in = sem(c, "wq_in")
            wo_in = sem(c, "wo_in")
            bq_in = [sem(c, f"bq_in{i}") for i in range(2)]
            ao_in = sem(c, "ao_in")
            kt_in = [sem(c, f"kt_in{i}") for i in range(2)]
            v_in = [sem(c, f"v_in{i}") for i in range(2)]
            wq_hi_done = sem(c, "wq_hi_done")
            wq_lo_done = sem(c, "wq_lo_done")
            wo_hi_done = sem(c, "wo_hi_done")
            wo_lo_done = sem(c, "wo_lo_done")
            bq_hi_done = sem(c, "bq_hi_done")
            bq_lo_done = sem(c, "bq_lo_done")
            ao_hi_done = sem(c, "ao_hi_done")
            ao_lo_done = sem(c, "ao_lo_done")
            s_ready = sem(c, "s_ready")
            q_ready = sem(c, "q_ready")
            q_mult = sem(c, "q_mult")
            q_done = sem(c, "q_done")
            max_done = sem(c, "max_done")
            exp_done = sem(c, "exp_done")
            inv_done = sem(c, "inv_done")
            prob_done = sem(c, "prob_done")
            t_ready = sem(c, "t_ready")
            pt_hi_done = sem(c, "pt_hi_done")
            pt_lo_done = sem(c, "pt_lo_done")
            o_ready = sem(c, "o_ready")
            ot_hi_done = sem(c, "ot_hi_done")
            ot_lo_done = sem(c, "ot_lo_done")
            out_ready = sem(c, "out_ready")
            res_done = sem(c, "res_done")
            axo_done = sem(c, "axo_done")

            def over_heads(eng, slots):
                slots(0, True, False)
                with eng.Fori(1, KVH - 1) as g:
                    slots(g, False, False)
                slots(KVH - 1, False, True)

            with nc.Block() as block:
                @block.sync
                def _(sp):
                    def load_wq(g):
                        sp.dma_start(wq_raw[:, :, :], wq[:, bass.DynSlice(g * GW, GW)].rearrange("(c p) n -> p c n", p=P)).then_inc(wq_in, 16)

                    def load_bq(g, h):
                        for quad in range(4):
                            sp.dma_start(bq_raw[32 * quad:32 * quad + 32, 2 * h:2 * h + 2, :],
                                         bq_sel.rearrange("(c two) r n -> (two r) c n", two=2)[:, 2 * h:2 * h + 2, bass.DynSlice(g * GW, GW)]
                                         ).then_inc(bq_in[h], 16)

                    def load_wo(g):
                        sp.dma_start(wo_raw[:, :, :], wo[bass.DynSlice(g * GW, GW), :].rearrange("(h p) n -> p h n", p=P)).then_inc(wo_in, 16)
                        for b in range(B):
                            sp.dma_start(ao_raw[:, b, :, :], ao_sel[b, bass.DynSlice(g * GW, GW), :].rearrange("(h p) r -> p h r", p=P)).then_inc(ao_in, 16)

                    def load_kv(g, h):
                        one = bass.DynSlice(g, 1)
                        cols, half = slice(h * HT, (h + 1) * HT), slice(h * HALF, (h + 1) * HALF)
                        sp.dma_start(kt[:, cols], k_rot[one, :, cols].rearrange("a p t -> p (a t)")).then_inc(kt_in[h], 16)
                        sp.dma_start(v_hi[:, half, :].bitcast(F32), v_hi_d[one, :, half, :].rearrange("a p b d -> p (a b) d")).then_inc(v_in[h], 16)
                        sp.dma_start(v_lo[:, half, :].bitcast(F32), v_lo_d[one, :, half, :].rearrange("a p b d -> p (a b) d")).then_inc(v_in[h], 16)

                    load_wq(0)
                    load_bq(0, 0)
                    load_bq(0, 1)
                    load_kv(0, 0)
                    load_wo(0)
                    load_kv(0, 1)
                    sp.wait_ge(wq_lo_done, G)
                    load_wq(1)
                    sp.wait_ge(bq_lo_done, PAIRS)
                    load_bq(1, 0)
                    load_bq(1, 1)

                    def slots(g, first, last):
                        if last:
                            return
                        sp.wait_ge(wo_lo_done, G * (g + 1))
                        sp.wait_ge(ao_lo_done, g + 1)
                        load_wo(g + 1)
                        if not (isinstance(g, int) and g + 2 >= KVH):
                            next_raw(g)
                        sp.wait_ge(s_ready, B * g + HALF)
                        sp.wait_ge(o_ready, B * g + HALF)
                        load_kv(g + 1, 0)
                        sp.wait_ge(s_ready, B * g + B)
                        sp.wait_ge(o_ready, B * g + B)
                        load_kv(g + 1, 1)

                    def next_raw(g):
                        sp.wait_ge(wq_lo_done, G * (g + 2))
                        load_wq(g + 2)
                        sp.wait_ge(bq_lo_done, PAIRS * (g + 1) + 2)
                        load_bq(g + 2, 0)

                    def next_raw_late(g):
                        sp.wait_ge(bq_lo_done, PAIRS * (g + 2))
                        load_bq(g + 2, 1)

                    def body(g):
                        slots(g, False, False)
                        next_raw_late(g)

                    body(0)
                    with sp.Fori(1, KVH - 2) as g:
                        body(g)
                    slots(KVH - 2, False, False)

                @block.scalar
                def _(act):
                    def wq_hi_part(g, h):
                        act.wait_ge(wq_in, 16 * (g + 1))
                        cols = slice(h * D, (h + 1) * D)
                        act.activation(wq_hi[:, :, cols], wq_raw[:, :, cols], ACT.Copy).then_inc(wq_hi_done, 1)

                    def bq_hi_part(g, p):
                        act.wait_ge(bq_in[p // 2], 64 * (g + 1))
                        act.activation(bq_pack[:, p, :], bq_raw[:, p, :], ACT.Copy).then_inc(bq_hi_done, 1)

                    def wo_hi_part(g):
                        act.wait_ge(wo_in, 16 * (g + 1))
                        for h in range(G):
                            act.activation(wo_hi[:, h, :], wo_raw[:, h, :], ACT.Copy).then_inc(wo_hi_done, 1)
                        act.wait_ge(ao_in, 16 * B * (g + 1))
                        act.activation(ao_pack[:, :, :, 0, :], ao_raw[:, :, :, :], ACT.Copy).then_inc(ao_hi_done, 1)

                    def pt(t, i):
                        act.wait_ge(t_ready, t + 1)
                        if i is None or i >= 1:
                            act.wait_ge(o_ready, t)
                        act.activation(pt_hi[:, :], ps_t[:, :], ACT.Copy).then_inc(pt_hi_done, 1)

                    def ot(t, i):
                        act.wait_ge(o_ready, t + 1)
                        if i is None or i >= 1:
                            act.wait_ge(out_ready, t)
                        act.activation(ot_hi[:, :], ps_o[:, :], ACT.Copy).then_inc(ot_hi_done, 1)

                    def slots(g, first, last):
                        for b in range(B):
                            t = B * g + b
                            number = t if first else None
                            act.wait_ge(max_done, t + 1)
                            if not first or b >= 2:
                                act.wait_ge(t_ready, t - 1)
                            i = b % 2
                            for h in range(G):
                                e = act.activation(prob[i][:, h, :], sm[:, h, :], ACT.Exp, bias=nmax[i][:, h:h + 1], scale=-1.0,
                                                   accum_out=rsum[i][:, h:h + 1])
                            e.then_inc(exp_done, 1)
                            if b < HALF and not last:
                                act.wait_ge(q_ready, B * g + G + b + 1)
                                wq_hi_part(g + 1, b)
                            if not last and b in (0, 2, 5, 7):
                                p = (0, 2, 5, 7).index(b)
                                act.wait_ge(q_ready, B * g + (G if p < 2 else B))
                                bq_hi_part(g + 1, p)
                            if not first or b >= 1:
                                pt(t - 1, None if not first else t - 1)
                                ot(t - 1, None if not first else t - 1)
                            if b == 1 and not first:
                                act.wait_ge(out_ready, B * g)
                                wo_hi_part(g)

                    for h in range(G):
                        wq_hi_part(0, h)
                    for p in range(PAIRS):
                        bq_hi_part(0, p)
                    wo_hi_part(0)
                    over_heads(act, slots)
                    pt(B * KVH - 1, None)
                    ot(B * KVH - 1, None)

                @block.gpsimd
                def _(pool):
                    def wq_lo_part(n, h):
                        pool.wait_ge(wq_hi_done, n)
                        cols = slice(h * D, (h + 1) * D)
                        pool.tensor_tensor(wq_lo[:, :, cols], wq_raw[:, :, cols], wq_hi[:, :, cols].bitcast(F32),
                                           ALU.subtract).then_inc(wq_lo_done, 1)

                    def rotate(n, half, h):
                        pool.wait_ge(q_mult, 3 * (n + 1))
                        if not isinstance(n, int) or n >= 2 * G:
                            pool.wait_ge(s_ready, n - G)
                        pool.tensor_tensor(qt[:, half, h, :], qc[:, :], qs[:, :], ALU.add).then_inc(q_done, 1)

                    def slots(g, first, last):
                        for b in range(B):
                            t = B * g + b
                            i = b % 2
                            if not (last and b >= HALF):
                                rotate(t + G, (b // HALF + 1) % 2, b % HALF)
                            pool.wait_ge(inv_done, t + 1)
                            pool.tensor_tensor(prob[i][:, :, :], prob[i][:, :, :], rinv[i][:, :].unsqueeze(2).broadcast_to([P, G, T]),
                                               ALU.mult).then_inc(prob_done, 1)
                            if not last and b < HALF:
                                wq_lo_part(G * (g + 1) + b + 1, b)

                    for h in range(G):
                        wq_lo_part(h + 1, h)
                    for h in range(G):
                        rotate(h, 0, h)
                    over_heads(pool, slots)

                @block.vector
                def _(dve):
                    def rotate(n, half):
                        tok = slice(half * HT, (half + 1) * HT)
                        dve.wait_ge(q_ready, n + 1)
                        if not isinstance(n, int) or n >= 1:
                            dve.wait_ge(q_done, n)
                        dve.tensor_tensor(qc[:, :], ps_q[:, :], cos_t[:, tok], ALU.mult).then_inc(q_mult, 1)
                        for to, at in ((0, 64), (64, 0)):
                            dve.tensor_tensor(qs[to:to + 64, :], ps_q[at:at + 64, :], sin_t[to:to + 64, tok],
                                              ALU.mult).then_inc(q_mult, 1)

                    def bq_lo_part(n, p):
                        dve.wait_ge(bq_hi_done, n)
                        lo = slice(P // 2, P)
                        dve.tensor_tensor(bq_pack[lo, p, :], bq_raw[lo, p, :], bq_pack[lo, p, :].bitcast(F32),
                                           ALU.subtract).then_inc(bq_lo_done, 1)

                    def wo_lo_part(g):
                        for h in range(G):
                            dve.wait_ge(wo_hi_done, G * g + h + 1)
                            dve.tensor_tensor(wo_lo[:, h, :], wo_raw[:, h, :], wo_hi[:, h, :].bitcast(F32), ALU.subtract).then_inc(wo_lo_done, 1)
                        dve.wait_ge(ao_hi_done, g + 1)
                        dve.tensor_tensor(ao_pack[:, :, :, 1, :], ao_raw[:, :, :, :], ao_pack[:, :, :, 0, :].bitcast(F32),
                                          ALU.subtract).then_inc(ao_lo_done, 1)

                    def pt(t):
                        dve.wait_ge(pt_hi_done, t + 1)
                        dve.tensor_tensor(pt_lo[:, :], ps_t[:, :], pt_hi[:, :].bitcast(F32), ALU.subtract).then_inc(pt_lo_done, 1)

                    def ot(t):
                        dve.wait_ge(ot_hi_done, t + 1)
                        dve.tensor_tensor(ot_lo[:, :], ps_o[:, :], ot_hi[:, :].bitcast(F32), ALU.subtract).then_inc(ot_lo_done, 1)

                    def add(t, b):
                        dve.wait_ge(out_ready, t + 1)
                        dve.tensor_tensor(res[:, b, :], ps_out[:, :], res[:, b, :], ALU.add).then_inc(res_done, 1)
                        dve.tensor_tensor(axo[:, b, :], ps_ao[0:2 * R, 0:T], axo[:, b, :], ALU.add).then_inc(axo_done, 1)

                    def slots(g, first, last):
                        for b in range(B):
                            t = B * g + b
                            i = b % 2
                            dve.wait_ge(s_ready, t + 1)
                            if not first or b >= 1:
                                dve.wait_ge(exp_done, t)
                            dve.memset(gate[:, :], 0.0)
                            for h in range(G):
                                m = dve.tensor_tensor_reduce(out=sm[:, h, :], in0=ps_s[:, h, :], in1=maskbias[:, b, :], scale=-1.0,
                                                             scalar=3.0e38, op0=ALU.add, op1=ALU.min, accum_out=nmax[i][:, h:h + 1])
                            m.then_inc(max_done, 1)
                            if not (last and b >= HALF):
                                rotate(t + G, (b // HALF + 1) % 2)
                            dve.wait_ge(exp_done, t + 1)
                            if not first or b >= 2:
                                dve.wait_ge(prob_done, t - 1)
                            dve.reciprocal(rinv[i][:, :], rsum[i][:, :]).then_inc(inv_done, 1)
                            if not first or b >= 1:
                                pt(t - 1)
                            if not first or b >= 2:
                                add(t - 2, (b - 2) % B)
                            if not first or b >= 1:
                                ot(t - 1)
                            if not last and b in (0, 2, 5, 7):
                                p = (0, 2, 5, 7).index(b)
                                bq_lo_part(PAIRS * (g + 1) + p + 1, p)
                            if b == 1 and not first:
                                wo_lo_part(g)

                    dve.memset(axo[:, :, :], 0.0).then_inc(axo_done, 1)
                    for p in range(PAIRS):
                        bq_lo_part(p + 1, p)
                    for h in range(G):
                        rotate(h, 0)
                    wo_lo_part(0)
                    over_heads(dve, slots)
                    end = B * KVH
                    pt(end - 1)
                    add(end - 2, B - 2)
                    ot(end - 1)
                    add(end - 1, B - 1)

                @block.tensor
                def _(pe):
                    def queries(n, half, h, pe_wait_pack):
                        if not isinstance(n, int) or n >= 1:
                            pe.wait_ge(q_mult, 3 * n)
                        pe.wait_ge(wq_lo_done, pe_wait_pack[0])
                        pe.wait_ge(bq_lo_done, pe_wait_pack[1])
                        project(pe, ps_q, wq_hi, wq_lo, bq_pack, axt[0], slice(h * D, (h + 1) * D), half).then_inc(q_ready, 1)

                    def scores(t, g, b):
                        half = b // HALF
                        pe.wait_ge(q_done, B * g + G * (half + 1))
                        pe.wait_ge(kt_in[half], 16 * (g + 1))
                        if not isinstance(t, int) or t >= 1:
                            pe.wait_ge(max_done, t)
                        at = (b % HALF) * T
                        for h in range(G):
                            mm = pe.matmul(ps_s[:, h, :], qt[:, half, h, at:at + T], kt[:, b * T:(b + 1) * T], start=True, stop=True)
                        mm.then_inc(s_ready, 1)

                    def turn(t, b):
                        pe.wait_ge(prob_done, t + 1)
                        if not isinstance(t, int) or t >= 1:
                            pe.wait_ge(pt_lo_done, t)
                        for h in range(G):
                            mm = pe.matmul(ps_t[:, h * T:(h + 1) * T], prob[b % 2][:, h, :], ident[:, :], start=True, stop=True)
                        mm.then_inc(t_ready, 1)

                    def values(t, g, b):
                        pe.wait_ge(v_in[b // HALF], 32 * (g + 1))
                        pe.wait_ge(pt_lo_done, t + 1)
                        if not isinstance(t, int) or t >= 1:
                            pe.wait_ge(ot_lo_done, t)
                        pe.matmul(ps_o[:, :], v_hi[:, b, :], pt_hi[:, :], start=True, stop=False)
                        pe.matmul(ps_o[:, :], v_hi[:, b, :], pt_lo[:, :], start=False, stop=False)
                        pe.matmul(ps_o[:, :], v_lo[:, b, :], pt_hi[:, :], start=False, stop=True).then_inc(o_ready, 1)

                    def outputs(t, g, b):
                        pe.wait_ge(ot_lo_done, t + 1)
                        pe.wait_ge(wo_lo_done, G * (g + 1))
                        pe.wait_ge(ao_lo_done, g + 1)
                        if not isinstance(t, int) or t >= 1:
                            pe.wait_ge(res_done, t)
                        for h in range(G):
                            q = slice(h * T, (h + 1) * T)
                            pe.matmul(ps_out[:, :], ot_hi[:, q], wo_hi[:, h, :], start=(h == 0), stop=False)
                            pe.matmul(ps_out[:, :], ot_hi[:, q], wo_lo[:, h, :], start=False, stop=False)
                            pe.matmul(ps_out[:, :], ot_lo[:, q], wo_hi[:, h, :], start=False, stop=(h == G - 1))
                        pe.wait_ge(axo_done, t + 1)
                        for h in range(G):
                            q = slice(h * T, (h + 1) * T)
                            w = ao_pack[:, b, h, :, :].rearrange("p a r -> p (a r)")
                            pe.matmul(ps_ao[0:2 * R, 0:T], w, ot_hi[:, q], start=(h == 0), stop=False)
                            mm = pe.matmul(ps_ao[0:2 * R, 0:T], w, ot_lo[:, q], start=False, stop=(h == G - 1))
                        mm.then_inc(out_ready, 1)

                    def slots(g, first, last):
                        for b in range(B):
                            t = B * g + b
                            scores(t, g, b)
                            if b < HALF:
                                queries(t + G, 1, b, (G * (g + 1), PAIRS * (g + 1)))
                            elif not last:
                                queries(t + G, 0, b - HALF, (G * (g + 1) + b - HALF + 1, PAIRS * (g + 1) + 2))
                            if not first or b >= 1:
                                turn(t - 1, (b - 1) % B)
                            if not first or b >= 2:
                                outputs(t - 2, g - 1 if b < 2 else g, (b - 2) % B)
                            if not first or b >= 1:
                                values(t - 1, g - 1 if b < 1 else g, (b - 1) % B)

                    for h in range(G):
                        queries(h, 0, h, (h + 1, PAIRS))
                    over_heads(pe, slots)
                    end, g = B * KVH, KVH - 1
                    turn(end - 1, B - 1)
                    outputs(end - 2, g, B - 2)
                    values(end - 1, g, B - 1)
                    outputs(end - 1, g, B - 1)
        attn.close()

        with ExitStack() as c:
            bo_sel = sb(c, "bo_sel", [2 * R, B, HID])
            l2b_sel = sb(c, "l2b_sel", [P, HID])
            l2a_sel = sb(c, "l2a_sel", [P, B, KC, R])
            l3a_sel = sb(c, "l3a_sel", [P, B, KC, R])
            l3b_sel = sb(c, "l3b_sel", [R, B, HID])
            w3_raw = sb(c, "w3_raw", [P, KC, HID])
            bias3 = sb(c, "bias3", [P, HID])
            w3t_hi = sb(c, "w3t_hi", [P, KC, HID], F32R)
            w3t_lo = sb(c, "w3t_lo", [P, KC, HID], F32R)
            l2bt = sb(c, "l2bt", [P, KC, P])
            l2at = sb(c, "l2at", [R, B, HID])
            x2t = sb(c, "x2t", [P, B, KC, T])
            x3t = sb(c, "x3t", [P, B, KC, T])
            x3t_hi = sb(c, "x3t_hi", [P, B, KC, T], F32R)
            x3t_lo = sb(c, "x3t_lo", [P, B, KC, T], F32R)
            h2 = sb(c, "h2", [R, B, T])
            h3 = sb(c, "h3", [R, B, T])
            y = sb(c, "y", [P, B, HID])
            ps_wide = [ps(c, f"ps_wide{i}", [P, HID]) for i in range(2)]
            ps_turn = [ps(c, f"ps_turn{i}", [P, HID]) for i in range(2)]
            ps_small = [ps(c, f"ps_small{i}", [P, 512]) for i in range(2)]
            bo_in = sem(c, "bo_in")
            w3_in = sem(c, "w3_in")
            l2_in = sem(c, "l2_in")
            l3_in = sem(c, "l3_in")
            wide_ready = sem(c, "wide_ready")
            wide_done = sem(c, "wide_done")
            turn_ready = sem(c, "turn_ready")
            turn_act = sem(c, "turn_act")
            turn_dve = sem(c, "turn_dve")
            small_ready = sem(c, "small_ready")
            small_done = sem(c, "small_done")
            bias_done = sem(c, "bias_done")
            y_out = sem(c, "y_out")
            L2B, L2A, X2 = KC, KC + 1, KC + 1 + B
            X3 = X2 + B

            def act_reads(n):
                return n + 1 if n < X3 else X3 + 2 * (n - X3 + 1)

            def dve_reads(n):
                return min(n + 1, KC) if n < X3 else KC + n - X3 + 1

            with nc.Block() as block:
                @block.sync
                def _(sp):
                    sp.dma_start(w3_raw[:, :, :], w3.rearrange("(c p) i -> p c i", p=P)).then_inc(w3_in, 16)
                    for b in range(B):
                        a = sp.value_load(id_rows[0:1, 1, b:b + 1], min_val=0, max_val=bo.shape[0] - 1)
                        for half in range(2):
                            sp.dma_start(bo_sel[half * R:(half + 1) * R, b, :], bo[bass.DynSlice(a, 1)].rearrange("a r n -> (a r) n")).then_inc(bo_in, 16)
                    for b in range(B):
                        a = sp.value_load(id_rows[0:1, 0, b:b + 1], min_val=0, max_val=l2a.shape[0] - 1)
                        sp.dma_start(l2b_sel[b * R:(b + 1) * R, :], l2b[bass.DynSlice(a, 1)].rearrange("a r n -> (a r) n")).then_inc(l2_in, 16)
                        sp.dma_start(l2a_sel[:, b, :, :], l2a[bass.DynSlice(a, 1)].rearrange("a (c p) r -> p (a c) r", p=P)).then_inc(l2_in, 16)
                    for b in range(B):
                        a = sp.value_load(id_rows[0:1, 2, b:b + 1], min_val=0, max_val=l3a.shape[0] - 1)
                        sp.dma_start(l3a_sel[:, b, :, :], l3a[bass.DynSlice(a, 1)].rearrange("a (c p) r -> p (a c) r", p=P)).then_inc(l3_in, 16)
                        sp.dma_start(l3b_sel[:, b, :], l3b[bass.DynSlice(a, 1)].rearrange("a r n -> (a r) n")).then_inc(l3_in, 16)
                    sp.dma_start(bias3[:, :], b3.partition_broadcast(P)).then_inc(l3_in, 16)
                    for b in range(B):
                        sp.wait_ge(wide_done, 2 * B + b + 1)
                        sp.dma_start(out[b], y[:, b, :]).then_inc(y_out, 16)
                    sp.wait_ge(y_out, 16 * B)

                @block.tensor
                def _(pe):
                    def turn(n, rows, tiles):
                        if n >= 2:
                            pe.wait_ge(turn_act, act_reads(n - 2))
                            pe.wait_ge(turn_dve, dve_reads(n - 2))
                        for k, tile in enumerate(tiles):
                            mm = pe.matmul(ps_turn[n % 2][0:rows, k * P:(k + 1) * P], tile, ident[:, :], start=True, stop=True)
                        mm.then_inc(turn_ready, 1)

                    def wide(n):
                        if n >= 2:
                            pe.wait_ge(wide_done, n - 1)
                        return ps_wide[n % 2][:, :]

                    def small(n):
                        if n >= 2:
                            pe.wait_ge(small_done, n - 1)
                        return ps_small[n % 2][0:R, 0:T]

                    pe.wait_ge(w3_in, 16)
                    for k in range(KC):
                        turn(k, P, [w3_raw[:, o, k * P:(k + 1) * P] for o in range(KC)])
                    pe.wait_ge(bo_in, 32 * B)
                    for b in range(B):
                        pe.matmul(wide(b), axo[:, b, :], bo_sel[:, b, :], start=True, stop=True).then_inc(wide_ready, 1)
                    pe.wait_ge(l2_in, 32 * B)
                    turn(L2B, P, [l2b_sel[:, k * P:(k + 1) * P] for k in range(KC)])
                    for b in range(B):
                        turn(L2A + b, R, [l2a_sel[:, b, k, :] for k in range(KC)])
                    for b in range(B):
                        pe.wait_ge(wide_done, b + 1)
                        turn(X2 + b, P, [res[:, b, k * P:(k + 1) * P] for k in range(KC)])
                    for b in range(B):
                        o = small(b)
                        pe.wait_ge(turn_act, act_reads(X2 + b))
                        for k in range(KC):
                            mm = pe.matmul(o, l2bt[:, k, b * R:(b + 1) * R], x2t[:, b, k, :], start=(k == 0), stop=(k == KC - 1))
                        mm.then_inc(small_ready, 1)
                    for b in range(B):
                        o = wide(B + b)
                        pe.wait_ge(small_done, b + 1)
                        pe.matmul(o, h2[:, b, :], l2at[:, b, :], start=True, stop=True).then_inc(wide_ready, 1)
                    for b in range(B):
                        pe.wait_ge(wide_done, B + b + 1)
                        turn(X3 + b, P, [res[:, b, k * P:(k + 1) * P] for k in range(KC)])
                    pe.wait_ge(l3_in, 32 * B + 16)
                    for b in range(B):
                        o = small(B + b)
                        pe.wait_ge(turn_act, act_reads(X3 + b))
                        for k in range(KC):
                            mm = pe.matmul(o, l3a_sel[:, b, k, :], x3t[:, b, k, :], start=(k == 0), stop=(k == KC - 1))
                        mm.then_inc(small_ready, 1)
                    for b in range(B):
                        o = wide(2 * B + b)
                        pe.wait_ge(turn_dve, dve_reads(X3 + b))
                        for k in range(KC):
                            pe.matmul(o, x3t_hi[:, b, k, :], w3t_hi[:, k, :], start=(k == 0), stop=False)
                            pe.matmul(o, x3t_hi[:, b, k, :], w3t_lo[:, k, :], start=False, stop=False)
                            pe.matmul(o, x3t_lo[:, b, k, :], w3t_hi[:, k, :], start=False, stop=False)
                        pe.wait_ge(small_done, B + b + 1)
                        pe.matmul(o, h3[:, b, :], l3b_sel[:, b, :], start=False, stop=True).then_inc(wide_ready, 1)

                @block.scalar
                def _(act):
                    def tile(n, rows=P):
                        act.wait_ge(turn_ready, n + 1)
                        return ps_turn[n % 2][0:rows, :]

                    for k in range(KC):
                        act.activation(w3t_hi[:, k, :], tile(k), ACT.Copy).then_inc(turn_act, 1)
                    act.activation(l2bt[:, :, :].rearrange("p c n -> p (c n)"), tile(L2B), ACT.Copy).then_inc(turn_act, 1)
                    for b in range(B):
                        act.activation(l2at[:, b, :], tile(L2A + b, R), ACT.Copy).then_inc(turn_act, 1)
                    for b in range(B):
                        act.activation(x2t[:, b, :, :].rearrange("p c n -> p (c n)"), tile(X2 + b), ACT.Copy).then_inc(turn_act, 1)
                    for b in range(B):
                        for dst in (x3t_hi, x3t):
                            act.activation(dst[:, b, :, :].rearrange("p c n -> p (c n)"), tile(X3 + b), ACT.Copy).then_inc(turn_act, 1)

                @block.vector
                def _(dve):
                    def add(n, dst):
                        b = n % B
                        dve.wait_ge(wide_ready, n + 1)
                        dve.tensor_tensor(dst[:, b, :], ps_wide[n % 2][:, :], res[:, b, :], ALU.add).then_inc(wide_done, 1)

                    for k in range(KC):
                        dve.wait_ge(turn_act, k + 1)
                        dve.tensor_tensor(w3t_lo[:, k, :], ps_turn[k % 2][:, :], w3t_hi[:, k, :].bitcast(F32), ALU.subtract).then_inc(turn_dve, 1)
                    for b in range(B):
                        add(b, res)
                    for b in range(B):
                        dve.wait_ge(small_ready, b + 1)
                        dve.tensor_copy(h2[:, b, :], ps_small[b % 2][0:R, 0:T]).then_inc(small_done, 1)
                    for b in range(B):
                        add(B + b, res)
                    for b in range(B):
                        dve.wait_ge(turn_act, act_reads(X3 + b))
                        dve.tensor_tensor(x3t_lo[:, b, :, :].rearrange("p c n -> p (c n)"), ps_turn[(X3 + b) % 2][:, :],
                                          x3t_hi[:, b, :, :].rearrange("p c n -> p (c n)").bitcast(F32), ALU.subtract).then_inc(turn_dve, 1)
                    for b in range(B):
                        dve.wait_ge(small_ready, B + b + 1)
                        dve.tensor_scalar(h3[:, b, :], ps_small[(B + b) % 2][0:R, 0:T], LORA_SCALE, None, ALU.mult).then_inc(small_done, 1)
                    for b in range(B):
                        dve.wait_ge(bias_done, b + 1)
                        add(2 * B + b, y)

                @block.gpsimd
                def _(pool):
                    pool.wait_ge(l3_in, 32 * B + 16)
                    for b in range(B):
                        pool.wait_ge(turn_ready, X3 + b + 1)
                        pool.tensor_tensor(res[:, b, :], res[:, b, :], bias3[:, :], ALU.add).then_inc(bias_done, 1)


_INS = ["x", "itok_B_3_7", "pos_BxS", "itok_B_0_7", "itok_B_0_23", "mask_BxS_bf1", "L0_cond_weight", "L1_cond_wq",
        "L1_cond_wk", "L1_cond_wv", "L1_cond_wo", "L1_cond_aq", "L1_cond_bq", "L1_cond_ak", "L1_cond_bk", "L1_cond_av",
        "L1_cond_bv", "L1_cond_ao", "L1_cond_bo", "L2_cond_A", "L2_cond_B", "L3_cond_W", "L3_cond_b",
        "L3_cond_lora_As", "L3_cond_lora_Bs"]


def constants():
    half = HEAD_DIM // 2
    freq = np.float32(THETA) ** (-np.arange(half, dtype=np.float32) / np.float32(half))
    root = float(HEAD_DIM) ** -0.25
    rope = np.zeros((P, 3), np.float32)
    rope[:, 0] = np.concatenate([freq, freq])
    rope[:, 1] = root
    rope[:half, 2] = -root
    rope[half:, 2] = root
    causal = np.where(np.tril(np.ones((P, P), bool)), 0.0, NEG).astype(np.float32)
    return {"ident_c": np.eye(P, dtype=np.float32), "causal_c": causal, "rope_c": rope}


def kernel(**inputs):
    import concourse.bacc as bacc
    from concourse.bass_utils import run_bass_kernel_spmd

    nc = bacc.Bacc("TRN2", target_bir_lowering=False, num_devices=1)
    arrays, args = {}, []
    for name, a in [(n, inputs[n]) for n in _INS] + list(constants().items()):
        a = np.ascontiguousarray(a)
        if a.dtype == bool:
            a = a.view(np.uint8)
        arrays[f"in_{name}"] = a
        args.append(nc.dram_tensor(f"in_{name}", a.shape, mybir.dt.from_np(a.dtype), kind="ExternalInput").ap())
    out = nc.dram_tensor("out_x", inputs["x"].shape, F32, kind="ExternalOutput").ap()
    program(nc, *args, out)
    result = run_bass_kernel_spmd(nc, [arrays], core_ids=[0])
    return result.results[0]["out_x"]
```

```python
from contextlib import ExitStack

import numpy as np

import concourse.bass as bass
from concourse import mybir

P = 128
F32 = mybir.dt.float32
F32R = mybir.dt.float32r
I32 = mybir.dt.int32
U8 = mybir.dt.uint8
ALU = mybir.AluOpType
ACT = mybir.ActivationFunctionType

NEG = -1.0e30
MAGIC = 1.5 * 2.0**23
TWO_PI = 2.0 * float(np.pi)
PI_A = 6.28125
PI_B = float(np.float32(np.floor((TWO_PI - PI_A) * 2.0**20) / 2.0**20))
PI_C = TWO_PI - PI_A - PI_B
PI_LIMIT = 3.1415925
THETA = 500000.0
HEAD_DIM = 128
R_PACK = 16
LORA_SCALE = 2.0


def program(nc, x, lora_ids, pos, attn_ids, slot_ids, mask, w0, wq, wk, wv, wo, aq, bq, ak, bk, av, bv, ao, bo,
            l2a, l2b, w3, b3, l3a, l3b, ident_c, causal_c, rope_c, gather_c, twin_c, out):
    B, T, HID = x.shape
    KC = HID // P
    D = P
    KVH = wk.shape[1] // D
    G = wq.shape[1] // wk.shape[1]
    R = aq.shape[2]
    NT = B * T
    assert R == R_PACK and KC * R * 2 == P
    HALF = B // 2
    HT = HALF * T
    PAIRS = B // 2
    GW = G * D

    bq_sel = nc.dram_tensor("bq_sel", (B, R, KVH * GW), F32, kind="Internal").ap()
    bkv_sel = nc.dram_tensor("bkv_sel", (B, R, 2, KVH * D), F32, kind="Internal").ap()
    ao_sel = nc.dram_tensor("ao_sel", (B, KVH * GW, R), F32, kind="Internal").ap()
    bo_sel = nc.dram_tensor("bo_sel", (B, R, HID), F32, kind="Internal").ap()
    l3b_sel = nc.dram_tensor("l3b_sel", (B, R, HID), F32, kind="Internal").ap()
    c_rows = nc.dram_tensor("c_rows", (B, R, HID), F32, kind="Internal").ap()
    m_rows = nc.dram_tensor("m_rows", (B, R, 2 * R), F32, kind="Internal").ap()
    k_rot = nc.dram_tensor("k_rot", (KVH, D, NT), F32, kind="Internal").ap()
    v_hi_d = nc.dram_tensor("v_hi_d", (KVH, T, B, D), F32, kind="Internal").ap()
    v_lo_d = nc.dram_tensor("v_lo_d", (KVH, T, B, D), F32, kind="Internal").ap()

    whole = ExitStack()
    with whole:
        def sb(ctx, name, shape, dt=F32):
            return ctx.enter_context(nc.sbuf_tensor(name, shape, dt))

        def ps(ctx, name, shape, dt=F32):
            return ctx.enter_context(nc.psum_tensor(name, shape, dt))

        def sem(ctx, name):
            return ctx.enter_context(nc.semaphore(name))

        def project(pe, bank, w_hi, w_lo, b_pack, ax, cols, half):
            tok = slice(half * HT, (half + 1) * HT)
            for k in range(KC):
                pe.matmul(bank[:, :], w_hi[:, k, cols], x1t_hi[:, k, tok], start=(k == 0), stop=False)
                pe.matmul(bank[:, :], w_hi[:, k, cols], x1t_lo[:, k, tok], start=False, stop=False)
                pe.matmul(bank[:, :], w_lo[:, k, cols], x1t_hi[:, k, tok], start=False, stop=False)
            for pair in range(PAIRS // 2):
                n = half * PAIRS // 2 + pair
                last = pe.matmul(bank[:, pair * 2 * T:(pair + 1) * 2 * T], b_pack[:, n, cols],
                                 ax[:, n * 2 * T:(n + 1) * 2 * T], start=False, stop=(pair == PAIRS // 2 - 1))
            return last

        res = sb(whole, "res", [P, B, HID])
        ident = sb(whole, "ident", [P, P])
        ident_r = sb(whole, "ident_r", [P, P], F32R)
        axo = sb(whole, "axo", [2 * R, B, T])
        id_rows = sb(whole, "id_rows", [1, 3, B], I32)
        raw_w = sb(whole, "raw_w", [P, KC, GW])
        raw_b = sb(whole, "raw_b", [P, PAIRS, GW])
        row_gather = sb(whole, "row_gather", [2 * R, 2, P])
        twin = sb(whole, "twin", [P, 2])
        l2b_sel = sb(whole, "l2b_sel", [P, HID])
        l2a_sel = sb(whole, "l2a_sel", [P, KC, B, R])
        l3a_sel = sb(whole, "l3a_sel", [P, KC, B, R])
        last_gathered = sem(whole, "last_gathered")
        w3_in = sem(whole, "w3_in")
        bo_in = sem(whole, "bo_in")
        l2_in = sem(whole, "l2_in")
        l3a_in = sem(whole, "l3a_in")

        attn = ExitStack()
        attn.__enter__()
        x1t_hi = sb(attn, "x1t_hi", [P, KC, NT], F32R)
        x1t_lo = sb(attn, "x1t_lo", [P, KC, NT], F32R)
        cos_t = sb(attn, "cos_t", [P, NT])
        sin_t = sb(attn, "sin_t", [P, NT])
        maskbias = sb(attn, "maskbias", [P, B, T])
        axt = [sb(attn, f"axt_{n}", [P, NT], F32R) for n in "qk"]

        blk_hi = [sb(attn, "blk_hi0", [P, KC, GW], F32R)]
        blk_lo = [sb(attn, "blk_lo0", [P, KC, GW], F32R)]
        blk_b = [sb(attn, "blk_b0", [P, PAIRS, GW], F32R)]
        VB = KVH * D // GW
        UNITS = B
        assert VB * GW == KVH * D and GW // D * 2 == UNITS and KC + PAIRS == UNITS

        def load_block(dma, n, w_in, b_in):
            kind, j = ((1, n), (0, n - VB), (2, 0))[min(n // VB, 2)]
            cols = slice(j * GW, (j + 1) * GW)
            dma.dma_start(raw_w[:, :, :], (wk, wv, wq)[kind][:, cols].rearrange("(c p) n -> p c n", p=P)).then_inc(w_in, 16)
            src = (bq_sel if kind == 2 else bkv_sel[:, :, kind, :]).rearrange("(c two) r n -> two r c n", two=2)[:, :, :, cols]
            for quad in range(4):
                for two in range(2):
                    at = 32 * quad + two * R
                    dma.dma_start(raw_b[at:at + R, :, :], src[two]).then_inc(b_in, 16)

        def load_rows(dma, pack, src, done):
            for quad in range(4):
                dma.dma_start(pack[32 * quad:32 * quad + 32, :, :], src.rearrange("(c two) r n -> (two r) c n", two=2)).then_inc(done, 16)

        mid = ExitStack()
        mid.__enter__()
        axt_v = sb(mid, "axt_v", [P, NT], F32R)
        with ExitStack() as c:
            w0_raw = [sb(c, f"w0_raw{i}", [P, KC, HID]) for i in range(2)]
            xt_hi = [sb(c, f"xt_hi{i}", [P, KC * T], F32R) for i in range(2)]
            xt_lo = [sb(c, f"xt_lo{i}", [P, KC * T], F32R) for i in range(2)]
            wt_hi = [sb(c, f"wt_hi{i}", [P, KC, HID], F32R) for i in range(2)]
            wt_lo = [sb(c, f"wt_lo{i}", [P, KC, HID], F32R) for i in range(2)]
            pos_i = sb(c, "pos_i", [P, NT], I32)
            ang = sb(c, "ang", [P, NT])
            turns = sb(c, "turns", [P, NT])
            rope_cols = sb(c, "rope_cols", [P, 3])
            mask_u8 = sb(c, "mask_u8", [P, NT], U8)
            causal = sb(c, "causal", [P, T])
            a_raw = sb(c, "a_raw", [P, B, KC, 3, R])
            a_hi = [sb(c, f"a_hi{i}", [P, KC, 3, R], F32R) for i in range(2)]
            a_lo = [sb(c, f"a_lo{i}", [P, KC, 3, R], F32R) for i in range(2)]
            axn = [sb(c, f"axn{i}", [P, 3, 4, 2, R], F32R) for i in range(2)]
            ps_ring = [ps(c, f"ps_ring{i}", [P, HID]) for i in range(3)]
            ps_y = [ps(c, f"ps_y{i}", [P, HID]) for i in range(2)]
            ps_x1 = ps(c, "ps_x1", [P, KC, T])
            ps_a = ps(c, "ps_a", [P, 3, R])
            ps_at = ps(c, "ps_at", [P, 3, T])
            ids_in = sem(c, "ids_in")
            consts_in = sem(c, "consts_in")
            tables_in = sem(c, "tables_in")
            x_in = [sem(c, f"x_in{b}") for b in range(B)]
            w0_in = [sem(c, f"w0_in{i}") for i in range(2)]
            a_in = [sem(c, f"a_in{b}") for b in range(B)]
            gathered_kv = sem(c, "gathered_kv")
            gathered = sem(c, "gathered")
            raw_w_in = sem(c, "raw_w_in")
            raw_b_in = sem(c, "raw_b_in")
            raw_hi_done = sem(c, "raw_hi_done")
            raw_lo_done = sem(c, "raw_lo_done")
            ident_ready = sem(c, "ident_ready")
            tile_ready = sem(c, "tile_ready")
            tile_hi_done = sem(c, "tile_hi_done")
            tile_lo_done = sem(c, "tile_lo_done")
            y_ready = sem(c, "y_ready")
            x1_done = sem(c, "x1_done")
            x1t_ready = sem(c, "x1t_ready")
            x1t_hi_done = sem(c, "x1t_hi_done")
            x1t_lo_done = sem(c, "x1t_lo_done")
            zeroed = sem(c, "zeroed")
            a_hi_done = sem(c, "a_hi_done")
            a_lo_done = sem(c, "a_lo_done")
            ax_ready = sem(c, "ax_ready")
            axn_done = sem(c, "axn_done")
            axt_ready = sem(c, "axt_ready")
            axt_done = sem(c, "axt_done")
            tab = sem(c, "tab")
            sines = sem(c, "sines")
            TILES = 1 + KC

            with nc.Block() as block:
                @block.sync
                def _(sp):
                    for n, ids in enumerate((lora_ids, attn_ids, slot_ids)):
                        sp.dma_start(id_rows[:, n, :], ids.rearrange("(a b) -> a b", a=1)).then_inc(ids_in, 16)
                    sp.dma_start(ident[:, :], ident_c).then_inc(consts_in, 16)
                    sp.dma_start(res[:, 0, :], x[0]).then_inc(x_in[0], 16)
                    sp.wait_ge(ids_in, 48)
                    for b in range(B):
                        a = sp.value_load(id_rows[0:1, 0, b:b + 1], min_val=0, max_val=w0.shape[0] - 1)
                        if b >= 2:
                            sp.wait_ge(tile_ready, TILES * (b - 1))
                        sp.dma_start(w0_raw[b % 2][:, :, :],
                                     w0[bass.DynSlice(a, 1), :, :].rearrange("a (c p) i -> p (a c) i", p=P)).then_inc(w0_in[b % 2], 16)
                        if b + 1 < B:
                            sp.dma_start(res[:, b + 1, :], x[b + 1]).then_inc(x_in[b + 1], 16)
                        pick = sp.value_load(id_rows[0:1, 1, b:b + 1], min_val=0, max_val=aq.shape[0] - 1)
                        for n, src in enumerate((aq, ak, av)):
                            sp.dma_start(a_raw[:, b, :, n, :],
                                         src[bass.DynSlice(pick, 1)].rearrange("a (c p) r -> p (a c) r", p=P)).then_inc(a_in[b], 16)
                        if b == 4:
                            sp.wait_ge(gathered_kv, 2 * B * 16)
                            load_block(sp, 0, raw_w_in, raw_b_in)

                @block.gpsimd
                def _(pool):
                    pool.dma_start(pos_i[:, :], pos.rearrange("b t -> (b t)").partition_broadcast(P)).then_inc(tables_in, 16)
                    pool.dma_start(mask_u8[:, :], mask.rearrange("b t -> (b t)").partition_broadcast(P)).then_inc(tables_in, 16)
                    pool.dma_start(causal[:, :], causal_c).then_inc(tables_in, 16)
                    pool.dma_start(rope_cols[:, :], rope_c).then_inc(tables_in, 16)
                    pool.wait_ge(ids_in, 48)
                    for b in range(B):
                        a = pool.value_load(id_rows[0:1, 1, b:b + 1], min_val=0, max_val=bq.shape[0] - 1)
                        pick = bass.DynSlice(a, 1)
                        pool.dma_start(bkv_sel[b:b + 1, :, 0, :], bk[pick]).then_inc(gathered_kv, 16)
                        pool.dma_start(bkv_sel[b:b + 1, :, 1, :], bv[pick]).then_inc(gathered_kv, 16)
                    for b in range(B):
                        a = pool.value_load(id_rows[0:1, 1, b:b + 1], min_val=0, max_val=bq.shape[0] - 1)
                        pick = bass.DynSlice(a, 1)
                        pool.dma_start(bq_sel[b:b + 1], bq[pick]).then_inc(gathered, 16)
                        pool.dma_start(ao_sel[b:b + 1], ao[pick]).then_inc(gathered, 16)
                    pool.wait_ge(tables_in, 64)
                    pool.wait_ge(gathered, 2 * B * 16)

                @block.tensor
                def _(pe):
                    def transposes(b):
                        pe.wait_ge(x_in[b], 16)
                        if b == 0:
                            pe.wait_ge(consts_in, 16)
                        for j in range(TILES):
                            m = TILES * b + j
                            if j == 1:
                                pe.wait_ge(w0_in[b % 2], 16 * (b // 2 + 1))
                            if m >= 3:
                                pe.wait_ge(tile_lo_done, m - 2)
                            for n in range(KC):
                                src = res[:, b, n * P:(n + 1) * P] if j == 0 else w0_raw[b % 2][:, n, (j - 1) * P:j * P]
                                mm = pe.matmul(ps_ring[m % 3][:, n * P:(n + 1) * P], src, ident[:, :], start=True, stop=True)
                            mm.then_inc(tile_ready, 1)

                    def product(b):
                        pe.wait_ge(tile_lo_done, TILES * b + 1)
                        if b >= 2:
                            pe.wait_ge(x1_done, b - 1)
                        i = b % 2
                        for k in range(KC):
                            pe.wait_ge(tile_lo_done, TILES * b + k + 2)
                            row = slice(k * T, (k + 1) * T)
                            pe.matmul(ps_y[i][:, :], xt_hi[i][:, row], wt_hi[i][:, k, :], start=(k == 0), stop=False)
                            pe.matmul(ps_y[i][:, :], xt_hi[i][:, row], wt_lo[i][:, k, :], start=False, stop=False)
                            mm = pe.matmul(ps_y[i][:, :], xt_lo[i][:, row], wt_hi[i][:, k, :], start=False, stop=(k == KC - 1))
                        mm.then_inc(y_ready, 1)

                    def turn_x1(b):
                        pe.wait_ge(x1_done, b + 1)
                        if b >= 1:
                            pe.wait_ge(x1t_lo_done, b)
                        for k in range(KC):
                            mm = pe.matmul(ps_x1[:, k, :], res[:, b, k * P:(k + 1) * P], ident[:, :], start=True, stop=True)
                        mm.then_inc(x1t_ready, 1)

                    def adapters(b):
                        i = b % 2
                        cols = slice(b * T, (b + 1) * T)
                        pe.wait_ge(x1t_lo_done, b + 1)
                        pe.wait_ge(a_lo_done, b + 1)
                        if b >= 1:
                            pe.wait_ge(axn_done, 4 * b)
                        for k in range(KC):
                            pe.matmul(ps_a[:, :, :], x1t_hi[:, k, cols], a_hi[i][:, k, :, :], start=(k == 0), stop=False)
                            pe.matmul(ps_a[:, :, :], x1t_hi[:, k, cols], a_lo[i][:, k, :, :], start=False, stop=False)
                            mm = pe.matmul(ps_a[:, :, :], x1t_lo[:, k, cols], a_hi[i][:, k, :, :], start=False, stop=(k == KC - 1))
                        mm.then_inc(ax_ready, 1)

                    def turn_ax(b):
                        pe.wait_ge(axn_done, 4 * b + 4)
                        if b == 0:
                            pe.wait_ge(ident_ready, 1)
                        else:
                            pe.wait_ge(axt_done, 3 * b)
                        for n in range(3):
                            mm = pe.matmul(ps_at[:, n, :], axn[b % 2][:, n, :, :, :].rearrange("p a b r -> p (a b r)"),
                                           ident_r[:, :], start=True, stop=True)
                        mm.then_inc(axt_ready, 1)

                    transposes(0)
                    for b in range(B + 3):
                        if b + 1 < B:
                            transposes(b + 1)
                        if b < B:
                            product(b)
                        if 1 <= b <= B:
                            turn_x1(b - 1)
                        if 2 <= b <= B + 1:
                            adapters(b - 2)
                        if b >= 3:
                            turn_ax(b - 3)

                @block.scalar
                def _(act):
                    def split(b):
                        i = b % 2
                        if b >= 2:
                            act.wait_ge(y_ready, b - 1)
                        for j in range(TILES):
                            m = TILES * b + j
                            act.wait_ge(tile_ready, m + 1)
                            act.activation(xt_hi[i][:, :] if j == 0 else wt_hi[i][:, j - 1, :], ps_ring[m % 3][:, :],
                                           ACT.Copy).then_inc(tile_hi_done, 1)

                    def split_x1(b):
                        act.wait_ge(x1t_ready, b + 1)
                        act.activation(x1t_hi[:, :, b * T:(b + 1) * T], ps_x1[:, :, :], ACT.Copy).then_inc(x1t_hi_done, 1)

                    def split_a(b):
                        act.wait_ge(a_in[b], 48)
                        if b >= 2:
                            act.wait_ge(ax_ready, b - 1)
                        act.activation(a_hi[b % 2][:, :, :, :], a_raw[:, b, :, :, :], ACT.Copy).then_inc(a_hi_done, 1)

                    def copy_axt(b):
                        act.wait_ge(axt_ready, b + 1)
                        cols = slice(b * T, (b + 1) * T)
                        for n, dst in enumerate((axt[0], axt[1], axt_v)):
                            act.activation(dst[:, cols], ps_at[:, n, :], ACT.Copy).then_inc(axt_done, 1)

                    act.wait_ge(consts_in, 16)
                    act.activation(ident_r[:, :], ident[:, :], ACT.Copy).then_inc(ident_ready, 1)
                    split(0)
                    for b in range(B + 3):
                        if b + 1 < B:
                            split(b + 1)
                        if 1 <= b <= B:
                            split_x1(b - 1)
                        if 1 <= b <= B:
                            split_a(b - 1)
                        if b >= 3:
                            copy_axt(b - 3)
                        if b == 2:
                            act.wait_ge(tab, 7)
                            act.activation(sin_t[:, :], ang[:, :], ACT.Sin).then_inc(sines, 1)
                        if b == 5:
                            act.wait_ge(tab, 15)
                            act.activation(cos_t[:, :], ang[:, :], ACT.Sin).then_inc(sines, 1)
                            act.wait_ge(raw_w_in, 16)
                        if b in (5, 6):
                            for k in range(2 * (b - 5), 2 * (b - 5) + 2):
                                act.activation(blk_hi[0][:, k, :], raw_w[:, k, :], ACT.Copy).then_inc(raw_hi_done, 1)
                        if b == 7:
                            act.wait_ge(raw_b_in, 128)
                            for p in range(PAIRS):
                                act.activation(blk_b[0][:, p, :], raw_b[:, p, :], ACT.Copy).then_inc(raw_hi_done, 1)

                @block.vector
                def _(dve):
                    def split(b):
                        i = b % 2
                        for j in range(TILES):
                            m = TILES * b + j
                            hi, lo = (xt_hi[i][:, :], xt_lo[i][:, :]) if j == 0 else (wt_hi[i][:, j - 1, :], wt_lo[i][:, j - 1, :])
                            dve.wait_ge(tile_hi_done, m + 1)
                            dve.tensor_tensor(lo, ps_ring[m % 3][:, :], hi.bitcast(F32), ALU.subtract).then_inc(tile_lo_done, 1)

                    def add(b):
                        dve.wait_ge(y_ready, b + 1)
                        dve.tensor_tensor(res[:, b, :], ps_y[b % 2][:, :], res[:, b, :], ALU.add).then_inc(x1_done, 1)

                    def split_x1(b):
                        dve.wait_ge(x1t_hi_done, b + 1)
                        cols = slice(b * T, (b + 1) * T)
                        dve.tensor_tensor(x1t_lo[:, :, cols], ps_x1[:, :, :], x1t_hi[:, :, cols].bitcast(F32),
                                          ALU.subtract).then_inc(x1t_lo_done, 1)

                    def split_a(b):
                        dve.wait_ge(a_hi_done, b + 1)
                        dve.tensor_tensor(a_lo[b % 2][:, :, :, :], a_raw[:, b, :, :, :], a_hi[b % 2][:, :, :, :].bitcast(F32),
                                          ALU.subtract).then_inc(a_lo_done, 1)

                    def pack_ax(b):
                        i = b % 2
                        dve.wait_ge(zeroed, i + 1)
                        dve.wait_ge(ax_ready, b + 1)
                        if b >= 2:
                            dve.wait_ge(axt_ready, b - 1)
                        for quad in (0, 2):
                            dve.tensor_copy(axn[i][:, :, quad, i, :], ps_a[:, :, :]).then_inc(axn_done, 1)
                        dve.wait_ge(axn_done, 4 * b + 2)
                        for quad in (1, 3):
                            dve.tensor_tensor(axn[i][:, :, quad, i, :], ps_a[:, :, :],
                                              axn[i][:, :, 0, i, :].bitcast(F32), ALU.subtract).then_inc(axn_done, 1)

                    steps = [0]

                    def step(instruction):
                        steps[0] += 1
                        instruction.then_inc(tab, 1)
                        dve.wait_ge(tab, steps[0])

                    def angles(quarter, part):
                        if part == 0:
                            if quarter:
                                dve.wait_ge(sines, 1)
                            else:
                                dve.wait_ge(tables_in, 64)
                            step(dve.tensor_scalar(ang[:, :], pos_i[:, :], rope_cols[:, 0:1], None, ALU.mult))
                            step(dve.tensor_scalar(turns[:, :], ang[:, :], 1.0 / TWO_PI, quarter, ALU.mult, ALU.add))
                            step(dve.tensor_scalar(turns[:, :], turns[:, :], MAGIC, -MAGIC, ALU.add, ALU.add))
                        elif part == 1:
                            for share in (PI_A, PI_B):
                                step(dve.scalar_tensor_tensor(ang[:, :], turns[:, :], -share, ang[:, :], ALU.mult, ALU.add))
                        else:
                            step(dve.scalar_tensor_tensor(ang[:, :], turns[:, :], -PI_C, ang[:, :], ALU.mult, ALU.add))
                            if quarter:
                                step(dve.tensor_scalar(ang[:, :], ang[:, :], TWO_PI / 4, None, ALU.add))
                            step(dve.tensor_scalar(ang[:, :], ang[:, :], PI_LIMIT, -PI_LIMIT, ALU.min, ALU.max))

                    def scale_tables():
                        dve.wait_ge(sines, 2)
                        step(dve.tensor_scalar(cos_t[:, :], cos_t[:, :], rope_cols[:, 1:2], None, ALU.mult))
                        step(dve.tensor_scalar(sin_t[:, :], sin_t[:, :], rope_cols[:, 2:3], None, ALU.mult))

                    def mask_table():
                        mb = maskbias[:, :, :].rearrange("p b t -> p (b t)")
                        step(dve.tensor_scalar(mb, mask_u8[:, :], -NEG, NEG, ALU.mult, ALU.add))
                        for b in range(B):
                            step(dve.tensor_tensor(maskbias[:, b, :], maskbias[:, b, :], causal[:, :], ALU.min))

                    def block_lo(first, last):
                        low = slice(P // 2, P)
                        for u in range(first, last):
                            dve.wait_ge(raw_hi_done, u + 1)
                            if u < KC:
                                dve.tensor_tensor(blk_lo[0][:, u, :], raw_w[:, u, :], blk_hi[0][:, u, :].bitcast(F32),
                                                  ALU.subtract).then_inc(raw_lo_done, 1)
                            else:
                                p = u - KC
                                dve.tensor_tensor(blk_b[0][low, p, :], raw_b[low, p, :], blk_b[0][low, p, :].bitcast(F32),
                                                  ALU.subtract).then_inc(raw_lo_done, 1)

                    def tables(b):
                        if b < 3:
                            angles(0.0, b)
                        elif b < 6:
                            angles(0.25, b - 3)
                        elif b == 6:
                            mask_table()
                            block_lo(0, 2)
                        elif b == 7:
                            block_lo(2, 4)
                            scale_tables()

                    for i in range(2):
                        dve.memset(axn[i][:, :, :, :, :].bitcast(F32), 0.0).then_inc(zeroed, 1)
                    split(0)
                    for b in range(B + 3):
                        if b + 1 < B:
                            split(b + 1)
                        if b < B:
                            tables(b)
                            add(b)
                        if 1 <= b <= B:
                            split_x1(b - 1)
                            split_a(b - 1)
                        if 2 <= b <= B + 1:
                            pack_ax(b - 2)
                        if b == B:
                            block_lo(KC, UNITS)

        with ExitStack() as c:
            blk_hi.append(sb(c, "blk_hi1", [P, KC, GW], F32R))
            blk_lo.append(sb(c, "blk_lo1", [P, KC, GW], F32R))
            blk_b.append(sb(c, "blk_b1", [P, PAIRS, GW], F32R))
            v_hi = [sb(c, f"v_hi{i}", [P, GW], F32R) for i in range(2)]
            v_lo = [sb(c, f"v_lo{i}", [P, GW], F32R) for i in range(2)]
            k_cos = [sb(c, f"k_cos{i}", [P, HT]) for i in range(2)]
            k_sin = [sb(c, f"k_sin{i}", [P, HT]) for i in range(2)]
            kr = [sb(c, f"kr{i}", [P, HT]) for i in range(2)]
            ps_p = [ps(c, f"ps_p{i}", [P, GW]) for i in range(4)]
            raw_w_in = sem(c, "raw_w_in2")
            raw_b_in = sem(c, "raw_b_in2")
            raw_hi_done = sem(c, "raw_hi_done2")
            raw_lo_done = sem(c, "raw_lo_done2")
            p_ready = sem(c, "p_ready")
            v_hi_done = sem(c, "v_hi_done")
            v_lo_done = sem(c, "v_lo_done")
            v_out = [sem(c, f"v_out{i}") for i in range(2)]
            k_mult = sem(c, "k_mult")
            k_done = sem(c, "k_done")
            k_out = [sem(c, f"k_out{i}") for i in range(2)]
            BLOCKS = 2 * VB
            VU = VB * UNITS

            with nc.Block() as block:
                @block.sync
                def _(sp):
                    load_block(sp, 1, raw_w_in, raw_b_in)
                    for n in range(BLOCKS * UNITS):
                        i = n % 2
                        if n < VU:
                            h, b = divmod(n, UNITS)
                            sp.wait_ge(v_lo_done, n + 1)
                            g = slice(h * GW // D, (h + 1) * GW // D)
                            for src, dst in ((v_hi, v_hi_d), (v_lo, v_lo_d)):
                                sp.dma_start(dst[g, :, b, :].rearrange("g t d -> t g d"),
                                             src[i][:, :].bitcast(F32).rearrange("t (g d) -> t g d", d=D)).then_inc(v_out[i], 16)
                        else:
                            g, h = divmod(n - VU, 2)
                            sp.wait_ge(k_done, n - VU + 1)
                            sp.dma_start(k_rot[g, :, h * HT:(h + 1) * HT], kr[i][:, :]).then_inc(k_out[i], 16)
                        if n % UNITS == UNITS - 1 and n // UNITS + 2 <= BLOCKS:
                            block_n = n // UNITS + 2
                            sp.wait_ge(raw_lo_done, UNITS * (block_n - 1))
                            load_block(sp, block_n, raw_w_in, raw_b_in)
                    for i in range(2):
                        sp.wait_ge(v_out[i], 16 * VU)
                        sp.wait_ge(k_out[i], 16 * VU // 2)

                @block.scalar
                def _(act):
                    for n in range(BLOCKS * UNITS):
                        blk, u = divmod(n, UNITS)
                        if n < VU:
                            act.wait_ge(p_ready, n + 1)
                            if n >= 2:
                                act.wait_ge(v_out[n % 2], 32 * (n // 2))
                            act.activation(v_hi[n % 2][:, :], ps_p[n % 4][:, :], ACT.Copy).then_inc(v_hi_done, 1)
                        i = (blk + 1) % 2
                        if u == 0:
                            act.wait_ge(raw_w_in, 16 * (blk + 1))
                            act.wait_ge(raw_b_in, 128 * (blk + 1))
                            act.wait_ge(p_ready, UNITS * blk)
                        if u < KC:
                            act.activation(blk_hi[i][:, u, :], raw_w[:, u, :], ACT.Copy).then_inc(raw_hi_done, 1)
                        else:
                            act.activation(blk_b[i][:, u - KC, :], raw_b[:, u - KC, :], ACT.Copy).then_inc(raw_hi_done, 1)

                @block.vector
                def _(dve):
                    low = slice(P // 2, P)
                    for n in range(BLOCKS * UNITS):
                        blk, u = divmod(n, UNITS)
                        if n < VU:
                            dve.wait_ge(v_hi_done, n + 1)
                            dve.tensor_tensor(v_lo[n % 2][:, :], ps_p[n % 4][:, :], v_hi[n % 2][:, :].bitcast(F32),
                                              ALU.subtract).then_inc(v_lo_done, 1)
                        else:
                            m, half = n - VU, n % 2
                            tok = slice(half * HT, (half + 1) * HT)
                            dve.wait_ge(p_ready, n + 1)
                            if m >= 2:
                                dve.wait_ge(k_done, m - 1)
                            dve.tensor_tensor(k_cos[half][:, :], ps_p[n % 4][:, :], cos_t[:, tok], ALU.mult).then_inc(k_mult, 1)
                            for to, at in ((0, 64), (64, 0)):
                                dve.tensor_tensor(k_sin[half][to:to + 64, :], ps_p[n % 4][at:at + 64, :], sin_t[to:to + 64, tok],
                                                  ALU.mult).then_inc(k_mult, 1)
                        i = (blk + 1) % 2
                        dve.wait_ge(raw_hi_done, n + 1)
                        if u < KC:
                            dve.tensor_tensor(blk_lo[i][:, u, :], raw_w[:, u, :], blk_hi[i][:, u, :].bitcast(F32),
                                              ALU.subtract).then_inc(raw_lo_done, 1)
                        else:
                            p = u - KC
                            dve.tensor_tensor(blk_b[i][low, p, :], raw_b[low, p, :], blk_b[i][low, p, :].bitcast(F32),
                                              ALU.subtract).then_inc(raw_lo_done, 1)

                @block.gpsimd
                def _(pool):
                    for b in range(B):
                        a = pool.value_load(id_rows[0:1, 1, b:b + 1], min_val=0, max_val=bo.shape[0] - 1)
                        pool.dma_start(bo_sel[b:b + 1], bo[bass.DynSlice(a, 1)]).then_inc(last_gathered, 16)
                        a = pool.value_load(id_rows[0:1, 2, b:b + 1], min_val=0, max_val=l3b.shape[0] - 1)
                        pool.dma_start(l3b_sel[b:b + 1], l3b[bass.DynSlice(a, 1)]).then_inc(last_gathered, 16)
                    for m in range(VU):
                        i = m % 2
                        pool.wait_ge(k_mult, 3 * m + 3)
                        if m >= 2:
                            pool.wait_ge(k_out[i], 16 * (m // 2))
                        pool.tensor_tensor(kr[i][:, :], k_cos[i][:, :], k_sin[i][:, :], ALU.add).then_inc(k_done, 1)

                @block.tensor
                def _(pe):
                    for n in range(BLOCKS * UNITS):
                        blk, u = divmod(n, UNITS)
                        i = blk % 2
                        if u == 0 and blk >= 1:
                            pe.wait_ge(raw_lo_done, UNITS * blk)
                        if 4 <= n < VU + 4:
                            pe.wait_ge(v_lo_done, n - 3)
                        elif n >= 4:
                            pe.wait_ge(k_mult, 3 * (n - VU - 3))
                        if n < VU:
                            tok = slice(u * T, (u + 1) * T)
                            o = ps_p[n % 4][:, :]
                            for k in range(KC):
                                pe.matmul(o, x1t_hi[:, k, tok], blk_hi[i][:, k, :], start=(k == 0), stop=False)
                                pe.matmul(o, x1t_hi[:, k, tok], blk_lo[i][:, k, :], start=False, stop=False)
                                pe.matmul(o, x1t_lo[:, k, tok], blk_hi[i][:, k, :], start=False, stop=False)
                            pe.matmul(o, axt_v[:, tok], blk_b[i][:, u // 2, :], start=False, stop=True).then_inc(p_ready, 1)
                        else:
                            head = slice(u // 2 * D, (u // 2 + 1) * D)
                            project(pe, ps_p[n % 4], blk_hi[i], blk_lo[i], blk_b[i], axt[1], head, n % 2).then_inc(p_ready, 1)
        mid.close()

        with ExitStack() as c:
            wq_raw, bq_raw, wq_hi, wq_lo, bq_pack = raw_w, raw_b, blk_hi[0], blk_lo[0], blk_b[0]
            wo_raw = sb(c, "wo_raw", [P, G, HID])
            wo_hi = sb(c, "wo_hi", [P, G, HID], F32R)
            wo_lo = sb(c, "wo_lo", [P, G, HID], F32R)
            ao_raw = sb(c, "ao_raw", [P, B, G, R])
            ao_pack = sb(c, "ao_pack", [P, B, G, 2, R], F32R)
            kt = sb(c, "kt", [P, NT])
            v_hi = sb(c, "v_hi3", [P, B, D], F32R)
            v_lo = sb(c, "v_lo3", [P, B, D], F32R)
            qc = sb(c, "qc", [P, HT])
            qs = sb(c, "qs", [P, HT])
            qt = sb(c, "qt", [P, 2, G, HT])
            gate = sb(c, "gate", [P, 1])
            sm = sb(c, "sm", [P, G, T])
            nmax = [sb(c, f"nmax{i}", [P, G]) for i in range(2)]
            rsum = [sb(c, f"rsum{i}", [P, G]) for i in range(2)]
            rinv = [sb(c, f"rinv{i}", [P, G]) for i in range(2)]
            prob = [sb(c, f"prob{i}", [P, G, T]) for i in range(2)]
            pt_hi = sb(c, "pt_hi", [P, G * T], F32R)
            pt_lo = sb(c, "pt_lo", [P, G * T], F32R)
            ot_hi = sb(c, "ot_hi", [P, G * T], F32R)
            ot_lo = sb(c, "ot_lo", [P, G * T], F32R)
            ps_s = ps(c, "ps_s", [P, G, T])
            ps_q = ps(c, "ps_q", [P, HT])
            ps_t = ps(c, "ps_t", [P, G * T])
            ps_o = ps(c, "ps_o", [P, G * T])
            ps_out = ps(c, "ps_out", [P, HID])
            ps_ao = ps(c, "ps_ao", [P, 512])
            wq_in = sem(c, "wq_in")
            wo_in = sem(c, "wo_in")
            bq_in = [sem(c, f"bq_in{i}") for i in range(2)]
            ao_in = sem(c, "ao_in")
            kt_in = [sem(c, f"kt_in{i}") for i in range(2)]
            v_in = [sem(c, f"v_in{i}") for i in range(2)]
            wq_hi_done = sem(c, "wq_hi_done")
            wq_lo_done = sem(c, "wq_lo_done")
            wo_hi_done = sem(c, "wo_hi_done")
            wo_lo_done = sem(c, "wo_lo_done")
            bq_hi_done = sem(c, "bq_hi_done")
            bq_lo_done = sem(c, "bq_lo_done")
            ao_hi_done = sem(c, "ao_hi_done")
            ao_lo_done = sem(c, "ao_lo_done")
            s_ready = sem(c, "s_ready")
            q_ready = sem(c, "q_ready")
            q_mult = sem(c, "q_mult")
            q_done = sem(c, "q_done")
            max_done = sem(c, "max_done")
            exp_done = sem(c, "exp_done")
            inv_done = sem(c, "inv_done")
            prob_done = sem(c, "prob_done")
            t_ready = sem(c, "t_ready")
            pt_hi_done = sem(c, "pt_hi_done")
            pt_lo_done = sem(c, "pt_lo_done")
            o_ready = sem(c, "o_ready")
            ot_hi_done = sem(c, "ot_hi_done")
            ot_lo_done = sem(c, "ot_lo_done")
            out_ready = sem(c, "out_ready")
            res_done = sem(c, "res_done")
            axo_done = sem(c, "axo_done")

            def over_heads(eng, slots):
                slots(0, True, False)
                with eng.Fori(1, KVH - 1) as g:
                    slots(g, False, False)
                slots(KVH - 1, False, True)

            with nc.Block() as block:
                @block.sync
                def _(sp):
                    def load_wq(g):
                        sp.dma_start(wq_raw[:, :, :], wq[:, bass.DynSlice(g * GW, GW)].rearrange("(c p) n -> p c n", p=P)).then_inc(wq_in, 16)

                    def load_bq(g, h):
                        for quad in range(4):
                            sp.dma_start(bq_raw[32 * quad:32 * quad + 32, 2 * h:2 * h + 2, :],
                                         bq_sel.rearrange("(c two) r n -> (two r) c n", two=2)[:, 2 * h:2 * h + 2, bass.DynSlice(g * GW, GW)]
                                         ).then_inc(bq_in[h], 16)

                    def load_wo(g):
                        sp.dma_start(wo_raw[:, :, :], wo[bass.DynSlice(g * GW, GW), :].rearrange("(h p) n -> p h n", p=P)).then_inc(wo_in, 16)
                        for b in range(B):
                            sp.dma_start(ao_raw[:, b, :, :], ao_sel[b, bass.DynSlice(g * GW, GW), :].rearrange("(h p) r -> p h r", p=P)).then_inc(ao_in, 16)

                    def load_kv(g, h):
                        one = bass.DynSlice(g, 1)
                        cols, half = slice(h * HT, (h + 1) * HT), slice(h * HALF, (h + 1) * HALF)
                        sp.dma_start(kt[:, cols], k_rot[one, :, cols].rearrange("a p t -> p (a t)")).then_inc(kt_in[h], 16)
                        sp.dma_start(v_hi[:, half, :].bitcast(F32), v_hi_d[one, :, half, :].rearrange("a p b d -> p (a b) d")).then_inc(v_in[h], 16)
                        sp.dma_start(v_lo[:, half, :].bitcast(F32), v_lo_d[one, :, half, :].rearrange("a p b d -> p (a b) d")).then_inc(v_in[h], 16)

                    load_kv(0, 0)
                    load_wo(0)
                    load_kv(0, 1)
                    load_wq(1)
                    load_bq(1, 0)
                    load_bq(1, 1)

                    def slots(g, first, last):
                        if last:
                            return
                        sp.wait_ge(wo_lo_done, G * (g + 1))
                        sp.wait_ge(ao_lo_done, g + 1)
                        load_wo(g + 1)
                        if not (isinstance(g, int) and g + 2 >= KVH):
                            next_raw(g)
                        sp.wait_ge(s_ready, B * g + HALF)
                        sp.wait_ge(o_ready, B * g + HALF)
                        load_kv(g + 1, 0)
                        sp.wait_ge(s_ready, B * g + B)
                        sp.wait_ge(o_ready, B * g + B)
                        load_kv(g + 1, 1)

                    def next_raw(g):
                        sp.wait_ge(wq_lo_done, G * (g + 1))
                        load_wq(g + 2)
                        sp.wait_ge(bq_lo_done, PAIRS * g + 2)
                        load_bq(g + 2, 0)

                    def next_raw_late(g):
                        sp.wait_ge(bq_lo_done, PAIRS * (g + 1))
                        load_bq(g + 2, 1)

                    def body(g):
                        slots(g, False, False)
                        next_raw_late(g)

                    body(0)
                    with sp.Fori(1, KVH - 2) as g:
                        body(g)
                    slots(KVH - 2, False, False)

                    sp.wait_ge(wq_lo_done, G * (KVH - 1))
                    sp.dma_start(raw_w[:, :, :], w3.rearrange("(c p) i -> p c i", p=P)).then_inc(w3_in, 16)
                    sp.dma_start(row_gather[:, :, :], gather_c).then_inc(w3_in, 16)
                    sp.dma_start(twin[:, :], twin_c).then_inc(w3_in, 16)
                    sp.wait_ge(bq_lo_done, PAIRS * (KVH - 1))
                    sp.wait_ge(last_gathered, 2 * B * 16)
                    load_rows(sp, raw_b, bo_sel, bo_in)
                    for b in range(B):
                        a = sp.value_load(id_rows[0:1, 0, b:b + 1], min_val=0, max_val=l2a.shape[0] - 1)
                        sp.dma_start(l2b_sel[b * R:(b + 1) * R, :], l2b[bass.DynSlice(a, 1)].rearrange("a r n -> (a r) n")).then_inc(l2_in, 16)
                        sp.dma_start(l2a_sel[:, :, b, :], l2a[bass.DynSlice(a, 1)].rearrange("a (c p) r -> p (a c) r", p=P)).then_inc(l2_in, 16)
                    for b in range(B):
                        a = sp.value_load(id_rows[0:1, 2, b:b + 1], min_val=0, max_val=l3a.shape[0] - 1)
                        sp.dma_start(l3a_sel[:, :, b, :], l3a[bass.DynSlice(a, 1)].rearrange("a (c p) r -> p (a c) r", p=P)).then_inc(l3a_in, 16)

                @block.scalar
                def _(act):
                    def wq_hi_part(g, h):
                        act.wait_ge(wq_in, 16 * g)
                        cols = slice(h * D, (h + 1) * D)
                        act.activation(wq_hi[:, :, cols], wq_raw[:, :, cols], ACT.Copy).then_inc(wq_hi_done, 1)

                    def bq_hi_part(g, p):
                        act.wait_ge(bq_in[p // 2], 64 * g)
                        act.activation(bq_pack[:, p, :], bq_raw[:, p, :], ACT.Copy).then_inc(bq_hi_done, 1)

                    def wo_hi_part(g):
                        act.wait_ge(wo_in, 16 * (g + 1))
                        for h in range(G):
                            act.activation(wo_hi[:, h, :], wo_raw[:, h, :], ACT.Copy).then_inc(wo_hi_done, 1)
                        act.wait_ge(ao_in, 16 * B * (g + 1))
                        act.activation(ao_pack[:, :, :, 0, :], ao_raw[:, :, :, :], ACT.Copy).then_inc(ao_hi_done, 1)

                    def pt(t, i):
                        act.wait_ge(t_ready, t + 1)
                        if i is None or i >= 1:
                            act.wait_ge(o_ready, t)
                        act.activation(pt_hi[:, :], ps_t[:, :], ACT.Copy).then_inc(pt_hi_done, 1)

                    def ot(t, i):
                        act.wait_ge(o_ready, t + 1)
                        if i is None or i >= 1:
                            act.wait_ge(out_ready, t)
                        act.activation(ot_hi[:, :], ps_o[:, :], ACT.Copy).then_inc(ot_hi_done, 1)

                    def slots(g, first, last):
                        for b in range(B):
                            t = B * g + b
                            number = t if first else None
                            act.wait_ge(max_done, t + 1)
                            if not first or b >= 2:
                                act.wait_ge(t_ready, t - 1)
                            i = b % 2
                            for h in range(G):
                                e = act.activation(prob[i][:, h, :], sm[:, h, :], ACT.Exp, bias=nmax[i][:, h:h + 1], scale=-1.0,
                                                   accum_out=rsum[i][:, h:h + 1])
                            e.then_inc(exp_done, 1)
                            if b < HALF and not last:
                                act.wait_ge(q_ready, B * g + G + b + 1)
                                wq_hi_part(g + 1, b)
                            if not last and b in (0, 2, 5, 7):
                                p = (0, 2, 5, 7).index(b)
                                act.wait_ge(q_ready, B * g + (G if p < 2 else B))
                                bq_hi_part(g + 1, p)
                            if not first or b >= 1:
                                pt(t - 1, None if not first else t - 1)
                                ot(t - 1, None if not first else t - 1)
                            if b == 1 and not first:
                                act.wait_ge(out_ready, B * g)
                                wo_hi_part(g)

                    wo_hi_part(0)
                    over_heads(act, slots)
                    pt(B * KVH - 1, None)
                    ot(B * KVH - 1, None)

                @block.gpsimd
                def _(pool):
                    def wq_lo_part(n, h):
                        pool.wait_ge(wq_hi_done, n)
                        cols = slice(h * D, (h + 1) * D)
                        pool.tensor_tensor(wq_lo[:, :, cols], wq_raw[:, :, cols], wq_hi[:, :, cols].bitcast(F32),
                                           ALU.subtract).then_inc(wq_lo_done, 1)

                    def rotate(n, half, h):
                        pool.wait_ge(q_mult, 3 * (n + 1))
                        if not isinstance(n, int) or n >= 2 * G:
                            pool.wait_ge(s_ready, n - G)
                        pool.tensor_tensor(qt[:, half, h, :], qc[:, :], qs[:, :], ALU.add).then_inc(q_done, 1)

                    def slots(g, first, last):
                        for b in range(B):
                            t = B * g + b
                            i = b % 2
                            if not (last and b >= HALF):
                                rotate(t + G, (b // HALF + 1) % 2, b % HALF)
                            pool.wait_ge(inv_done, t + 1)
                            pool.tensor_tensor(prob[i][:, :, :], prob[i][:, :, :], rinv[i][:, :].unsqueeze(2).broadcast_to([P, G, T]),
                                               ALU.mult).then_inc(prob_done, 1)
                            if not last and b < HALF:
                                wq_lo_part(G * g + b + 1, b)

                    for h in range(G):
                        rotate(h, 0, h)
                    over_heads(pool, slots)

                @block.vector
                def _(dve):
                    def rotate(n, half):
                        tok = slice(half * HT, (half + 1) * HT)
                        dve.wait_ge(q_ready, n + 1)
                        if not isinstance(n, int) or n >= 1:
                            dve.wait_ge(q_done, n)
                        dve.tensor_tensor(qc[:, :], ps_q[:, :], cos_t[:, tok], ALU.mult).then_inc(q_mult, 1)
                        for to, at in ((0, 64), (64, 0)):
                            dve.tensor_tensor(qs[to:to + 64, :], ps_q[at:at + 64, :], sin_t[to:to + 64, tok],
                                              ALU.mult).then_inc(q_mult, 1)

                    def bq_lo_part(n, p):
                        dve.wait_ge(bq_hi_done, n)
                        lo = slice(P // 2, P)
                        dve.tensor_tensor(bq_pack[lo, p, :], bq_raw[lo, p, :], bq_pack[lo, p, :].bitcast(F32),
                                           ALU.subtract).then_inc(bq_lo_done, 1)

                    def wo_lo_part(g):
                        for h in range(G):
                            dve.wait_ge(wo_hi_done, G * g + h + 1)
                            dve.tensor_tensor(wo_lo[:, h, :], wo_raw[:, h, :], wo_hi[:, h, :].bitcast(F32), ALU.subtract).then_inc(wo_lo_done, 1)
                        dve.wait_ge(ao_hi_done, g + 1)
                        dve.tensor_tensor(ao_pack[:, :, :, 1, :], ao_raw[:, :, :, :], ao_pack[:, :, :, 0, :].bitcast(F32),
                                          ALU.subtract).then_inc(ao_lo_done, 1)

                    def pt(t):
                        dve.wait_ge(pt_hi_done, t + 1)
                        dve.tensor_tensor(pt_lo[:, :], ps_t[:, :], pt_hi[:, :].bitcast(F32), ALU.subtract).then_inc(pt_lo_done, 1)

                    def ot(t):
                        dve.wait_ge(ot_hi_done, t + 1)
                        dve.tensor_tensor(ot_lo[:, :], ps_o[:, :], ot_hi[:, :].bitcast(F32), ALU.subtract).then_inc(ot_lo_done, 1)

                    def add(t, b):
                        dve.wait_ge(out_ready, t + 1)
                        dve.tensor_tensor(res[:, b, :], ps_out[:, :], res[:, b, :], ALU.add).then_inc(res_done, 1)
                        dve.tensor_tensor(axo[:, b, :], ps_ao[0:2 * R, 0:T], axo[:, b, :], ALU.add).then_inc(axo_done, 1)

                    def slots(g, first, last):
                        for b in range(B):
                            t = B * g + b
                            i = b % 2
                            dve.wait_ge(s_ready, t + 1)
                            if not first or b >= 1:
                                dve.wait_ge(exp_done, t)
                            dve.memset(gate[:, :], 0.0)
                            for h in range(G):
                                m = dve.tensor_tensor_reduce(out=sm[:, h, :], in0=ps_s[:, h, :], in1=maskbias[:, b, :], scale=-1.0,
                                                             scalar=3.0e38, op0=ALU.add, op1=ALU.min, accum_out=nmax[i][:, h:h + 1])
                            m.then_inc(max_done, 1)
                            if not (last and b >= HALF):
                                rotate(t + G, (b // HALF + 1) % 2)
                            dve.wait_ge(exp_done, t + 1)
                            if not first or b >= 2:
                                dve.wait_ge(prob_done, t - 1)
                            dve.reciprocal(rinv[i][:, :], rsum[i][:, :]).then_inc(inv_done, 1)
                            if not first or b >= 1:
                                pt(t - 1)
                            if not first or b >= 2:
                                add(t - 2, (b - 2) % B)
                            if not first or b >= 1:
                                ot(t - 1)
                            if not last and b in (0, 2, 5, 7):
                                p = (0, 2, 5, 7).index(b)
                                bq_lo_part(PAIRS * g + p + 1, p)
                            if b == 1 and not first:
                                wo_lo_part(g)

                    dve.memset(axo[:, :, :], 0.0).then_inc(axo_done, 1)
                    for h in range(G):
                        rotate(h, 0)
                    wo_lo_part(0)
                    over_heads(dve, slots)
                    end = B * KVH
                    pt(end - 1)
                    add(end - 2, B - 2)
                    ot(end - 1)
                    add(end - 1, B - 1)

                @block.tensor
                def _(pe):
                    def queries(n, half, h, weights=None):
                        if not isinstance(n, int) or n >= 1:
                            pe.wait_ge(q_mult, 3 * n)
                        if weights:
                            pe.wait_ge(wq_lo_done, weights[0])
                            pe.wait_ge(bq_lo_done, weights[1])
                        project(pe, ps_q, wq_hi, wq_lo, bq_pack, axt[0], slice(h * D, (h + 1) * D), half).then_inc(q_ready, 1)

                    def scores(t, g, b):
                        half = b // HALF
                        pe.wait_ge(q_done, B * g + G * (half + 1))
                        pe.wait_ge(kt_in[half], 16 * (g + 1))
                        if not isinstance(t, int) or t >= 1:
                            pe.wait_ge(max_done, t)
                        at = (b % HALF) * T
                        for h in range(G):
                            mm = pe.matmul(ps_s[:, h, :], qt[:, half, h, at:at + T], kt[:, b * T:(b + 1) * T], start=True, stop=True)
                        mm.then_inc(s_ready, 1)

                    def turn(t, b):
                        pe.wait_ge(prob_done, t + 1)
                        if not isinstance(t, int) or t >= 1:
                            pe.wait_ge(pt_lo_done, t)
                        for h in range(G):
                            mm = pe.matmul(ps_t[:, h * T:(h + 1) * T], prob[b % 2][:, h, :], ident[:, :], start=True, stop=True)
                        mm.then_inc(t_ready, 1)

                    def values(t, g, b):
                        pe.wait_ge(v_in[b // HALF], 32 * (g + 1))
                        pe.wait_ge(pt_lo_done, t + 1)
                        if not isinstance(t, int) or t >= 1:
                            pe.wait_ge(ot_lo_done, t)
                        pe.matmul(ps_o[:, :], v_hi[:, b, :], pt_hi[:, :], start=True, stop=False)
                        pe.matmul(ps_o[:, :], v_hi[:, b, :], pt_lo[:, :], start=False, stop=False)
                        pe.matmul(ps_o[:, :], v_lo[:, b, :], pt_hi[:, :], start=False, stop=True).then_inc(o_ready, 1)

                    def outputs(t, g, b):
                        pe.wait_ge(ot_lo_done, t + 1)
                        pe.wait_ge(wo_lo_done, G * (g + 1))
                        pe.wait_ge(ao_lo_done, g + 1)
                        if not isinstance(t, int) or t >= 1:
                            pe.wait_ge(res_done, t)
                        for h in range(G):
                            q = slice(h * T, (h + 1) * T)
                            pe.matmul(ps_out[:, :], ot_hi[:, q], wo_hi[:, h, :], start=(h == 0), stop=False)
                            pe.matmul(ps_out[:, :], ot_hi[:, q], wo_lo[:, h, :], start=False, stop=False)
                            pe.matmul(ps_out[:, :], ot_lo[:, q], wo_hi[:, h, :], start=False, stop=(h == G - 1))
                        pe.wait_ge(axo_done, t + 1)
                        for h in range(G):
                            q = slice(h * T, (h + 1) * T)
                            w = ao_pack[:, b, h, :, :].rearrange("p a r -> p (a r)")
                            pe.matmul(ps_ao[0:2 * R, 0:T], w, ot_hi[:, q], start=(h == 0), stop=False)
                            mm = pe.matmul(ps_ao[0:2 * R, 0:T], w, ot_lo[:, q], start=False, stop=(h == G - 1))
                        mm.then_inc(out_ready, 1)

                    def slots(g, first, last):
                        for b in range(B):
                            t = B * g + b
                            scores(t, g, b)
                            if b < HALF:
                                queries(t + G, 1, b, None if first else (G * g, PAIRS * g))
                            elif not last:
                                queries(t + G, 0, b - HALF, (G * g + b - HALF + 1, PAIRS * g + 2))
                            if not first or b >= 1:
                                turn(t - 1, (b - 1) % B)
                            if not first or b >= 2:
                                outputs(t - 2, g - 1 if b < 2 else g, (b - 2) % B)
                            if not first or b >= 1:
                                values(t - 1, g - 1 if b < 1 else g, (b - 1) % B)

                    for h in range(G):
                        queries(h, 0, h)
                    over_heads(pe, slots)
                    end, g = B * KVH, KVH - 1
                    turn(end - 1, B - 1)
                    outputs(end - 2, g, B - 2)
                    values(end - 1, g, B - 1)
                    outputs(end - 1, g, B - 1)
        attn.close()

        with ExitStack() as c:
            bo_pack = sb(c, "bo_pack", [P, PAIRS, HID], F32R)
            axo_pack = sb(c, "axo_pack", [P, B, T], F32R)
            w3t_hi = sb(c, "w3t_hi", [P, KC, HID], F32R)
            w3t_lo = sb(c, "w3t_lo", [P, KC, HID], F32R)
            l2b_hi = sb(c, "l2b_hi", [P, KC, PAIRS, 4, 2 * R], F32R)
            l2b_lo = sb(c, "l2b_lo", [P, KC, PAIRS, 4, 2 * R], F32R)
            l3a_hi = sb(c, "l3a_hi", [P, KC, PAIRS, 4, 2 * R], F32R)
            l3a_lo = sb(c, "l3a_lo", [P, KC, PAIRS, 4, 2 * R], F32R)
            l2a_hi = sb(c, "l2a_hi", [P, KC, B * R], F32R)
            l2a_lo = sb(c, "l2a_lo", [P, KC, B * R], F32R)
            cm = sb(c, "cm", [P, HID])
            mm_sb = sb(c, "mm_sb", [P, 2 * R])
            c_raw = sb(c, "c_raw", [P, PAIRS, HID])
            c_pack = sb(c, "c_pack", [P, PAIRS, HID], F32R)
            m_raw = sb(c, "m_raw", [P, PAIRS, 2 * R])
            m_pack = sb(c, "m_pack", [P, PAIRS, 4, 2 * R], F32R)
            l3b_raw = sb(c, "l3b_raw", [P, PAIRS, HID])
            l3b_pack = sb(c, "l3b_pack", [P, PAIRS, HID], F32R)
            bias3 = sb(c, "bias3", [P, HID])
            x2t_hi = sb(c, "x2t_hi", [P, B, KC, T], F32R)
            x2t_lo = sb(c, "x2t_lo", [P, B, KC, T], F32R)
            own = [sb(c, f"own{i}", [P, 2, T]) for i in range(2)]
            h2_pack = sb(c, "h2_pack", [P, B, T], F32R)
            h3_pack = sb(c, "h3_pack", [P, B, T], F32R)
            ps_wide = [ps(c, f"ps_wide{i}", [P, HID]) for i in range(3)]
            ps_turn = [ps(c, f"ps_turn{i}", [P, HID]) for i in range(3)]
            ps_h = [ps(c, f"ps_h{i}", [P, 512]) for i in range(2)]
            l3b_in = sem(c, "l3b_in")
            bias_in = sem(c, "bias_in")
            axo_ready = sem(c, "axo_ready")
            axo_hi_done = sem(c, "axo_hi_done")
            axo_lo_done = sem(c, "axo_lo_done")
            turn_ready = sem(c, "turn_ready")
            turn_hi_done = sem(c, "turn_hi_done")
            turn_lo_done = sem(c, "turn_lo_done")
            l2a_hi_done = sem(c, "l2a_hi_done")
            l2a_lo_done = sem(c, "l2a_lo_done")
            l3a_hi_done = sem(c, "l3a_hi_done")
            l3a_lo_done = sem(c, "l3a_lo_done")
            bo_hi_done = sem(c, "bo_hi_done")
            bo_lo_done = sem(c, "bo_lo_done")
            wide_ready = sem(c, "wide_ready")
            wide_done = sem(c, "wide_done")
            m_ready = sem(c, "m_ready")
            m_done = sem(c, "m_done")
            m_out = sem(c, "m_out")
            m_in = sem(c, "m_in")
            c_out = sem(c, "c_out")
            c_in = sem(c, "c_in")
            c_hi_done = sem(c, "c_hi_done")
            c_lo_done = sem(c, "c_lo_done")
            m_hi_done = sem(c, "m_hi_done")
            m_lo_done = sem(c, "m_lo_done")
            l3b_hi_done = sem(c, "l3b_hi_done")
            l3b_lo_done = sem(c, "l3b_lo_done")
            h_ready = sem(c, "h_ready")
            own_done = sem(c, "own_done")
            h_hi_done = sem(c, "h_hi_done")
            h_lo_done = sem(c, "h_lo_done")
            bias_done = sem(c, "bias_done")
            y_out = sem(c, "y_out")
            L2B, X2 = KC, KC + 1
            CW = B

            with nc.Block() as block:
                @block.sync
                def _(sp):
                    load_rows(sp, l3b_raw, l3b_sel, l3b_in)
                    sp.dma_start(bias3[:, :], b3.partition_broadcast(P)).then_inc(bias_in, 16)
                    sp.wait_ge(m_done, PAIRS)
                    sp.dma_start(m_rows.rearrange("b r n -> (b r) n"), mm_sb[:, :]).then_inc(m_out, 16)
                    sp.wait_ge(m_out, 16)
                    load_rows(sp, m_raw, m_rows, m_in)
                    sp.wait_ge(wide_done, CW + 1)
                    sp.dma_start(c_rows.rearrange("b r n -> (b r) n"), cm[:, :]).then_inc(c_out, 16)
                    sp.wait_ge(c_out, 16)
                    load_rows(sp, c_raw, c_rows, c_in)
                    for b in range(B):
                        sp.wait_ge(wide_done, CW + 1 + b + 1)
                        sp.dma_start(out[b], res[:, b, :]).then_inc(y_out, 16)
                    sp.wait_ge(y_out, 16 * B)

                @block.tensor
                def _(pe):
                    def turn(n, tiles):
                        if n >= 3:
                            pe.wait_ge(turn_lo_done, n - 2)
                        for k, tile in enumerate(tiles):
                            mm = pe.matmul(ps_turn[n % 3][:, k * P:(k + 1) * P], tile, ident[:, :], start=True, stop=True)
                        mm.then_inc(turn_ready, 1)

                    def wide(n):
                        if n >= 3:
                            pe.wait_ge(wide_done, n - 2)
                        return ps_wide[n % 3][:, :]

                    def narrow(n, hi, lo):
                        o = ps_h[n % 2][:, 0:2 * T]
                        pair = n % PAIRS
                        both = slice(2 * pair, 2 * pair + 2)
                        pe.wait_ge(turn_lo_done, X2 + 2 * pair + 2)
                        if n >= 2:
                            pe.wait_ge(own_done, n - 1)
                        for k in range(KC):
                            w_hi = hi[:, k, pair, :, :].rearrange("p q r -> p (q r)")
                            w_lo = lo[:, k, pair, :, :].rearrange("p q r -> p (q r)")
                            pe.matmul(o, w_hi, x2t_hi[:, both, k, :], start=(k == 0), stop=False)
                            pe.matmul(o, w_hi, x2t_lo[:, both, k, :], start=False, stop=False)
                            mm = pe.matmul(o, w_lo, x2t_hi[:, both, k, :], start=False, stop=(k == KC - 1 and n < PAIRS))
                        return o, mm

                    pe.wait_ge(w3_in, 48)
                    for i in range(2):
                        pe.matmul(ps_h[i][:, :], row_gather[:, i, :], axo[:, i:B:2, :], start=True, stop=True).then_inc(axo_ready, 1)
                    for k in range(KC):
                        turn(k, [raw_w[:, o, k * P:(k + 1) * P] for o in range(KC)])
                    pe.wait_ge(l2_in, 32 * B)
                    turn(L2B, [l2b_sel[:, k * P:(k + 1) * P] for k in range(KC)])
                    pe.wait_ge(axo_lo_done, 4)
                    pe.wait_ge(bo_lo_done, 1)
                    for b in range(B):
                        pe.matmul(wide(b), axo_pack[:, b, :], bo_pack[:, b // 2, :], start=True, stop=True).then_inc(wide_ready, 1)
                    pe.wait_ge(l3a_in, 16 * B)
                    for k in range(KC):
                        mm = pe.matmul(ps_h[0][:, 0:P], l2a_sel[:, k, :, :].rearrange("p b r -> p (b r)"),
                                       l3a_sel[:, k, :, :].rearrange("p b r -> p (b r)"), start=(k == 0), stop=(k == KC - 1))
                    mm.then_inc(m_ready, 1)
                    o = wide(CW)
                    pe.wait_ge(l2a_lo_done, 1)
                    pe.wait_ge(turn_lo_done, KC)
                    for k in range(KC):
                        pe.matmul(o, l2a_hi[:, k, :], w3t_hi[:, k, :], start=(k == 0), stop=False)
                        pe.matmul(o, l2a_hi[:, k, :], w3t_lo[:, k, :], start=False, stop=False)
                        pe.matmul(o, l2a_lo[:, k, :], w3t_hi[:, k, :], start=False, stop=False)
                    for k in range(KC):
                        mm = pe.matmul(o[:, k * P:(k + 1) * P], l2a_sel[:, k, :, :].rearrange("p b r -> p (b r)"), ident[:, :],
                                       start=False, stop=(k == KC - 1))
                    mm.then_inc(wide_ready, 1)
                    for b in range(B):
                        pe.wait_ge(wide_done, b + 1)
                        turn(X2 + b, [res[:, b, k * P:(k + 1) * P] for k in range(KC)])
                    pe.wait_ge(m_done, PAIRS)
                    for pair in range(PAIRS):
                        o, mm = narrow(pair, l2b_hi, l2b_lo)
                        mm.then_inc(h_ready, 1)
                    pe.wait_ge(l3a_lo_done, 4)
                    pe.wait_ge(m_lo_done, 1)
                    for pair in range(PAIRS):
                        o, mm = narrow(PAIRS + pair, l3a_hi, l3a_lo)
                        pe.wait_ge(h_lo_done, 2 * pair + 2)
                        pe.matmul(o, m_pack[:, pair, :, :].rearrange("p q r -> p (q r)"), h2_pack[:, 2 * pair:2 * pair + 2, :],
                                  start=False, stop=True).then_inc(h_ready, 1)
                    for b in range(B):
                        o = wide(CW + 1 + b)
                        for k in range(KC):
                            pe.matmul(o, x2t_hi[:, b, k, :], w3t_hi[:, k, :], start=(k == 0), stop=False)
                            pe.matmul(o, x2t_hi[:, b, k, :], w3t_lo[:, k, :], start=False, stop=False)
                            pe.matmul(o, x2t_lo[:, b, k, :], w3t_hi[:, k, :], start=False, stop=False)
                        pe.wait_ge(c_lo_done, 1)
                        pe.matmul(o, h2_pack[:, b, :], c_pack[:, b // 2, :], start=False, stop=False)
                        pe.wait_ge(l3b_lo_done, 1)
                        pe.wait_ge(h_lo_done, 2 * (PAIRS + b // 2) + 2)
                        pe.matmul(o, h3_pack[:, b, :], l3b_pack[:, b // 2, :], start=False, stop=True).then_inc(wide_ready, 1)

                @block.scalar
                def _(act):
                    def tile(n):
                        act.wait_ge(turn_ready, n + 1)
                        return ps_turn[n % 3]

                    def pack_hi(n, pack):
                        pair = n % PAIRS
                        act.wait_ge(own_done, n + 1)
                        act.activation(pack[:, 2 * pair:2 * pair + 2, :], own[n % 2][:, :, :], ACT.Copy).then_inc(h_hi_done, 1)

                    act.wait_ge(bo_in, 64)
                    act.activation(bo_pack[:, :, :], raw_b[:, :, :], ACT.Copy).then_inc(bo_hi_done, 1)
                    for i in range(2):
                        act.wait_ge(axo_ready, i + 1)
                        act.activation(axo_pack[:, i:B:2, :], ps_h[i][:, :].rearrange("p (b t) -> p b t", t=T), ACT.Copy).then_inc(axo_hi_done, 1)
                    for k in range(KC):
                        act.activation(w3t_hi[:, k, :], tile(k)[:, :], ACT.Copy).then_inc(turn_hi_done, 1)
                    bank = tile(L2B)[:, :].rearrange("p (k c r) -> p k c r", k=KC, c=PAIRS)
                    for quad in range(4):
                        act.activation(l2b_hi[:, :, :, quad, :], bank, ACT.Copy).then_inc(turn_hi_done, 1)
                    act.activation(l2a_hi[:, :, :], l2a_sel[:, :, :, :].rearrange("p k b r -> p k (b r)"), ACT.Copy).then_inc(l2a_hi_done, 1)
                    for b in range(B):
                        act.activation(x2t_hi[:, b, :, :].rearrange("p c n -> p (c n)"), tile(X2 + b)[:, :], ACT.Copy).then_inc(turn_hi_done, 1)
                        if b == 0:
                            act.wait_ge(l3a_in, 16 * B)
                        if b < 4:
                            act.activation(l3a_hi[:, :, :, b, :], l3a_sel[:, :, :, :].rearrange("p k (c two) r -> p k c (two r)", two=2),
                                           ACT.Copy).then_inc(l3a_hi_done, 1)
                    for pair in range(PAIRS):
                        pack_hi(pair, h2_pack)
                        if pair == 0:
                            act.wait_ge(m_in, 64)
                            for quad in range(4):
                                act.activation(m_pack[:, :, quad, :], m_raw[:, :, :], ACT.Copy).then_inc(m_hi_done, 1)
                        if pair == 1:
                            act.wait_ge(c_in, 64)
                            act.activation(c_pack[:, :, :], c_raw[:, :, :], ACT.Copy).then_inc(c_hi_done, 1)
                        if pair == 2:
                            act.wait_ge(l3b_in, 64)
                            act.activation(l3b_pack[:, :, :], l3b_raw[:, :, :], ACT.Copy).then_inc(l3b_hi_done, 1)
                    for pair in range(PAIRS):
                        pack_hi(PAIRS + pair, h3_pack)

                @block.vector
                def _(dve):
                    low = slice(P // 2, P)

                    def tile(n):
                        dve.wait_ge(turn_hi_done, n + 1 if n < L2B else n + 4)
                        return ps_turn[n % 3]

                    def add(n, dst):
                        dve.wait_ge(wide_ready, n + 1)
                        dve.tensor_tensor(dst, ps_wide[n % 3][:, :], dst, ALU.add).then_inc(wide_done, 1)

                    def own_columns(n, scale):
                        dve.wait_ge(h_ready, n + 1)
                        if n >= 2:
                            dve.wait_ge(h_hi_done, n - 1)
                            dve.wait_ge(h_lo_done, 2 * (n - 1))
                        dve.scalar_tensor_tensor(own[n % 2][:, :, :], ps_h[n % 2][:, 0:2 * T].rearrange("p (a t) -> p a t", t=T), scale,
                                                 twin[:, :].unsqueeze(2).broadcast_to([P, 2, T]), ALU.mult, ALU.mult).then_inc(own_done, 1)

                    def pack_lo(n, pack):
                        both = slice(2 * (n % PAIRS), 2 * (n % PAIRS) + 2)
                        dve.wait_ge(h_hi_done, n + 1)
                        for at in (32, 96):
                            dve.tensor_tensor(pack[at:at + 32, both, :], own[n % 2][at:at + 32, :, :],
                                              pack[at:at + 32, both, :].bitcast(F32), ALU.subtract).then_inc(h_lo_done, 1)

                    def low_half(pack, raw):
                        return dve.tensor_tensor(pack[low], raw[low], pack[low].bitcast(F32), ALU.subtract)

                    for i in range(2):
                        dve.wait_ge(axo_hi_done, i + 1)
                        for at in (32, 96):
                            dve.tensor_tensor(axo_pack[at:at + 32, i:B:2, :], ps_h[i][at:at + 32, :].rearrange("p (b t) -> p b t", t=T),
                                              axo_pack[at:at + 32, i:B:2, :].bitcast(F32), ALU.subtract).then_inc(axo_lo_done, 1)
                    for k in range(KC):
                        tile(k)
                        dve.tensor_tensor(w3t_lo[:, k, :], ps_turn[k % 3][:, :], w3t_hi[:, k, :].bitcast(F32), ALU.subtract).then_inc(turn_lo_done, 1)
                        if k == 1:
                            dve.wait_ge(bo_hi_done, 1)
                            low_half(bo_pack, raw_b).then_inc(bo_lo_done, 1)
                    for b in range(B):
                        add(b, res[:, b, :])
                    dve.wait_ge(l2a_hi_done, 1)
                    dve.tensor_tensor(l2a_lo[:, :, :], l2a_sel[:, :, :, :].rearrange("p k b r -> p k (b r)"), l2a_hi[:, :, :].bitcast(F32),
                                      ALU.subtract).then_inc(l2a_lo_done, 1)
                    bank = tile(L2B)[:, :].rearrange("p (k c r) -> p k c r", k=KC, c=PAIRS)
                    for quad in range(4):
                        lo = dve.tensor_tensor(l2b_lo[:, :, :, quad, :], bank, l2b_hi[:, :, :, quad, :].bitcast(F32), ALU.subtract)
                    lo.then_inc(turn_lo_done, 1)
                    dve.wait_ge(m_ready, 1)
                    for pair in range(PAIRS):
                        rows = slice(2 * R * pair, 2 * R * (pair + 1))
                        dve.tensor_copy(mm_sb[rows, :], ps_h[0][rows, rows]).then_inc(m_done, 1)
                    dve.wait_ge(wide_ready, CW + 1)
                    dve.tensor_copy(cm[:, :], ps_wide[CW % 3][:, :]).then_inc(wide_done, 1)
                    for b in range(B):
                        tile(X2 + b)
                        dve.tensor_tensor(x2t_lo[:, b, :, :].rearrange("p c n -> p (c n)"), ps_turn[(X2 + b) % 3][:, :],
                                          x2t_hi[:, b, :, :].rearrange("p c n -> p (c n)").bitcast(F32), ALU.subtract).then_inc(turn_lo_done, 1)
                    for pair in range(PAIRS):
                        own_columns(pair, 1.0)
                        pack_lo(pair, h2_pack)
                        if pair == 0:
                            dve.wait_ge(m_hi_done, 4)
                            for quad in range(4):
                                lo = dve.tensor_tensor(m_pack[low, :, quad, :], m_raw[low, :, :], m_pack[low, :, quad, :].bitcast(F32), ALU.subtract)
                            lo.then_inc(m_lo_done, 1)
                    dve.wait_ge(c_hi_done, 1)
                    low_half(c_pack, c_raw).then_inc(c_lo_done, 1)
                    for pair in range(PAIRS):
                        own_columns(PAIRS + pair, LORA_SCALE)
                        pack_lo(PAIRS + pair, h3_pack)
                    dve.wait_ge(l3b_hi_done, 1)
                    low_half(l3b_pack, l3b_raw).then_inc(l3b_lo_done, 1)
                    for b in range(B):
                        dve.wait_ge(bias_done, b + 1)
                        add(CW + 1 + b, res[:, b, :])

                @block.gpsimd
                def _(pool):
                    for quad in range(4):
                        pool.wait_ge(l3a_hi_done, quad + 1)
                        pool.tensor_tensor(l3a_lo[:, :, :, quad, :], l3a_sel[:, :, :, :].rearrange("p k (c two) r -> p k c (two r)", two=2),
                                           l3a_hi[:, :, :, quad, :].bitcast(F32), ALU.subtract).then_inc(l3a_lo_done, 1)
                    pool.wait_ge(bias_in, 16)
                    for b in range(B):
                        pool.wait_ge(turn_ready, X2 + b + 1)
                        pool.tensor_tensor(res[:, b, :], res[:, b, :], bias3[:, :], ALU.add).then_inc(bias_done, 1)


_INS = ["x", "itok_B_3_7", "pos_BxS", "itok_B_0_7", "itok_B_0_23", "mask_BxS_bf1", "L0_cond_weight", "L1_cond_wq",
        "L1_cond_wk", "L1_cond_wv", "L1_cond_wo", "L1_cond_aq", "L1_cond_bq", "L1_cond_ak", "L1_cond_bk", "L1_cond_av",
        "L1_cond_bv", "L1_cond_ao", "L1_cond_bo", "L2_cond_A", "L2_cond_B", "L3_cond_W", "L3_cond_b",
        "L3_cond_lora_As", "L3_cond_lora_Bs"]


def constants():
    half = HEAD_DIM // 2
    freq = np.float32(THETA) ** (-np.arange(half, dtype=np.float32) / np.float32(half))
    root = float(HEAD_DIM) ** -0.25
    rope = np.zeros((P, 3), np.float32)
    rope[:, 0] = np.concatenate([freq, freq])
    rope[:, 1] = root
    rope[:half, 2] = -root
    rope[half:, 2] = root
    causal = np.where(np.tril(np.ones((P, P), bool)), 0.0, NEG).astype(np.float32)
    row, col = np.arange(2 * R_PACK)[:, None], np.arange(P)[None, :]
    twin = np.stack([(np.arange(P) // R_PACK) % 2 == i for i in range(2)], 1).astype(np.float32)
    gather = np.stack([(row % R_PACK == col % R_PACK) & (col // R_PACK % 2 == i) for i in range(2)], 1).astype(np.float32)
    return {"ident_c": np.eye(P, dtype=np.float32), "causal_c": causal, "rope_c": rope, "gather_c": gather, "twin_c": twin}


def kernel(**inputs):
    import concourse.bacc as bacc
    from concourse.bass_utils import run_bass_kernel_spmd

    nc = bacc.Bacc("TRN2", target_bir_lowering=False, num_devices=1)
    arrays, args = {}, []
    for name, a in [(n, inputs[n]) for n in _INS] + list(constants().items()):
        a = np.ascontiguousarray(a)
        if a.dtype == bool:
            a = a.view(np.uint8)
        arrays[f"in_{name}"] = a
        args.append(nc.dram_tensor(f"in_{name}", a.shape, mybir.dt.from_np(a.dtype), kind="ExternalInput").ap())
    out = nc.dram_tensor("out_x", inputs["x"].shape, F32, kind="ExternalOutput").ap()
    program(nc, *args, out)
    result = run_bass_kernel_spmd(nc, [arrays], core_ids=[0])
    return result.results[0]["out_x"]
```

```python
from contextlib import ExitStack

import numpy as np

import concourse.bass as bass
from concourse import mybir

P = 128
F32 = mybir.dt.float32
F32R = mybir.dt.float32r
F16 = mybir.dt.float16
I32 = mybir.dt.int32
U8 = mybir.dt.uint8
ALU = mybir.AluOpType
ACT = mybir.ActivationFunctionType

NEG = -1.0e30
MAGIC = 1.5 * 2.0**23
TWO_PI = 2.0 * float(np.pi)
PI_A = 6.28125
PI_B = float(np.float32(np.floor((TWO_PI - PI_A) * 2.0**20) / 2.0**20))
PI_C = TWO_PI - PI_A - PI_B
PI_LIMIT = 3.1415925
THETA = 500000.0
HEAD_DIM = 128
R_PACK = 16
P_SCALE = 4096.0
LORA_SCALE = 2.0


def program(nc, x, lora_ids, pos, attn_ids, slot_ids, mask, w0, wq, wk, wv, wo, aq, bq, ak, bk, av, bv, ao, bo,
            l2a, l2b, w3, b3, l3a, l3b, ident_c, causal_c, rope_c, gather_c, twin_c, out):
    B, T, HID = x.shape
    KC = HID // P
    D = P
    KVH = wk.shape[1] // D
    G = wq.shape[1] // wk.shape[1]
    R = aq.shape[2]
    NT = B * T
    assert R == R_PACK and KC * R * 2 == P
    HALF = B // 2
    HT = HALF * T
    PAIRS = B // 2
    GW = G * D

    bq_sel = nc.dram_tensor("bq_sel", (B, R, KVH * GW), F32, kind="Internal").ap()
    bkv_sel = nc.dram_tensor("bkv_sel", (B, R, 2, KVH * D), F32, kind="Internal").ap()
    ao_sel = nc.dram_tensor("ao_sel", (B, KVH * GW, R), F32, kind="Internal").ap()
    bo_sel = nc.dram_tensor("bo_sel", (B, R, HID), F32, kind="Internal").ap()
    l3b_sel = nc.dram_tensor("l3b_sel", (B, R, HID), F32, kind="Internal").ap()
    c_rows = nc.dram_tensor("c_rows", (B, R, HID), F32, kind="Internal").ap()
    m_rows = nc.dram_tensor("m_rows", (B, R, 2 * R), F32, kind="Internal").ap()
    k_rot = nc.dram_tensor("k_rot", (KVH, D, NT), F32, kind="Internal").ap()
    v_hi_d = nc.dram_tensor("v_hi_d", (KVH, T, B, D), F32, kind="Internal").ap()
    v_lo_d = nc.dram_tensor("v_lo_d", (KVH, T, B, D), F32, kind="Internal").ap()

    whole = ExitStack()
    with whole:
        def sb(ctx, name, shape, dt=F32):
            return ctx.enter_context(nc.sbuf_tensor(name, shape, dt))

        def ps(ctx, name, shape, dt=F32):
            return ctx.enter_context(nc.psum_tensor(name, shape, dt))

        def sem(ctx, name):
            return ctx.enter_context(nc.semaphore(name))

        def project(pe, bank, w_hi, w_lo, b_pack, ax, cols, half):
            tok = slice(half * HT, (half + 1) * HT)
            for k in range(KC):
                pe.matmul(bank[:, :], w_hi[:, k, cols], x1t_hi[:, k, tok], start=(k == 0), stop=False)
                pe.matmul(bank[:, :], w_hi[:, k, cols], x1t_lo[:, k, tok], start=False, stop=False)
                pe.matmul(bank[:, :], w_lo[:, k, cols], x1t_hi[:, k, tok], start=False, stop=False)
            for pair in range(PAIRS // 2):
                n = half * PAIRS // 2 + pair
                last = pe.matmul(bank[:, pair * 2 * T:(pair + 1) * 2 * T], b_pack[:, n, cols],
                                 ax[:, n * 2 * T:(n + 1) * 2 * T], start=False, stop=(pair == PAIRS // 2 - 1))
            return last

        res = sb(whole, "res", [P, B, HID])
        ident = sb(whole, "ident", [P, P])
        ident_r = sb(whole, "ident_r", [P, P], F32R)
        ident_h = sb(whole, "ident_h", [P, P], F16)
        axo = sb(whole, "axo", [2 * R, B, T])
        id_rows = sb(whole, "id_rows", [1, 3, B], I32)
        raw_w = sb(whole, "raw_w", [P, KC, GW])
        raw_b = sb(whole, "raw_b", [P, PAIRS, GW])
        row_gather = sb(whole, "row_gather", [2 * R, 2, P])
        twin = sb(whole, "twin", [P, 3])
        l2b_sel = sb(whole, "l2b_sel", [P, HID])
        l2a_sel = sb(whole, "l2a_sel", [P, KC, B, R])
        l3a_sel = sb(whole, "l3a_sel", [P, KC, B, R])
        last_gathered = sem(whole, "last_gathered")
        w3_in = sem(whole, "w3_in")
        bo_in = sem(whole, "bo_in")
        l2_in = sem(whole, "l2_in")
        l3a_in = sem(whole, "l3a_in")

        attn = ExitStack()
        attn.__enter__()
        x1t_hi = sb(attn, "x1t_hi", [P, KC, NT], F32R)
        x1t_lo = sb(attn, "x1t_lo", [P, KC, NT], F32R)
        cos_t = sb(attn, "cos_t", [P, NT])
        sin_t = sb(attn, "sin_t", [P, NT])
        maskbias = sb(attn, "maskbias", [P, B, T])
        axt = [sb(attn, f"axt_{n}", [P, NT], F32R) for n in "qk"]
        axt_v = sb(attn, "axt_v", [P, NT], F32R)
        rope_cols = sb(attn, "rope_cols", [P, 3])

        blk_hi = [sb(attn, "blk_hi0", [P, KC, GW], F32R)]
        blk_lo = [sb(attn, "blk_lo0", [P, KC, GW], F32R)]
        blk_b = [sb(attn, "blk_b0", [P, PAIRS, GW], F32R)]
        VB = KVH * D // GW
        raw_w_in = sem(attn, "raw_w_in")
        raw_b_in = sem(attn, "raw_b_in")
        UNITS = B
        assert VB * GW == KVH * D and GW // D * 2 == UNITS and KC + PAIRS == UNITS

        def block_source(n):
            kind, j = ((1, n), (0, n - VB), (2, 0))[min(n // VB, 2)]
            return kind, slice(j * GW, (j + 1) * GW)

        def load_block_w(dma, n):
            kind, cols = block_source(n)
            dma.dma_start(raw_w[:, :, :], (wk, wv, wq)[kind][:, cols].rearrange("(c p) n -> p c n", p=P)).then_inc(raw_w_in, 16)

        def load_block_b(dma, n):
            kind, cols = block_source(n)
            src = (bq_sel if kind == 2 else bkv_sel[:, :, kind, :])[:, :, cols]
            load_rows(dma, raw_b, src, raw_b_in)

        def load_rows(dma, pack, src, done):
            for quad in range(4):
                dma.dma_start(pack[32 * quad:32 * quad + 32, :, :], src.rearrange("(c two) r n -> (two r) c n", two=2)).then_inc(done, 16)

        with ExitStack() as c:
            w0_raw = [sb(c, f"w0_raw{i}", [P, KC, HID]) for i in range(2)]
            xt_hi = [sb(c, f"xt_hi{i}", [P, KC * T], F32R) for i in range(2)]
            xt_lo = [sb(c, f"xt_lo{i}", [P, KC * T], F32R) for i in range(2)]
            wt_hi = [sb(c, f"wt_hi{i}", [P, KC, HID], F32R) for i in range(2)]
            wt_lo = [sb(c, f"wt_lo{i}", [P, KC, HID], F32R) for i in range(2)]
            pos_i = sb(c, "pos_i", [P, NT], I32)
            ang = sb(c, "ang", [P, NT])
            turns = sb(c, "turns", [P, NT])
            mask_u8 = sb(c, "mask_u8", [P, NT], U8)
            causal = sb(c, "causal", [P, T])
            a_raw = sb(c, "a_raw", [P, B, KC, 3, R])
            a_hi = [sb(c, f"a_hi{i}", [P, KC, 3, R], F32R) for i in range(2)]
            a_lo = [sb(c, f"a_lo{i}", [P, KC, 3, R], F32R) for i in range(2)]
            axn = [sb(c, f"axn{i}", [P, 3, 4, 2, R], F32R) for i in range(2)]
            ps_ring = [ps(c, f"ps_ring{i}", [P, HID]) for i in range(3)]
            ps_y = [ps(c, f"ps_y{i}", [P, HID]) for i in range(2)]
            ps_x1 = ps(c, "ps_x1", [P, KC, T])
            ps_a = ps(c, "ps_a", [P, 3, R])
            ps_at = ps(c, "ps_at", [P, 3, T])
            lora_ids_in = sem(c, "lora_ids_in")
            ids_in = sem(c, "ids_in")
            w0_first_in = [sem(c, f"w0_first_in{k}") for k in range(KC)]
            consts_in = sem(c, "consts_in")
            tables_in = sem(c, "tables_in")
            x_in = [sem(c, f"x_in{b}") for b in range(B)]
            w0_in = [sem(c, f"w0_in{i}") for i in range(2)]
            a_in = [sem(c, f"a_in{b}") for b in range(B)]
            gathered_kv = sem(c, "gathered_kv")
            gathered = sem(c, "gathered")
            raw_hi_done = sem(c, "raw_hi_done")
            raw_lo_done = sem(c, "raw_lo_done")
            ident_ready = sem(c, "ident_ready")
            tile_ready = sem(c, "tile_ready")
            tile_hi_done = sem(c, "tile_hi_done")
            tile_lo_done = sem(c, "tile_lo_done")
            y_ready = sem(c, "y_ready")
            x1_done = sem(c, "x1_done")
            x1t_ready = sem(c, "x1t_ready")
            x1t_hi_done = sem(c, "x1t_hi_done")
            x1t_lo_done = sem(c, "x1t_lo_done")
            zeroed = sem(c, "zeroed")
            a_hi_done = sem(c, "a_hi_done")
            a_lo_done = sem(c, "a_lo_done")
            ax_ready = sem(c, "ax_ready")
            axn_done = sem(c, "axn_done")
            axt_ready = sem(c, "axt_ready")
            axt_done = sem(c, "axt_done")
            tab = sem(c, "tab")
            sines = sem(c, "sines")
            TILES = 1 + KC

            with nc.Block() as block:
                @block.sync
                def _(sp):
                    sp.dma_start(id_rows[:, 0, :], lora_ids.rearrange("(a b) -> a b", a=1)).then_inc(lora_ids_in, 16)
                    sp.dma_start(res[:, 0, :], x[0]).then_inc(x_in[0], 16)
                    sp.wait_ge(lora_ids_in, 16)
                    for b in range(B):
                        a = sp.value_load(id_rows[0:1, 0, b:b + 1], min_val=0, max_val=w0.shape[0] - 1)
                        if b >= 2:
                            sp.wait_ge(tile_ready, TILES * (b - 1))
                        src = w0[bass.DynSlice(a, 1), :, :].rearrange("a (c p) i -> p (a c) i", p=P)
                        if b == 0:
                            for k in range(KC):
                                cols = slice(k * P, (k + 1) * P)
                                sp.dma_start(w0_raw[0][:, :, cols], src[:, :, cols]).then_inc(w0_first_in[k], 16)
                            sp.wait_ge(ids_in, 32)
                        else:
                            sp.dma_start(w0_raw[b % 2][:, :, :], src).then_inc(w0_in[b % 2], 16)
                        if b + 1 < B:
                            sp.dma_start(res[:, b + 1, :], x[b + 1]).then_inc(x_in[b + 1], 16)
                        pick = sp.value_load(id_rows[0:1, 1, b:b + 1], min_val=0, max_val=aq.shape[0] - 1)
                        for n, src in enumerate((aq, ak, av)):
                            sp.dma_start(a_raw[:, b, :, n, :],
                                         src[bass.DynSlice(pick, 1)].rearrange("a (c p) r -> p (a c) r", p=P)).then_inc(a_in[b], 16)
                        if b == 4:
                            sp.wait_ge(gathered_kv, 2 * B * 16)
                            load_block_w(sp, 0)
                            load_block_b(sp, 0)
                    sp.wait_ge(raw_lo_done, KC)
                    load_block_w(sp, 1)

                @block.gpsimd
                def _(pool):
                    pool.dma_start(pos_i[:, :], pos.rearrange("b t -> (b t)").partition_broadcast(P)).then_inc(tables_in, 16)
                    pool.dma_start(mask_u8[:, :], mask.rearrange("b t -> (b t)").partition_broadcast(P)).then_inc(tables_in, 16)
                    pool.dma_start(causal[:, :], causal_c).then_inc(tables_in, 16)
                    pool.dma_start(rope_cols[:, :], rope_c).then_inc(tables_in, 16)
                    pool.wait_ge(ids_in, 32)
                    for b in range(B):
                        a = pool.value_load(id_rows[0:1, 1, b:b + 1], min_val=0, max_val=bq.shape[0] - 1)
                        pick = bass.DynSlice(a, 1)
                        pool.dma_start(bkv_sel[b:b + 1, :, 0, :], bk[pick]).then_inc(gathered_kv, 16)
                        pool.dma_start(bkv_sel[b:b + 1, :, 1, :], bv[pick]).then_inc(gathered_kv, 16)
                    for b in range(B):
                        a = pool.value_load(id_rows[0:1, 1, b:b + 1], min_val=0, max_val=bq.shape[0] - 1)
                        pick = bass.DynSlice(a, 1)
                        pool.dma_start(bq_sel[b:b + 1], bq[pick]).then_inc(gathered, 16)
                        pool.dma_start(ao_sel[b:b + 1], ao[pick]).then_inc(gathered, 16)
                    pool.wait_ge(tables_in, 64)
                    pool.wait_ge(gathered, 2 * B * 16)

                @block.tensor
                def _(pe):
                    def transposes(b):
                        pe.wait_ge(x_in[b], 16)
                        if b == 0:
                            pe.wait_ge(consts_in, 16)
                        for j in range(TILES):
                            m = TILES * b + j
                            if b == 0 and j >= 1:
                                pe.wait_ge(w0_first_in[j - 1], 16)
                            elif j == 1:
                                pe.wait_ge(w0_in[b % 2], 16 * ((b + 1) // 2))
                            if m >= 3:
                                pe.wait_ge(tile_lo_done, m - 2)
                            for n in range(KC):
                                src = res[:, b, n * P:(n + 1) * P] if j == 0 else w0_raw[b % 2][:, n, (j - 1) * P:j * P]
                                mm = pe.matmul(ps_ring[m % 3][:, n * P:(n + 1) * P], src, ident[:, :], start=True, stop=True)
                            mm.then_inc(tile_ready, 1)

                    def product(b):
                        pe.wait_ge(tile_lo_done, TILES * b + 1)
                        if b >= 2:
                            pe.wait_ge(x1_done, b - 1)
                        i = b % 2
                        for k in range(KC):
                            pe.wait_ge(tile_lo_done, TILES * b + k + 2)
                            row = slice(k * T, (k + 1) * T)
                            pe.matmul(ps_y[i][:, :], xt_hi[i][:, row], wt_hi[i][:, k, :], start=(k == 0), stop=False)
                            pe.matmul(ps_y[i][:, :], xt_hi[i][:, row], wt_lo[i][:, k, :], start=False, stop=False)
                            mm = pe.matmul(ps_y[i][:, :], xt_lo[i][:, row], wt_hi[i][:, k, :], start=False, stop=(k == KC - 1))
                        mm.then_inc(y_ready, 1)

                    def turn_x1(b):
                        pe.wait_ge(x1_done, b + 1)
                        if b >= 1:
                            pe.wait_ge(x1t_lo_done, b)
                        for k in range(KC):
                            mm = pe.matmul(ps_x1[:, k, :], res[:, b, k * P:(k + 1) * P], ident[:, :], start=True, stop=True)
                        mm.then_inc(x1t_ready, 1)

                    def adapters(b):
                        i = b % 2
                        cols = slice(b * T, (b + 1) * T)
                        pe.wait_ge(x1t_lo_done, b + 1)
                        pe.wait_ge(a_lo_done, b + 1)
                        if b >= 1:
                            pe.wait_ge(axn_done, 4 * b)
                        for k in range(KC):
                            pe.matmul(ps_a[:, :, :], x1t_hi[:, k, cols], a_hi[i][:, k, :, :], start=(k == 0), stop=False)
                            pe.matmul(ps_a[:, :, :], x1t_hi[:, k, cols], a_lo[i][:, k, :, :], start=False, stop=False)
                            mm = pe.matmul(ps_a[:, :, :], x1t_lo[:, k, cols], a_hi[i][:, k, :, :], start=False, stop=(k == KC - 1))
                        mm.then_inc(ax_ready, 1)

                    def turn_ax(b):
                        pe.wait_ge(axn_done, 4 * b + 4)
                        if b == 0:
                            pe.wait_ge(ident_ready, 2)
                        else:
                            pe.wait_ge(axt_done, 3 * b)
                        for n in range(3):
                            mm = pe.matmul(ps_at[:, n, :], axn[b % 2][:, n, :, :, :].rearrange("p a b r -> p (a b r)"),
                                           ident_r[:, :], start=True, stop=True)
                        mm.then_inc(axt_ready, 1)

                    transposes(0)
                    for b in range(B + 3):
                        if b + 1 < B:
                            transposes(b + 1)
                        if b < B:
                            product(b)
                        if 1 <= b <= B:
                            turn_x1(b - 1)
                        if 2 <= b <= B + 1:
                            adapters(b - 2)
                        if b >= 3:
                            turn_ax(b - 3)

                @block.scalar
                def _(act):
                    def split(b):
                        i = b % 2
                        if b >= 2:
                            act.wait_ge(y_ready, b - 1)
                        for j in range(TILES):
                            m = TILES * b + j
                            act.wait_ge(tile_ready, m + 1)
                            act.activation(xt_hi[i][:, :] if j == 0 else wt_hi[i][:, j - 1, :], ps_ring[m % 3][:, :],
                                           ACT.Copy).then_inc(tile_hi_done, 1)

                    def split_x1(b):
                        act.wait_ge(x1t_ready, b + 1)
                        act.activation(x1t_hi[:, :, b * T:(b + 1) * T], ps_x1[:, :, :], ACT.Copy).then_inc(x1t_hi_done, 1)

                    def split_a(b):
                        act.wait_ge(a_in[b], 48)
                        if b >= 2:
                            act.wait_ge(ax_ready, b - 1)
                        act.activation(a_hi[b % 2][:, :, :, :], a_raw[:, b, :, :, :], ACT.Copy).then_inc(a_hi_done, 1)

                    def copy_axt(b):
                        act.wait_ge(axt_ready, b + 1)
                        cols = slice(b * T, (b + 1) * T)
                        for n, dst in enumerate((axt[0], axt[1], axt_v)):
                            act.activation(dst[:, cols], ps_at[:, n, :], ACT.Copy).then_inc(axt_done, 1)

                    act.dma_start(ident[:, :], ident_c).then_inc(consts_in, 16)
                    for n, ids in ((1, attn_ids), (2, slot_ids)):
                        act.dma_start(id_rows[:, n, :], ids.rearrange("(a b) -> a b", a=1)).then_inc(ids_in, 16)
                    act.wait_ge(consts_in, 16)
                    act.activation(ident_r[:, :], ident[:, :], ACT.Copy).then_inc(ident_ready, 1)
                    act.activation(ident_h[:, :], ident[:, :], ACT.Copy).then_inc(ident_ready, 1)
                    split(0)
                    for b in range(B + 3):
                        if b + 1 < B:
                            split(b + 1)
                        if 1 <= b <= B:
                            split_x1(b - 1)
                        if 1 <= b <= B:
                            split_a(b - 1)
                        if b >= 3:
                            copy_axt(b - 3)
                        if b == 2:
                            act.wait_ge(tab, 7)
                            act.activation(sin_t[:, :], ang[:, :], ACT.Sin).then_inc(sines, 1)
                        if b == 5:
                            act.wait_ge(tab, 15)
                            act.activation(cos_t[:, :], ang[:, :], ACT.Sin).then_inc(sines, 1)
                        if b in (6, 7):
                            act.wait_ge(raw_w_in, 16)
                            for k in range(2 * (b - 6), 2 * (b - 6) + 2):
                                act.activation(blk_hi[0][:, k, :], raw_w[:, k, :], ACT.Copy).then_inc(raw_hi_done, 1)

                @block.vector
                def _(dve):
                    def split(b):
                        i = b % 2
                        for j in range(TILES):
                            m = TILES * b + j
                            hi, lo = (xt_hi[i][:, :], xt_lo[i][:, :]) if j == 0 else (wt_hi[i][:, j - 1, :], wt_lo[i][:, j - 1, :])
                            dve.wait_ge(tile_hi_done, m + 1)
                            dve.tensor_tensor(lo, ps_ring[m % 3][:, :], hi.bitcast(F32), ALU.subtract).then_inc(tile_lo_done, 1)

                    def add(b):
                        dve.wait_ge(y_ready, b + 1)
                        dve.tensor_tensor(res[:, b, :], ps_y[b % 2][:, :], res[:, b, :], ALU.add).then_inc(x1_done, 1)

                    def split_x1(b):
                        dve.wait_ge(x1t_hi_done, b + 1)
                        cols = slice(b * T, (b + 1) * T)
                        dve.tensor_tensor(x1t_lo[:, :, cols], ps_x1[:, :, :], x1t_hi[:, :, cols].bitcast(F32),
                                          ALU.subtract).then_inc(x1t_lo_done, 1)

                    def split_a(b):
                        dve.wait_ge(a_hi_done, b + 1)
                        dve.tensor_tensor(a_lo[b % 2][:, :, :, :], a_raw[:, b, :, :, :], a_hi[b % 2][:, :, :, :].bitcast(F32),
                                          ALU.subtract).then_inc(a_lo_done, 1)

                    def pack_ax(b):
                        i = b % 2
                        dve.wait_ge(zeroed, i + 1)
                        dve.wait_ge(ax_ready, b + 1)
                        if b >= 2:
                            dve.wait_ge(axt_ready, b - 1)
                        for quad in (0, 2):
                            dve.tensor_copy(axn[i][:, :, quad, i, :], ps_a[:, :, :]).then_inc(axn_done, 1)
                        dve.wait_ge(axn_done, 4 * b + 2)
                        for quad in (1, 3):
                            dve.tensor_tensor(axn[i][:, :, quad, i, :], ps_a[:, :, :],
                                              axn[i][:, :, 0, i, :].bitcast(F32), ALU.subtract).then_inc(axn_done, 1)

                    steps = [0]

                    def step(instruction):
                        steps[0] += 1
                        instruction.then_inc(tab, 1)
                        dve.wait_ge(tab, steps[0])

                    def angles(quarter, part):
                        if part == 0:
                            if quarter:
                                dve.wait_ge(sines, 1)
                            else:
                                dve.wait_ge(tables_in, 64)
                            step(dve.tensor_scalar(ang[:, :], pos_i[:, :], rope_cols[:, 0:1], None, ALU.mult))
                            step(dve.tensor_scalar(turns[:, :], ang[:, :], 1.0 / TWO_PI, quarter, ALU.mult, ALU.add))
                            step(dve.tensor_scalar(turns[:, :], turns[:, :], MAGIC, -MAGIC, ALU.add, ALU.add))
                        elif part == 1:
                            for share in (PI_A, PI_B):
                                step(dve.scalar_tensor_tensor(ang[:, :], turns[:, :], -share, ang[:, :], ALU.mult, ALU.add))
                        else:
                            step(dve.scalar_tensor_tensor(ang[:, :], turns[:, :], -PI_C, ang[:, :], ALU.mult, ALU.add))
                            if quarter:
                                step(dve.tensor_scalar(ang[:, :], ang[:, :], TWO_PI / 4, None, ALU.add))
                            step(dve.tensor_scalar(ang[:, :], ang[:, :], PI_LIMIT, -PI_LIMIT, ALU.min, ALU.max))

                    def mask_table():
                        mb = maskbias[:, :, :].rearrange("p b t -> p (b t)")
                        step(dve.tensor_scalar(mb, mask_u8[:, :], -NEG, NEG, ALU.mult, ALU.add))
                        step(dve.tensor_tensor(maskbias[:, :, :], maskbias[:, :, :], causal[:, :].unsqueeze(1).broadcast_to([P, B, T]), ALU.min))

                    def block_lo(first, last):
                        for k in range(first, last):
                            dve.wait_ge(raw_hi_done, k + 1)
                            dve.tensor_tensor(blk_lo[0][:, k, :], raw_w[:, k, :], blk_hi[0][:, k, :].bitcast(F32),
                                              ALU.subtract).then_inc(raw_lo_done, 1)

                    def tables(b):
                        if b < 3:
                            angles(0.0, b)
                        elif b < 6:
                            angles(0.25, b - 3)
                        elif b == 6:
                            mask_table()
                        elif b == 7:
                            block_lo(0, 2)

                    for i in range(2):
                        dve.memset(axn[i][:, :, :, :, :].bitcast(F32), 0.0).then_inc(zeroed, 1)
                    split(0)
                    for b in range(B + 3):
                        if b + 1 < B:
                            split(b + 1)
                        if b < B:
                            tables(b)
                            add(b)
                        if 1 <= b <= B:
                            split_x1(b - 1)
                            split_a(b - 1)
                        if 2 <= b <= B + 1:
                            pack_ax(b - 2)
                        if b == B:
                            block_lo(2, KC)

        late = ExitStack()
        late.__enter__()
        wo_raw = sb(late, "wo_raw", [P, G, HID])
        ao_raw = sb(late, "ao_raw", [P, B, G, R])
        kt = sb(late, "kt", [P, NT])
        v_hi3 = sb(late, "v_hi3", [P, B, D], F32R)
        v_lo3 = sb(late, "v_lo3", [P, B, D], F32R)
        qt = sb(late, "qt", [P, 2, G, HT])
        wq_in = sem(late, "wq_in")
        wo_in = sem(late, "wo_in")
        bq_in = [sem(late, f"bq_in{i}") for i in range(2)]
        ao_in = sem(late, "ao_in")
        kt_in = [sem(late, f"kt_in{i}") for i in range(2)]
        v_in = [sem(late, f"v_in{i}") for i in range(2)]

        def load_wq(dma, g):
            dma.dma_start(raw_w[:, :, :], wq[:, bass.DynSlice(g * GW, GW)].rearrange("(c p) n -> p c n", p=P)).then_inc(wq_in, 16)

        def load_bq(dma, g, h):
            for quad in range(4):
                dma.dma_start(raw_b[32 * quad:32 * quad + 32, 2 * h:2 * h + 2, :],
                              bq_sel.rearrange("(c two) r n -> (two r) c n", two=2)[:, 2 * h:2 * h + 2, bass.DynSlice(g * GW, GW)]
                              ).then_inc(bq_in[h], 16)

        def load_wo(dma, g):
            dma.dma_start(wo_raw[:, :, :], wo[bass.DynSlice(g * GW, GW), :].rearrange("(h p) n -> p h n", p=P)).then_inc(wo_in, 16)
            for b in range(B):
                dma.dma_start(ao_raw[:, b, :, :], ao_sel[b, bass.DynSlice(g * GW, GW), :].rearrange("(h p) r -> p h r", p=P)).then_inc(ao_in, 16)

        def load_kv(dma, g, h):
            one = bass.DynSlice(g, 1)
            cols, half = slice(h * HT, (h + 1) * HT), slice(h * HALF, (h + 1) * HALF)
            dma.dma_start(kt[:, cols], k_rot[one, :, cols].rearrange("a p t -> p (a t)")).then_inc(kt_in[h], 16)
            dma.dma_start(v_hi3[:, half, :].bitcast(F32), v_hi_d[one, :, half, :].rearrange("a p b d -> p (a b) d")).then_inc(v_in[h], 16)
            dma.dma_start(v_lo3[:, half, :].bitcast(F32), v_lo_d[one, :, half, :].rearrange("a p b d -> p (a b) d")).then_inc(v_in[h], 16)

        with ExitStack() as c:
            blk_hi.append(sb(c, "blk_hi1", [P, KC, GW], F32R))
            blk_lo.append(sb(c, "blk_lo1", [P, KC, GW], F32R))
            blk_b.append(sb(c, "blk_b1", [P, PAIRS, GW], F32R))
            v_hi = [sb(c, f"v_hi{i}", [P, GW], F32R) for i in range(2)]
            v_lo = [sb(c, f"v_lo{i}", [P, GW], F32R) for i in range(2)]
            k_cos = [sb(c, f"k_cos{i}", [P, HT]) for i in range(2)]
            k_sin = [sb(c, f"k_sin{i}", [P, HT]) for i in range(2)]
            kr = [sb(c, f"kr{i}", [P, HT]) for i in range(2)]
            ps_p = [ps(c, f"ps_p{i}", [P, GW]) for i in range(4)]
            raw_hi_done = sem(c, "raw_hi_done2")
            raw_lo_done = sem(c, "raw_lo_done2")
            p_ready = sem(c, "p_ready")
            first_packs_hi = sem(c, "first_packs_hi")
            first_packs = sem(c, "first_packs")
            v_hi_done = sem(c, "v_hi_done")
            v_lo_done = sem(c, "v_lo_done")
            scaled = sem(c, "scaled")
            v_out = [sem(c, f"v_out{i}") for i in range(2)]
            k_mult = sem(c, "k_mult")
            k_done = sem(c, "k_done")
            k_out = [sem(c, f"k_out{i}") for i in range(2)]
            BLOCKS = 2 * VB
            VU = VB * UNITS

            with nc.Block() as block:
                @block.sync
                def _(sp):
                    sp.wait_ge(first_packs, PAIRS)
                    load_block_b(sp, 1)
                    for n in range(BLOCKS * UNITS):
                        i = n % 2
                        if n < VU:
                            h, b = divmod(n, UNITS)
                            sp.wait_ge(v_lo_done, n + 1)
                            g = slice(h * GW // D, (h + 1) * GW // D)
                            for src, dst in ((v_hi, v_hi_d), (v_lo, v_lo_d)):
                                sp.dma_start(dst[g, :, b, :].rearrange("g t d -> t g d"),
                                             src[i][:, :].bitcast(F32).rearrange("t (g d) -> t g d", d=D)).then_inc(v_out[i], 16)
                        else:
                            g, h = divmod(n - VU, 2)
                            sp.wait_ge(k_done, n - VU + 1)
                            sp.dma_start(k_rot[g, :, h * HT:(h + 1) * HT], kr[i][:, :]).then_inc(k_out[i], 16)
                        blk, u = divmod(n, UNITS)
                        if u == KC - 1:
                            sp.wait_ge(raw_lo_done, UNITS * blk + KC)
                            if blk + 2 <= BLOCKS:
                                load_block_w(sp, blk + 2)
                            else:
                                load_wq(sp, 1)
                        if u == UNITS - 1:
                            sp.wait_ge(raw_lo_done, UNITS * (blk + 1))
                            if blk + 2 <= BLOCKS:
                                load_block_b(sp, blk + 2)
                            else:
                                load_bq(sp, 1, 0)
                                load_bq(sp, 1, 1)
                        if n == VU:
                            load_wo(sp, 0)
                        if n == VU + 4:
                            for i in range(2):
                                sp.wait_ge(v_out[i], 16 * VU)
                                sp.wait_ge(k_out[i], 16)
                            load_kv(sp, 0, 0)
                            load_kv(sp, 0, 1)
                    for i in range(2):
                        sp.wait_ge(v_out[i], 16 * VU)
                        sp.wait_ge(k_out[i], 16 * VU // 2)

                @block.scalar
                def _(act):
                    act.wait_ge(raw_b_in, 64)
                    for p in range(PAIRS):
                        act.activation(blk_b[0][:, p, :], raw_b[:, p, :], ACT.Copy).then_inc(first_packs_hi, 1)
                    for n in range(BLOCKS * UNITS):
                        blk, u = divmod(n, UNITS)
                        i = (blk + 1) % 2
                        if u == 0:
                            act.wait_ge(raw_w_in, 16 * (blk + 2))
                            if blk >= 1:
                                act.wait_ge(p_ready, UNITS * blk)
                        if u == KC:
                            act.wait_ge(raw_b_in, 64 * (blk + 2))
                        if u < KC:
                            act.activation(blk_hi[i][:, u, :], raw_w[:, u, :], ACT.Copy).then_inc(raw_hi_done, 1)
                        else:
                            act.activation(blk_b[i][:, u - KC, :], raw_b[:, u - KC, :], ACT.Copy).then_inc(raw_hi_done, 1)
                        if n < VU:
                            act.wait_ge(p_ready, n + 1)
                            if n >= 2:
                                act.wait_ge(v_out[n % 2], 32 * (n // 2))
                            act.activation(v_hi[n % 2][:, :], ps_p[n % 4][:, :], ACT.Copy).then_inc(v_hi_done, 1)

                @block.vector
                def _(dve):
                    low = slice(P // 2, P)
                    for p in range(PAIRS):
                        dve.wait_ge(first_packs_hi, p + 1)
                        dve.tensor_tensor(blk_b[0][low, p, :], raw_b[low, p, :], blk_b[0][low, p, :].bitcast(F32),
                                          ALU.subtract).then_inc(first_packs, 1)
                    for n in range(BLOCKS * UNITS + G):
                        blk, u = divmod(n, UNITS)
                        if blk < BLOCKS:
                            i = (blk + 1) % 2
                            dve.wait_ge(raw_hi_done, n + 1)
                            if u < KC:
                                dve.tensor_tensor(blk_lo[i][:, u, :], raw_w[:, u, :], blk_hi[i][:, u, :].bitcast(F32),
                                                  ALU.subtract).then_inc(raw_lo_done, 1)
                            else:
                                p = u - KC
                                dve.tensor_tensor(blk_b[i][low, p, :], raw_b[low, p, :], blk_b[i][low, p, :].bitcast(F32),
                                                  ALU.subtract).then_inc(raw_lo_done, 1)
                        if n == 2:
                            dve.tensor_scalar(cos_t[:, :], cos_t[:, :], rope_cols[:, 1:2], None, ALU.mult).then_inc(scaled, 1)
                            dve.tensor_scalar(sin_t[:, :], sin_t[:, :], rope_cols[:, 2:3], None, ALU.mult).then_inc(scaled, 1)
                        if n == VU:
                            dve.wait_ge(scaled, 2)
                        if n < VU:
                            dve.wait_ge(v_hi_done, n + 1)
                            dve.tensor_tensor(v_lo[n % 2][:, :], ps_p[n % 4][:, :], v_hi[n % 2][:, :].bitcast(F32),
                                              ALU.subtract).then_inc(v_lo_done, 1)
                        else:
                            m, i = n - VU, n % 2
                            half = n % 2 if blk < BLOCKS else 0
                            tok = slice(half * HT, (half + 1) * HT)
                            dve.wait_ge(p_ready, n + 1)
                            if m >= 2:
                                dve.wait_ge(k_done, m - 1)
                            dve.tensor_tensor(k_cos[i][:, :], ps_p[n % 4][:, :], cos_t[:, tok], ALU.mult).then_inc(k_mult, 1)
                            for to, at in ((0, 64), (64, 0)):
                                dve.tensor_tensor(k_sin[i][to:to + 64, :], ps_p[n % 4][at:at + 64, :], sin_t[to:to + 64, tok],
                                                  ALU.mult).then_inc(k_mult, 1)

                @block.gpsimd
                def _(pool):
                    for b in range(B):
                        a = pool.value_load(id_rows[0:1, 1, b:b + 1], min_val=0, max_val=bo.shape[0] - 1)
                        pool.dma_start(bo_sel[b:b + 1], bo[bass.DynSlice(a, 1)]).then_inc(last_gathered, 16)
                        a = pool.value_load(id_rows[0:1, 2, b:b + 1], min_val=0, max_val=l3b.shape[0] - 1)
                        pool.dma_start(l3b_sel[b:b + 1], l3b[bass.DynSlice(a, 1)]).then_inc(last_gathered, 16)
                    for m in range(VU + G):
                        i = m % 2
                        pool.wait_ge(k_mult, 3 * m + 3)
                        if 2 <= m < VU:
                            pool.wait_ge(k_out[i], 16 * (m // 2))
                        rotated = kr[i][:, :] if m < VU else qt[:, 0, m - VU, :]
                        pool.tensor_tensor(rotated, k_cos[i][:, :], k_sin[i][:, :], ALU.add).then_inc(k_done, 1)

                @block.tensor
                def _(pe):
                    for n in range(BLOCKS * UNITS + G):
                        blk, u = divmod(n, UNITS)
                        i = blk % 2
                        if u == 0 and blk >= 1:
                            pe.wait_ge(raw_lo_done, UNITS * blk)
                        if 4 <= n < VU + 4:
                            pe.wait_ge(v_lo_done, n - 3)
                        elif n >= 4:
                            pe.wait_ge(k_mult, 3 * (n - VU - 3))
                        if n < VU:
                            tok = slice(u * T, (u + 1) * T)
                            o = ps_p[n % 4][:, :]
                            for k in range(KC):
                                pe.matmul(o, x1t_hi[:, k, tok], blk_hi[i][:, k, :], start=(k == 0), stop=False)
                                pe.matmul(o, x1t_hi[:, k, tok], blk_lo[i][:, k, :], start=False, stop=False)
                                pe.matmul(o, x1t_lo[:, k, tok], blk_hi[i][:, k, :], start=False, stop=False)
                            if blk == 0 and u % 2 == 0:
                                pe.wait_ge(first_packs, u // 2 + 1)
                            pe.matmul(o, axt_v[:, tok], blk_b[i][:, u // 2, :], start=False, stop=True).then_inc(p_ready, 1)
                        elif blk == BLOCKS:
                            head = slice(u * D, (u + 1) * D)
                            project(pe, ps_p[n % 4], blk_hi[i], blk_lo[i], blk_b[i], axt[0], head, 0).then_inc(p_ready, 1)
                        else:
                            head = slice(u // 2 * D, (u // 2 + 1) * D)
                            project(pe, ps_p[n % 4], blk_hi[i], blk_lo[i], blk_b[i], axt[1], head, n % 2).then_inc(p_ready, 1)

        with ExitStack() as c:
            wq_raw, bq_raw, wq_hi, wq_lo, bq_pack = raw_w, raw_b, blk_hi[0], blk_lo[0], blk_b[0]
            wo_hi = sb(c, "wo_hi", [P, G, HID], F32R)
            wo_lo = sb(c, "wo_lo", [P, G, HID], F32R)
            ao_pack = sb(c, "ao_pack", [P, B, G, 2, R], F32R)
            v_hi, v_lo = v_hi3, v_lo3
            qc = sb(c, "qc", [P, HT])
            qs = sb(c, "qs", [P, HT])
            gate = sb(c, "gate", [P, 1])
            sm = sb(c, "sm", [P, G, T])
            nmax = [sb(c, f"nmax{i}", [P, G]) for i in range(2)]
            rsum = [sb(c, f"rsum{i}", [P, G]) for i in range(2)]
            rinv = [sb(c, f"rinv{i}", [P, G]) for i in range(2)]
            prob = [sb(c, f"prob{i}", [P, G, T]) for i in range(2)]
            rsum_low = sb(c, "rsum_low", [P, G])
            p_hi = sb(c, "p_hi", [P, G, T], F16)
            p_lo = sb(c, "p_lo", [P, G, T], F16)
            pt_hi = sb(c, "pt_hi", [P, G * T], F32R)
            pt_lo = sb(c, "pt_lo", [P, G * T], F32R)
            ot_hi = sb(c, "ot_hi", [P, G * T], F32R)
            ot_lo = sb(c, "ot_lo", [P, G * T], F32R)
            ps_s = [ps(c, f"ps_s{i}", [P, G, T]) for i in range(2)]
            ps_q = [ps(c, f"ps_q{i}", [P, HT]) for i in range(2)]
            ps_t = ps(c, "ps_t", [P, G * T])
            ps_o = ps(c, "ps_o", [P, G * T])
            ps_out = ps(c, "ps_out", [P, HID])
            ps_ao = ps(c, "ps_ao", [P, 512])
            wq_hi_done = sem(c, "wq_hi_done")
            wq_lo_done = sem(c, "wq_lo_done")
            wo_hi_done = sem(c, "wo_hi_done")
            wo_lo_done = sem(c, "wo_lo_done")
            wo_lo_pool = sem(c, "wo_lo_pool")
            bq_hi_done = sem(c, "bq_hi_done")
            bq_lo_done = sem(c, "bq_lo_done")
            ao_hi_done = sem(c, "ao_hi_done")
            ao_lo_done = sem(c, "ao_lo_done")
            s_ready = sem(c, "s_ready")
            q_ready = sem(c, "q_ready")
            q_mult = sem(c, "q_mult")
            q_done = sem(c, "q_done")
            max_done = sem(c, "max_done")
            exp_done = sem(c, "exp_done")
            sum_done = sem(c, "sum_done")
            inv_done = sem(c, "inv_done")
            prob_done = sem(c, "prob_done")
            p_hi_done = sem(c, "p_hi_done")
            p_lo_done = sem(c, "p_lo_done")
            t_ready = sem(c, "t_ready")
            pt_hi_done = sem(c, "pt_hi_done")
            pt_lo_done = sem(c, "pt_lo_done")
            o_ready = sem(c, "o_ready")
            ot_hi_done = sem(c, "ot_hi_done")
            ot_lo_done = sem(c, "ot_lo_done")
            out_ready = sem(c, "out_ready")
            res_done = sem(c, "res_done")
            axo_done = sem(c, "axo_done")

            def over_heads(eng, slots):
                slots(0, True, False)
                with eng.Fori(1, KVH - 1) as g:
                    slots(g, False, False)
                slots(KVH - 1, False, True)

            with nc.Block() as block:
                @block.sync
                def _(sp):
                    def slots(g):
                        sp.wait_ge(wo_lo_done, G // 2 * (g + 1))
                        sp.wait_ge(wo_lo_pool, G // 2 * (g + 1))
                        sp.wait_ge(ao_lo_done, g + 1)
                        load_wo(sp, g + 1)
                        if not (isinstance(g, int) and g + 2 >= KVH):
                            next_raw(g)
                        sp.wait_ge(s_ready, B * g + HALF)
                        sp.wait_ge(o_ready, B * g + HALF)
                        load_kv(sp, g + 1, 0)
                        sp.wait_ge(s_ready, B * g + B)
                        sp.wait_ge(o_ready, B * g + B)
                        load_kv(sp, g + 1, 1)

                    def next_raw(g):
                        sp.wait_ge(wq_lo_done, G * (g + 1))
                        load_wq(sp, g + 2)
                        sp.wait_ge(bq_lo_done, PAIRS * g + 2)
                        load_bq(sp, g + 2, 0)

                    def next_raw_late(g):
                        sp.wait_ge(bq_lo_done, PAIRS * (g + 1))
                        load_bq(sp, g + 2, 1)

                    def body(g):
                        slots(g)
                        next_raw_late(g)

                    body(0)
                    with sp.Fori(1, KVH - 2) as g:
                        body(g)
                    slots(KVH - 2)

                    sp.wait_ge(wq_lo_done, G * (KVH - 1))
                    sp.dma_start(raw_w[:, :, :], w3.rearrange("(c p) i -> p c i", p=P)).then_inc(w3_in, 16)
                    sp.dma_start(row_gather[:, :, :], gather_c).then_inc(w3_in, 16)
                    sp.dma_start(twin[:, :], twin_c).then_inc(w3_in, 16)
                    sp.wait_ge(bq_lo_done, PAIRS * (KVH - 1))
                    sp.wait_ge(last_gathered, 2 * B * 16)
                    load_rows(sp, raw_b, bo_sel, bo_in)
                    for b in range(B):
                        a = sp.value_load(id_rows[0:1, 0, b:b + 1], min_val=0, max_val=l2a.shape[0] - 1)
                        sp.dma_start(l2b_sel[b * R:(b + 1) * R, :], l2b[bass.DynSlice(a, 1)].rearrange("a r n -> (a r) n")).then_inc(l2_in, 16)
                        sp.dma_start(l2a_sel[:, :, b, :], l2a[bass.DynSlice(a, 1)].rearrange("a (c p) r -> p (a c) r", p=P)).then_inc(l2_in, 16)
                    for b in range(B):
                        a = sp.value_load(id_rows[0:1, 2, b:b + 1], min_val=0, max_val=l3a.shape[0] - 1)
                        sp.dma_start(l3a_sel[:, :, b, :], l3a[bass.DynSlice(a, 1)].rearrange("a (c p) r -> p (a c) r", p=P)).then_inc(l3a_in, 16)

                @block.scalar
                def _(act):
                    def wq_hi_part(g, h):
                        act.wait_ge(wq_in, 16 * g)
                        cols = slice(h * D, (h + 1) * D)
                        act.activation(wq_hi[:, :, cols], wq_raw[:, :, cols], ACT.Copy).then_inc(wq_hi_done, 1)

                    def bq_hi_part(g, p):
                        act.wait_ge(bq_in[p // 2], 64 * g)
                        act.activation(bq_pack[:, p, :], bq_raw[:, p, :], ACT.Copy).then_inc(bq_hi_done, 1)

                    def wo_hi_part(g, h):
                        act.activation(wo_hi[:, h, :], wo_raw[:, h, :], ACT.Copy).then_inc(wo_hi_done, 1)

                    def ao_hi_part(g):
                        act.wait_ge(ao_in, 16 * B * (g + 1))
                        act.activation(ao_pack[:, :, :, 0, :], ao_raw[:, :, :, :], ACT.Copy).then_inc(ao_hi_done, 1)

                    def pt(t, i):
                        act.wait_ge(t_ready, t + 1)
                        if i is None or i >= 1:
                            act.wait_ge(o_ready, t)
                        act.activation(pt_hi[:, :], ps_t[:, :], ACT.Copy).then_inc(pt_hi_done, 1)

                    def ot(t, i):
                        act.wait_ge(o_ready, t + 1)
                        if i is None or i >= 1:
                            act.wait_ge(out_ready, t)
                        act.activation(ot_hi[:, :], ps_o[:, :], ACT.Copy, scale=1.0 / P_SCALE).then_inc(ot_hi_done, 1)

                    def slots(g, first, last):
                        for b in range(B):
                            t = B * g + b
                            number = t if first else None
                            act.wait_ge(max_done, t + 1)
                            if not first or b >= 2:
                                act.wait_ge(p_lo_done, t - 1)
                            i = b % 2
                            for h in range(G):
                                e = act.activation(prob[i][:, h, :], sm[:, h, :], ACT.Exp, bias=nmax[i][:, h:h + 1], scale=-1.0,
                                                   accum_out=rsum[i][:, h:h + 1])
                            e.then_inc(exp_done, 1)
                            if not first or b >= 1:
                                pt(t - 1, None if not first else t - 1)
                            if b < HALF and not last:
                                act.wait_ge(q_ready, B * g + b + 1)
                                wq_hi_part(g + 1, b)
                            if not last and b % 2 == 0:
                                p = b // 2
                                if not first or p >= 2:
                                    act.wait_ge(q_ready, B * g + (0 if p < 2 else G))
                                bq_hi_part(g + 1, p)
                            act.wait_ge(prob_done, t + 1)
                            if not first or b >= 1:
                                act.wait_ge(t_ready, t)
                            act.activation(p_hi[:, :, :], prob[i][:, :, :], ACT.Copy).then_inc(p_hi_done, 1)
                            if b == 1:
                                act.wait_ge(wo_in, 16 * (g + 1))
                                if not first:
                                    act.wait_ge(out_ready, B * g)
                                wo_hi_part(g, 0)
                                wo_hi_part(g, 2)
                            if not first or b >= 1:
                                ot(t - 1, None if not first else t - 1)
                            if b == 1:
                                wo_hi_part(g, 1)
                                wo_hi_part(g, 3)
                                ao_hi_part(g)

                    over_heads(act, slots)
                    pt(B * KVH - 1, None)
                    ot(B * KVH - 1, None)

                @block.gpsimd
                def _(pool):
                    def wq_lo_part(n, h):
                        pool.wait_ge(wq_hi_done, n)
                        cols = slice(h * D, (h + 1) * D)
                        pool.tensor_tensor(wq_lo[:, :, cols], wq_raw[:, :, cols], wq_hi[:, :, cols].bitcast(F32),
                                           ALU.subtract).then_inc(wq_lo_done, 1)

                    def rotate(n, half, h):
                        pool.wait_ge(q_mult, 3 * (n + 1))
                        if not isinstance(n, int) or n >= G:
                            pool.wait_ge(s_ready, n)
                        pool.tensor_tensor(qt[:, half, h, :], qc[:, :], qs[:, :], ALU.add).then_inc(q_done, 1)

                    def slots(g, first, last):
                        for b in range(B):
                            t = B * g + b
                            i = b % 2
                            pool.wait_ge(inv_done, t + 1)
                            pool.tensor_tensor(prob[i][:, :, :], prob[i][:, :, :], rinv[i][:, :].unsqueeze(2).broadcast_to([P, G, T]),
                                               ALU.mult).then_inc(prob_done, 1)
                            if not (last and b >= HALF):
                                rotate(t, (b // HALF + 1) % 2, b % HALF)
                            if not last and b < HALF:
                                wq_lo_part(G * g + b + 1, b)
                            if b == 1:
                                for h in range(G // 2, G):
                                    pool.wait_ge(wo_hi_done, G * g + 2 * (h - G // 2) + 2)
                                    pool.tensor_tensor(wo_lo[:, h, :], wo_raw[:, h, :], wo_hi[:, h, :].bitcast(F32),
                                                       ALU.subtract).then_inc(wo_lo_pool, 1)
                                pool.wait_ge(ao_hi_done, g + 1)
                                pool.tensor_tensor(ao_pack[:, :, :, 1, :], ao_raw[:, :, :, :], ao_pack[:, :, :, 0, :].bitcast(F32),
                                                   ALU.subtract).then_inc(ao_lo_done, 1)

                    over_heads(pool, slots)

                @block.vector
                def _(dve):
                    def rotate(n, half, i, before):
                        tok = slice(half * HT, (half + 1) * HT)
                        dve.wait_ge(q_ready, n + 1)
                        if not isinstance(n, int) or n >= 1:
                            dve.wait_ge(q_done, n)
                        dve.tensor_tensor(qc[:, :], ps_q[i][:, :], cos_t[:, tok], ALU.mult).then_inc(q_mult, 1)
                        if before:
                            pt(n - 1)
                        for to, at in ((0, 64), (64, 0)):
                            dve.tensor_tensor(qs[to:to + 64, :], ps_q[i][at:at + 64, :], sin_t[to:to + 64, tok],
                                              ALU.mult).then_inc(q_mult, 1)

                    def bq_lo_part(n, p):
                        dve.wait_ge(bq_hi_done, n)
                        lo = slice(P // 2, P)
                        dve.tensor_tensor(bq_pack[lo, p, :], bq_raw[lo, p, :], bq_pack[lo, p, :].bitcast(F32),
                                           ALU.subtract).then_inc(bq_lo_done, 1)

                    def wo_lo_part(g, h):
                        dve.wait_ge(wo_hi_done, G * g + 2 * h + 1)
                        dve.tensor_tensor(wo_lo[:, h, :], wo_raw[:, h, :], wo_hi[:, h, :].bitcast(F32), ALU.subtract).then_inc(wo_lo_done, 1)

                    def pt(t):
                        dve.wait_ge(pt_hi_done, t + 1)
                        dve.tensor_tensor(pt_lo[:, :], ps_t[:, :], pt_hi[:, :].bitcast(F32), ALU.subtract).then_inc(pt_lo_done, 1)

                    def ot(t):
                        dve.wait_ge(ot_hi_done, t + 1)
                        dve.scalar_tensor_tensor(ot_lo[:, :], ps_o[:, :], 1.0 / P_SCALE, ot_hi[:, :].bitcast(F32), ALU.mult, ALU.subtract).then_inc(ot_lo_done, 1)

                    def add(t, b):
                        dve.wait_ge(out_ready, t + 1)
                        dve.tensor_tensor(res[:, b, :], ps_out[:, :], res[:, b, :], ALU.add).then_inc(res_done, 1)
                        dve.tensor_tensor(axo[:, b, :], ps_ao[0:2 * R, 0:T], axo[:, b, :], ALU.add).then_inc(axo_done, 1)

                    def slots(g, first, last):
                        for b in range(B):
                            t = B * g + b
                            i = b % 2
                            early = last and b >= HALF
                            if early:
                                ot(t - 2)
                            dve.wait_ge(s_ready, t + 1)
                            if not first or b >= 1:
                                dve.wait_ge(exp_done, t)
                            dve.memset(gate[:, :], 0.0)
                            for h in range(G):
                                m = dve.tensor_tensor_reduce(out=sm[:, h, :], in0=ps_s[i][:, h, :], in1=maskbias[:, b, :], scale=-1.0,
                                                             scalar=3.0e38, op0=ALU.add, op1=ALU.min, accum_out=nmax[i][:, h:h + 1])
                            m.then_inc(max_done, 1)
                            if not early and (not first or b >= 2):
                                ot(t - 2)
                            if (not first or b >= 3) and not (early and b > HALF):
                                add(t - 3, (b - 3) % B)
                            if b == 2:
                                wo_lo_part(g, 1)
                            if not last and b % 2:
                                bq_lo_part(PAIRS * g + b // 2 + 1, b // 2)
                            dve.wait_ge(exp_done, t + 1)
                            if not first or b >= 1:
                                dve.wait_ge(inv_done, t)
                            if not first or b >= 2:
                                dve.wait_ge(prob_done, t - 1)
                            dve.tensor_scalar(rsum_low[:, :], rsum[i][:, :], 1.0 / P_SCALE, None, ALU.mult).then_inc(sum_done, 1)
                            dve.wait_ge(sum_done, t + 1)
                            dve.reciprocal(rinv[i][:, :], rsum_low[:, :]).then_inc(inv_done, 1)
                            if not (last and b >= HALF):
                                between = b % HALF != HALF - 1 and (not first or b >= 1)
                                rotate(t, (b // HALF + 1) % 2, i, between)
                            else:
                                between = False
                            if not between and (not first or b >= 1):
                                pt(t - 1)
                            dve.wait_ge(p_hi_done, t + 1)
                            dve.tensor_tensor(p_lo[:, :, :], prob[i][:, :, :], p_hi[:, :, :], ALU.subtract).then_inc(p_lo_done, 1)
                            if b == 1:
                                wo_lo_part(g, 0)
                            if early:
                                add(t - 2, b - 2)

                    dve.memset(axo[:, :, :], 0.0).then_inc(axo_done, 1)
                    over_heads(dve, slots)
                    end = B * KVH
                    ot(end - 2)
                    pt(end - 1)
                    add(end - 2, B - 2)
                    ot(end - 1)
                    add(end - 1, B - 1)

                @block.tensor
                def _(pe):
                    def queries(n, half, h, weights=None):
                        if not isinstance(n, int) or n >= 2:
                            pe.wait_ge(q_mult, 3 * (n - 1))
                        if weights:
                            pe.wait_ge(wq_lo_done, weights[0])
                            pe.wait_ge(bq_lo_done, weights[1])
                        project(pe, ps_q[h % 2], wq_hi, wq_lo, bq_pack, axt[0], slice(h * D, (h + 1) * D), half).then_inc(q_ready, 1)

                    def scores(t, g, b):
                        half = b // HALF
                        if not isinstance(g, int) or g + half >= 1:
                            pe.wait_ge(q_done, B * g + G * half)
                        pe.wait_ge(kt_in[half], 16 * (g + 1))
                        if not isinstance(t, int) or t >= 2:
                            pe.wait_ge(max_done, t - 1)
                        at = (b % HALF) * T
                        for h in range(G):
                            mm = pe.matmul(ps_s[b % 2][:, h, :], qt[:, half, h, at:at + T], kt[:, b * T:(b + 1) * T], start=True, stop=True)
                        mm.then_inc(s_ready, 1)

                    def turn(t, b):
                        pe.wait_ge(p_lo_done, t + 1)
                        if not isinstance(t, int) or t >= 1:
                            pe.wait_ge(pt_lo_done, t)
                        for h in range(G):
                            pe.matmul(ps_t[:, h * T:(h + 1) * T], p_hi[:, h, :], ident_h[:, :], start=True, stop=False)
                            mm = pe.matmul(ps_t[:, h * T:(h + 1) * T], p_lo[:, h, :], ident_h[:, :], start=False, stop=True)
                        mm.then_inc(t_ready, 1)

                    def values(t, g, b):
                        pe.wait_ge(v_in[b // HALF], 32 * (g + 1))
                        pe.wait_ge(pt_lo_done, t + 1)
                        if not isinstance(t, int) or t >= 1:
                            pe.wait_ge(ot_lo_done, t)
                        pe.matmul(ps_o[:, :], v_hi[:, b, :], pt_hi[:, :], start=True, stop=False)
                        pe.matmul(ps_o[:, :], v_hi[:, b, :], pt_lo[:, :], start=False, stop=False)
                        pe.matmul(ps_o[:, :], v_lo[:, b, :], pt_hi[:, :], start=False, stop=True).then_inc(o_ready, 1)

                    def outputs(t, g, b):
                        pe.wait_ge(ot_lo_done, t + 1)
                        if not isinstance(t, int) or t >= 1:
                            pe.wait_ge(res_done, t)
                        for h in range(G):
                            q = slice(h * T, (h + 1) * T)
                            if b == 0 and h < G // 2:
                                pe.wait_ge(wo_lo_done, G // 2 * g + h + 1)
                            elif b == 0:
                                pe.wait_ge(wo_lo_pool, G // 2 * g + h - G // 2 + 1)
                            pe.matmul(ps_out[:, :], ot_hi[:, q], wo_hi[:, h, :], start=(h == 0), stop=False)
                            pe.matmul(ps_out[:, :], ot_hi[:, q], wo_lo[:, h, :], start=False, stop=False)
                            pe.matmul(ps_out[:, :], ot_lo[:, q], wo_hi[:, h, :], start=False, stop=(h == G - 1))
                        if b == 0:
                            pe.wait_ge(ao_lo_done, g + 1)
                        pe.wait_ge(axo_done, t + 1)
                        for h in range(G):
                            q = slice(h * T, (h + 1) * T)
                            w = ao_pack[:, b, h, :, :].rearrange("p a r -> p (a r)")
                            pe.matmul(ps_ao[0:2 * R, 0:T], w, ot_hi[:, q], start=(h == 0), stop=False)
                            mm = pe.matmul(ps_ao[0:2 * R, 0:T], w, ot_lo[:, q], start=False, stop=(h == G - 1))
                        mm.then_inc(out_ready, 1)

                    def slots(g, first, last):
                        for b in range(B):
                            t = B * g + b
                            scores(t, g, b)
                            if b < HALF:
                                queries(t, 1, b, None if first else (G * g, PAIRS * g))
                            elif not last:
                                queries(t, 0, b - HALF, (G * g + b - HALF + 1, PAIRS * g + 2))
                            if not first or b >= 1:
                                turn(t - 1, (b - 1) % B)
                            if not first or b >= 2:
                                outputs(t - 2, g - 1 if b < 2 else g, (b - 2) % B)
                            if not first or b >= 1:
                                values(t - 1, g - 1 if b < 1 else g, (b - 1) % B)

                    over_heads(pe, slots)
                    end, g = B * KVH, KVH - 1
                    turn(end - 1, B - 1)
                    outputs(end - 2, g, B - 2)
                    values(end - 1, g, B - 1)
                    outputs(end - 1, g, B - 1)
        late.close()
        attn.close()

        with ExitStack() as c:
            bo_pack = sb(c, "bo_pack", [P, PAIRS, HID], F32R)
            axo_pack = sb(c, "axo_pack", [P, B, T], F32R)
            w3t_hi = sb(c, "w3t_hi", [P, KC, HID], F32R)
            w3t_lo = sb(c, "w3t_lo", [P, KC, HID], F32R)
            l2b_hi = sb(c, "l2b_hi", [P, KC, B * R], F32R)
            l2b_lo = sb(c, "l2b_lo", [P, KC, B * R], F32R)
            l3a_hi = sb(c, "l3a_hi", [P, KC, B * R], F32R)
            l3a_lo = sb(c, "l3a_lo", [P, KC, B * R], F32R)
            l2a_hi = sb(c, "l2a_hi", [P, KC, B * R], F32R)
            l2a_lo = sb(c, "l2a_lo", [P, KC, B * R], F32R)
            cm = sb(c, "cm", [P, HID])
            mm_sb = sb(c, "mm_sb", [P, 2 * R])
            c_raw = sb(c, "c_raw", [P, PAIRS, HID])
            c_pack = sb(c, "c_pack", [P, PAIRS, HID], F32R)
            m_raw = sb(c, "m_raw", [P, PAIRS, 2 * R])
            m_pack = sb(c, "m_pack", [P, PAIRS, 2 * R], F32R)
            l3b_raw = sb(c, "l3b_raw", [P, PAIRS, HID])
            l3b_pack = sb(c, "l3b_pack", [P, PAIRS, HID], F32R)
            bias3 = sb(c, "bias3", [P, HID])
            x2t_hi = sb(c, "x2t_hi", [P, B, KC, T], F32R)
            x2t_lo = sb(c, "x2t_lo", [P, B, KC, T], F32R)
            own = [sb(c, f"own{i}", [2 * R, 2, T]) for i in range(2)]
            h2_pack = sb(c, "h2_pack", [P, B, T], F32R)
            h3_pack = sb(c, "h3_pack", [P, B, T], F32R)
            ps_wide = [ps(c, f"ps_wide{i}", [P, HID]) for i in range(3)]
            ps_turn = [ps(c, f"ps_turn{i}", [P, HID]) for i in range(3)]
            ps_h = [ps(c, f"ps_h{i}", [P, 512]) for i in range(2)]
            l3b_in = sem(c, "l3b_in")
            bias_in = sem(c, "bias_in")
            axo_ready = sem(c, "axo_ready")
            axo_hi_done = sem(c, "axo_hi_done")
            axo_lo_done = sem(c, "axo_lo_done")
            turn_ready = sem(c, "turn_ready")
            turn_hi_done = sem(c, "turn_hi_done")
            turn_lo_done = sem(c, "turn_lo_done")
            l2a_hi_done = sem(c, "l2a_hi_done")
            l2a_lo_done = sem(c, "l2a_lo_done")
            l3a_hi_done = sem(c, "l3a_hi_done")
            l3a_lo_done = sem(c, "l3a_lo_done")
            bo_hi_done = sem(c, "bo_hi_done")
            bo_lo_done = sem(c, "bo_lo_done")
            wide_ready = sem(c, "wide_ready")
            wide_done = sem(c, "wide_done")
            m_ready = sem(c, "m_ready")
            m_done = sem(c, "m_done")
            m_out = sem(c, "m_out")
            m_in = sem(c, "m_in")
            c_out = sem(c, "c_out")
            c_in = sem(c, "c_in")
            c_ready = sem(c, "c_ready")
            c_done = sem(c, "c_done")
            c_hi_done = sem(c, "c_hi_done")
            c_lo_done = sem(c, "c_lo_done")
            m_hi_done = sem(c, "m_hi_done")
            m_lo_done = sem(c, "m_lo_done")
            l3b_hi_done = sem(c, "l3b_hi_done")
            l3b_lo_done = sem(c, "l3b_lo_done")
            h_ready = sem(c, "h_ready")
            own_done = sem(c, "own_done")
            h_hi_done = sem(c, "h_hi_done")
            h_lo_done = sem(c, "h_lo_done")
            bias_done = sem(c, "bias_done")
            y_out = sem(c, "y_out")
            L2B, X2 = KC, KC + 1

            with nc.Block() as block:
                @block.sync
                def _(sp):
                    load_rows(sp, l3b_raw, l3b_sel, l3b_in)
                    sp.dma_start(bias3[:, :], b3.partition_broadcast(P)).then_inc(bias_in, 16)
                    sp.wait_ge(m_done, PAIRS)
                    sp.dma_start(m_rows.rearrange("b r n -> (b r) n"), mm_sb[:, :]).then_inc(m_out, 16)
                    sp.wait_ge(m_out, 16)
                    load_rows(sp, m_raw, m_rows, m_in)
                    sp.wait_ge(c_done, 1)
                    sp.dma_start(c_rows.rearrange("b r n -> (b r) n"), cm[:, :]).then_inc(c_out, 16)
                    sp.wait_ge(c_out, 16)
                    load_rows(sp, c_raw, c_rows, c_in)
                    for b in range(B):
                        sp.wait_ge(wide_done, B + b + 1)
                        sp.dma_start(out[b], res[:, b, :]).then_inc(y_out, 16)
                    sp.wait_ge(y_out, 16 * B)

                @block.tensor
                def _(pe):
                    def turn(n, tiles):
                        if n >= 3:
                            pe.wait_ge(turn_lo_done, n - 2)
                        for k, tile in enumerate(tiles):
                            mm = pe.matmul(ps_turn[n % 3][:, k * P:(k + 1) * P], tile, ident[:, :], start=True, stop=True)
                        mm.then_inc(turn_ready, 1)

                    def wide(n):
                        if n >= 3:
                            pe.wait_ge(wide_done, n - 2)
                        return ps_wide[n % 3][:, :]

                    def narrow(n, hi, lo):
                        o = ps_h[n % 2][0:2 * R, 0:2 * T]
                        pair = n % PAIRS
                        rows = slice(2 * R * pair, 2 * R * (pair + 1))
                        both = slice(2 * pair, 2 * pair + 2)
                        pe.wait_ge(turn_lo_done, X2 + 2 * pair + 2)
                        if n >= 2:
                            pe.wait_ge(own_done, n - 1)
                        for k in range(KC):
                            w_hi, w_lo = hi[:, k, rows], lo[:, k, rows]
                            pe.matmul(o, w_hi, x2t_hi[:, both, k, :], start=(k == 0), stop=False)
                            pe.matmul(o, w_hi, x2t_lo[:, both, k, :], start=False, stop=False)
                            mm = pe.matmul(o, w_lo, x2t_hi[:, both, k, :], start=False, stop=(k == KC - 1 and n < PAIRS))
                        return o, mm

                    pe.wait_ge(w3_in, 48)
                    for i in range(2):
                        pe.matmul(ps_h[i][:, :], row_gather[:, i, :], axo[:, i:B:2, :], start=True, stop=True).then_inc(axo_ready, 1)
                    for k in range(KC):
                        turn(k, [raw_w[:, o, k * P:(k + 1) * P] for o in range(KC)])
                    pe.wait_ge(l2_in, 32 * B)
                    turn(L2B, [l2b_sel[:, k * P:(k + 1) * P] for k in range(KC)])
                    pe.wait_ge(axo_lo_done, 2)
                    pe.wait_ge(l3a_in, 16 * B)
                    for k in range(KC):
                        mm = pe.matmul(ps_h[0][:, 0:P], l2a_sel[:, k, :, :].rearrange("p b r -> p (b r)"),
                                       l3a_sel[:, k, :, :].rearrange("p b r -> p (b r)"), start=(k == 0), stop=(k == KC - 1))
                    mm.then_inc(m_ready, 1)
                    o = ps_h[1][:, :]
                    pe.wait_ge(l2a_lo_done, 1)
                    for k in range(KC):
                        pe.wait_ge(turn_lo_done, k + 1)
                        pe.matmul(o, l2a_hi[:, k, :], w3t_hi[:, k, :], start=(k == 0), stop=False)
                        pe.matmul(o, l2a_hi[:, k, :], w3t_lo[:, k, :], start=False, stop=False)
                        pe.matmul(o, l2a_lo[:, k, :], w3t_hi[:, k, :], start=False, stop=False)
                    for k in range(KC):
                        mm = pe.matmul(o[:, k * P:(k + 1) * P], l2a_sel[:, k, :, :].rearrange("p b r -> p (b r)"), ident[:, :],
                                       start=False, stop=(k == KC - 1))
                    mm.then_inc(c_ready, 1)
                    for b in range(B):
                        pe.wait_ge(bo_lo_done, b // 2 + 1)
                        pe.matmul(wide(b), axo_pack[:, b, :], bo_pack[:, b // 2, :], start=True, stop=True).then_inc(wide_ready, 1)
                    for b in range(B):
                        pe.wait_ge(wide_done, b + 1)
                        turn(X2 + b, [res[:, b, k * P:(k + 1) * P] for k in range(KC)])
                    pe.wait_ge(m_done, PAIRS)
                    pe.wait_ge(c_done, 1)
                    for pair in range(PAIRS):
                        o, mm = narrow(pair, l2b_hi, l2b_lo)
                        mm.then_inc(h_ready, 1)
                    pe.wait_ge(l3a_lo_done, 1)
                    pe.wait_ge(m_lo_done, 1)
                    for pair in range(PAIRS):
                        o, mm = narrow(PAIRS + pair, l3a_hi, l3a_lo)
                        pe.wait_ge(h_lo_done, 2 * pair + 2)
                        pe.matmul(o, m_pack[:, pair, :], h2_pack[:, 2 * pair:2 * pair + 2, :],
                                  start=False, stop=True).then_inc(h_ready, 1)
                    for b in range(B):
                        o = wide(B + b)
                        for k in range(KC):
                            pe.matmul(o, x2t_hi[:, b, k, :], w3t_hi[:, k, :], start=(k == 0), stop=False)
                            pe.matmul(o, x2t_hi[:, b, k, :], w3t_lo[:, k, :], start=False, stop=False)
                            pe.matmul(o, x2t_lo[:, b, k, :], w3t_hi[:, k, :], start=False, stop=False)
                        pe.wait_ge(c_lo_done, b // 2 + 1)
                        pe.matmul(o, h2_pack[:, b, :], c_pack[:, b // 2, :], start=False, stop=False)
                        pe.wait_ge(l3b_lo_done, b // 2 + 1)
                        pe.wait_ge(h_lo_done, 2 * (PAIRS + b // 2) + 2)
                        pe.matmul(o, h3_pack[:, b, :], l3b_pack[:, b // 2, :], start=False, stop=True).then_inc(wide_ready, 1)

                @block.scalar
                def _(act):
                    def tile(n):
                        act.wait_ge(turn_ready, n + 1)
                        return ps_turn[n % 3]

                    def pack_hi(n, pack):
                        both = slice(2 * (n % PAIRS), 2 * (n % PAIRS) + 2)
                        act.wait_ge(own_done, n + 1)
                        for at in (0, 64):
                            act.activation(pack[at:at + 32, both, :], own[n % 2][:, :, :], ACT.Copy).then_inc(h_hi_done, 1)

                    act.wait_ge(l2_in, 32 * B)
                    act.activation(l2a_hi[:, :, :], l2a_sel[:, :, :, :].rearrange("p k b r -> p k (b r)"), ACT.Copy).then_inc(l2a_hi_done, 1)
                    for i in range(2):
                        act.wait_ge(axo_ready, i + 1)
                        act.activation(axo_pack[:, i:B:2, :], ps_h[i][:, :].rearrange("p (b t) -> p b t", t=T), ACT.Copy).then_inc(axo_hi_done, 1)
                    for k in range(KC):
                        act.activation(w3t_hi[:, k, :], tile(k)[:, :], ACT.Copy).then_inc(turn_hi_done, 1)
                    act.activation(l2b_hi[:, :, :].rearrange("p k n -> p (k n)"), tile(L2B)[:, :], ACT.Copy).then_inc(turn_hi_done, 1)
                    act.wait_ge(bo_in, 64)
                    for pair in range(PAIRS):
                        act.activation(bo_pack[:, pair, :], raw_b[:, pair, :], ACT.Copy).then_inc(bo_hi_done, 1)
                    act.wait_ge(l3a_in, 16 * B)
                    act.activation(l3a_hi[:, :, :], l3a_sel[:, :, :, :].rearrange("p k b r -> p k (b r)"), ACT.Copy).then_inc(l3a_hi_done, 1)
                    act.wait_ge(l3b_in, 64)
                    for b in range(B):
                        act.activation(x2t_hi[:, b, :, :].rearrange("p c n -> p (c n)"), tile(X2 + b)[:, :], ACT.Copy).then_inc(turn_hi_done, 1)
                        if b % 2:
                            act.activation(l3b_pack[:, b // 2, :], l3b_raw[:, b // 2, :], ACT.Copy).then_inc(l3b_hi_done, 1)
                    act.wait_ge(m_in, 64)
                    act.activation(m_pack[:, :, :], m_raw[:, :, :], ACT.Copy).then_inc(m_hi_done, 1)
                    act.wait_ge(c_in, 64)
                    for pair in range(PAIRS):
                        pack_hi(pair, h2_pack)
                        act.activation(c_pack[:, pair, :], c_raw[:, pair, :], ACT.Copy).then_inc(c_hi_done, 1)
                    for pair in range(PAIRS):
                        pack_hi(PAIRS + pair, h3_pack)

                @block.vector
                def _(dve):
                    low = slice(P // 2, P)

                    def add(n, dst):
                        dve.wait_ge(wide_ready, n + 1)
                        dve.tensor_tensor(dst, ps_wide[n % 3][:, :], dst, ALU.add).then_inc(wide_done, 1)

                    def own_columns(n, scale):
                        dve.wait_ge(h_ready, n + 1)
                        if n >= 2:
                            dve.wait_ge(h_hi_done, 2 * (n - 1))
                            dve.wait_ge(h_lo_done, 2 * (n - 1))
                        dve.scalar_tensor_tensor(own[n % 2][:, :, :], ps_h[n % 2][0:2 * R, 0:2 * T].rearrange("p (a t) -> p a t", t=T), scale,
                                                 twin[0:2 * R, 0:2].unsqueeze(2).broadcast_to([2 * R, 2, T]), ALU.mult, ALU.mult).then_inc(own_done, 1)

                    def pack_lo(n, pack):
                        both = slice(2 * (n % PAIRS), 2 * (n % PAIRS) + 2)
                        dve.wait_ge(h_hi_done, 2 * (n + 1))
                        for at in (32, 96):
                            dve.tensor_tensor(pack[at:at + 32, both, :], own[n % 2][:, :, :],
                                              pack[0:32, both, :].bitcast(F32), ALU.subtract).then_inc(h_lo_done, 1)

                    def low_half(pack, raw, pair, hi_done, lo_done):
                        dve.wait_ge(hi_done, pair + 1)
                        dve.tensor_tensor(pack[low, pair, :], raw[low, pair, :], pack[low, pair, :].bitcast(F32), ALU.subtract).then_inc(lo_done, 1)

                    dve.wait_ge(l2a_hi_done, 1)
                    dve.tensor_tensor(l2a_lo[:, :, :], l2a_sel[:, :, :, :].rearrange("p k b r -> p k (b r)"), l2a_hi[:, :, :].bitcast(F32),
                                      ALU.subtract).then_inc(l2a_lo_done, 1)
                    for i in range(2):
                        dve.wait_ge(axo_hi_done, i + 1)
                        dve.scalar_tensor_tensor(axo_pack[:, i:B:2, :], axo_pack[:, i:B:2, :].bitcast(F32), twin[:, 2:3],
                                                 ps_h[i][:, :].rearrange("p (b t) -> p b t", t=T), ALU.mult, ALU.add).then_inc(axo_lo_done, 1)
                    for k in range(KC):
                        dve.wait_ge(turn_hi_done, k + 1)
                        dve.tensor_tensor(w3t_lo[:, k, :], ps_turn[k % 3][:, :], w3t_hi[:, k, :].bitcast(F32), ALU.subtract).then_inc(turn_lo_done, 1)
                    dve.wait_ge(turn_hi_done, L2B + 1)
                    dve.tensor_tensor(l2b_lo[:, :, :].rearrange("p k n -> p (k n)"), ps_turn[L2B % 3][:, :],
                                      l2b_hi[:, :, :].rearrange("p k n -> p (k n)").bitcast(F32), ALU.subtract).then_inc(turn_lo_done, 1)
                    dve.wait_ge(m_ready, 1)
                    for pair in range(PAIRS):
                        rows = slice(2 * R * pair, 2 * R * (pair + 1))
                        dve.tensor_copy(mm_sb[rows, :], ps_h[0][rows, rows]).then_inc(m_done, 1)
                    for pair in range(PAIRS):
                        low_half(bo_pack, raw_b, pair, bo_hi_done, bo_lo_done)
                    dve.wait_ge(c_ready, 1)
                    dve.tensor_copy(cm[:, :], ps_h[1][:, :]).then_inc(c_done, 1)
                    for b in range(B):
                        add(b, res[:, b, :])
                    for b in range(B):
                        dve.wait_ge(turn_hi_done, X2 + b + 1)
                        dve.tensor_tensor(x2t_lo[:, b, :, :].rearrange("p c n -> p (c n)"), ps_turn[(X2 + b) % 3][:, :],
                                          x2t_hi[:, b, :, :].rearrange("p c n -> p (c n)").bitcast(F32), ALU.subtract).then_inc(turn_lo_done, 1)
                    dve.wait_ge(m_hi_done, 1)
                    dve.tensor_tensor(m_pack[low, :, :], m_raw[low, :, :], m_pack[low, :, :].bitcast(F32), ALU.subtract).then_inc(m_lo_done, 1)
                    own_columns(0, 1.0)
                    for n in range(2 * PAIRS):
                        if n + 1 < 2 * PAIRS:
                            own_columns(n + 1, 1.0 if n + 1 < PAIRS else LORA_SCALE)
                        pack_lo(n, h2_pack if n < PAIRS else h3_pack)
                        if n == PAIRS:
                            low_half(c_pack, c_raw, 0, c_hi_done, c_lo_done)
                        if n == PAIRS + 1:
                            low_half(l3b_pack, l3b_raw, 0, l3b_hi_done, l3b_lo_done)
                    for b in range(B):
                        if b % 2 and b // 2 + 1 < PAIRS:
                            low_half(c_pack, c_raw, b // 2 + 1, c_hi_done, c_lo_done)
                            low_half(l3b_pack, l3b_raw, b // 2 + 1, l3b_hi_done, l3b_lo_done)
                        dve.wait_ge(bias_done, b + 1)
                        add(B + b, res[:, b, :])

                @block.gpsimd
                def _(pool):
                    pool.wait_ge(l3a_hi_done, 1)
                    pool.tensor_tensor(l3a_lo[:, :, :], l3a_sel[:, :, :, :].rearrange("p k b r -> p k (b r)"),
                                       l3a_hi[:, :, :].bitcast(F32), ALU.subtract).then_inc(l3a_lo_done, 1)
                    pool.wait_ge(bias_in, 16)
                    for b in range(B):
                        pool.wait_ge(turn_ready, X2 + b + 1)
                        pool.tensor_tensor(res[:, b, :], res[:, b, :], bias3[:, :], ALU.add).then_inc(bias_done, 1)


_INS = ["x", "itok_B_3_7", "pos_BxS", "itok_B_0_7", "itok_B_0_23", "mask_BxS_bf1", "L0_cond_weight", "L1_cond_wq",
        "L1_cond_wk", "L1_cond_wv", "L1_cond_wo", "L1_cond_aq", "L1_cond_bq", "L1_cond_ak", "L1_cond_bk", "L1_cond_av",
        "L1_cond_bv", "L1_cond_ao", "L1_cond_bo", "L2_cond_A", "L2_cond_B", "L3_cond_W", "L3_cond_b",
        "L3_cond_lora_As", "L3_cond_lora_Bs"]


def constants():
    half = HEAD_DIM // 2
    freq = np.float32(THETA) ** (-np.arange(half, dtype=np.float32) / np.float32(half))
    root = float(HEAD_DIM) ** -0.25
    rope = np.zeros((P, 3), np.float32)
    rope[:, 0] = np.concatenate([freq, freq])
    rope[:, 1] = root
    rope[:half, 2] = -root
    rope[half:, 2] = root
    causal = np.where(np.tril(np.ones((P, P), bool)), 0.0, NEG).astype(np.float32)
    row, col = np.arange(2 * R_PACK)[:, None], np.arange(P)[None, :]
    twin = np.stack([(np.arange(P) // R_PACK) % 2 == i for i in range(2)] + [-(np.arange(P) // (2 * R_PACK) % 2)], 1).astype(np.float32)
    gather = np.stack([(row % R_PACK == col % R_PACK) & (col // R_PACK % 2 == i) for i in range(2)], 1).astype(np.float32)
    return {"ident_c": np.eye(P, dtype=np.float32), "causal_c": causal, "rope_c": rope, "gather_c": gather, "twin_c": twin}


def kernel(**inputs):
    import concourse.bacc as bacc
    from concourse.bass_utils import run_bass_kernel_spmd

    nc = bacc.Bacc("TRN2", target_bir_lowering=False, num_devices=1)
    arrays, args = {}, []
    for name, a in [(n, inputs[n]) for n in _INS] + list(constants().items()):
        a = np.ascontiguousarray(a)
        if a.dtype == bool:
            a = a.view(np.uint8)
        arrays[f"in_{name}"] = a
        args.append(nc.dram_tensor(f"in_{name}", a.shape, mybir.dt.from_np(a.dtype), kind="ExternalInput").ap())
    out = nc.dram_tensor("out_x", inputs["x"].shape, F32, kind="ExternalOutput").ap()
    program(nc, *args, out)
    result = run_bass_kernel_spmd(nc, [arrays], core_ids=[0])
    return result.results[0]["out_x"]
```
